# Optimizing a Trainium2 kernel written in Bass

```python
import numpy as np
import jax
import jax.numpy as jnp

def _softmax(x, axis=-1):
    return jax.nn.softmax(x, axis=axis)

def _gelu(x):
    return jax.nn.gelu(x, approximate=True)

def _silu(x):
    return jax.nn.silu(x)

def _sigmoid(x):
    return jax.nn.sigmoid(x)

def _layernorm(x, axis=-1, eps=1e-05):
    m = jnp.mean(x, axis=axis, keepdims=True)
    v = jnp.var(x, axis=axis, keepdims=True)
    return (x - m) / jnp.sqrt(v + eps)

def _scatter_add(tgt, idx, src, axis=0):
    return tgt.at[idx].add(src)

def _segment_sum(src, seg, n):
    return jax.ops.segment_sum(src, seg, n)
kernel_name = 'mk_perceiver_d1_seqx_r4_e59c96'

def setup_inputs(seed: int=0):
    np.random.seed(seed)
    _w = jnp.asarray

    def _rec_inputs():
        import jax
        import jax.numpy as jnp
        _rk = jax.random.key(seed)
        x = -0.0002928 + 1 * jax.random.normal(jax.random.fold_in(_rk, 1), (2, 256, 256), jnp.float32)
        _lenS = 256 - jax.random.randint(jax.random.fold_in(_rk, 7), (2,), 0, max(1, 256 // 4) + 1, jnp.int32)
        _lenS2 = 4096 - jax.random.randint(jax.random.fold_in(_rk, 8), (2,), 0, max(1, 4096 // 4) + 1, jnp.int32)
        _ctx_1024P = jax.random.normal(jax.random.fold_in(_rk, 11), (2, 16, 256), jnp.float32)
        _ctx_1024c = jax.random.dirichlet(jax.random.fold_in(_rk, 511), 0.3 * jnp.ones((16,), jnp.float32), (2, 4096))
        _ctx_1024t = jnp.einsum('bsk,bkd->bsd', _ctx_1024c, _ctx_1024P)
        _ctx_1024t = _ctx_1024t * jax.lax.rsqrt(jnp.mean(jnp.square(_ctx_1024t)) + 1e-12) * 0.953939
        ctx_1024 = 0.00222621 + 0.99962 * (_ctx_1024t + 0.3 * jax.random.normal(jax.random.fold_in(_rk, 611), (2, 4096, 256), jnp.float32))
        itok_BxS_0_255 = jax.random.randint(jax.random.fold_in(_rk, 12), (2, 256), 0, 64, jnp.int32)
        return (x, ctx_1024, itok_BxS_0_255)
    x, ctx_1024, itok_BxS_0_255 = _rec_inputs()

    def _L0_xattn_setup():
        import jax, jax.numpy as jnp
        import numpy as np
        N_LAYERS = 4
        H = 16
        LOOKBACK = 128
        EPS = 1e-06
        ROPE_BASE = 10000.0
        NEG = jnp.float32(-1e+30)

        def rmsnorm(x, w):
            return x * jax.lax.rsqrt(jnp.mean(x * x, axis=-1, keepdims=True) + EPS) * w

        def rope_cache(L, hd):
            inv = 1.0 / ROPE_BASE ** (jnp.arange(0, hd, 2, dtype=jnp.float32) / hd)
            t = jnp.arange(L, dtype=jnp.float32)
            f = t[:, None] * inv[None, :]
            emb = jnp.concatenate([f, f], axis=-1)
            return (jnp.cos(emb), jnp.sin(emb))

        def apply_rope(x, cos, sin):
            d = x.shape[-1]
            x1, x2 = (x[..., :d // 2], x[..., d // 2:])
            rot = jnp.concatenate([-x2, x1], axis=-1)
            return x * cos + rot * sin

        def split_heads(x, n_heads):
            B, L, D = x.shape
            return x.reshape(B, L, n_heads, D // n_heads).transpose(0, 2, 1, 3)

        def merge_heads(x):
            B, h, L, d = x.shape
            return x.transpose(0, 2, 1, 3).reshape(B, L, h * d)

        def sdpa(q, k, v, bias):
            scale = q.shape[-1] ** (-0.5)
            s = jnp.einsum('bhqd,bhkd->bhqk', q, k) * scale + bias
            p = jax.nn.softmax(s, axis=-1)
            return jnp.einsum('bhqk,bhkd->bhqd', p, v)

        def forward(x, memory, seg_ids, Wqkv, bqkv, Wo, bo, Wq_c, Wkv_c, Wo_c, Wg, Wu, Wd, n1, n2, n3, nf):
            B, L, D = x.shape
            S = memory.shape[1]
            hd = D // H
            cos, sin = rope_cache(L, hd)
            i = jnp.arange(L)
            causal_bias = jnp.where(i[None, :] <= i[:, None], 0.0, NEG)[None, None]
            j = jnp.arange(S)
            allowed = (j[None, None, :] <= seg_ids[:, :, None]) & (j[None, None, :] > seg_ids[:, :, None] - LOOKBACK)
            cross_bias = jnp.where(allowed, 0.0, NEG)[:, None]
            for l in range(N_LAYERS):
                h = rmsnorm(x, n1[l])
                qkv = h @ Wqkv[l].T + bqkv[l]
                q, k, v = jnp.split(qkv, 3, axis=-1)
                q = apply_rope(split_heads(q, H), cos, sin)
                k = apply_rope(split_heads(k, H), cos, sin)
                v = split_heads(v, H)
                o = merge_heads(sdpa(q, k, v, causal_bias)) @ Wo[l].T + bo[l]
                x = x + o
                h2 = rmsnorm(x, n2[l])
                qc = split_heads(h2 @ Wq_c[l].T, H)
                kv = memory @ Wkv_c[l].T
                kc, vc = jnp.split(kv, 2, axis=-1)
                kc, vc = (split_heads(kc, H), split_heads(vc, H))
                oc = merge_heads(sdpa(qc, kc, vc, cross_bias)) @ Wo_c[l].T
                x = x + oc
                h3 = rmsnorm(x, n3[l])
                x = x + jax.nn.silu(h3 @ Wg[l].T) * (h3 @ Wu[l].T) @ Wd[l].T
            return rmsnorm(x, nf)
        key = jax.random.key(seed)
        ks = jax.random.split(key, 16)
        B, L, S, D, F = (2, 512, 64, 256, 1024)
        w = 0.02
        inp = {'x': jax.random.normal(ks[0], (B, L, D), jnp.float32), 'memory': jax.random.normal(ks[1], (B, S, D), jnp.float32), 'seg_ids': jnp.sort(jax.random.randint(ks[2], (B, L), 0, S), axis=-1), 'Wqkv': jax.random.normal(ks[3], (N_LAYERS, 3 * D, D), jnp.float32) * w, 'bqkv': jnp.zeros((N_LAYERS, 3 * D), jnp.float32), 'Wo': jax.random.normal(ks[4], (N_LAYERS, D, D), jnp.float32) * w, 'bo': jnp.zeros((N_LAYERS, D), jnp.float32), 'Wq_c': jax.random.normal(ks[5], (N_LAYERS, D, D), jnp.float32) * w, 'Wkv_c': jax.random.normal(ks[6], (N_LAYERS, 2 * D, D), jnp.float32) * w, 'Wo_c': jax.random.normal(ks[7], (N_LAYERS, D, D), jnp.float32) * w, 'Wg': jax.random.normal(ks[8], (N_LAYERS, F, D), jnp.float32) * w, 'Wu': jax.random.normal(ks[9], (N_LAYERS, F, D), jnp.float32) * w, 'Wd': jax.random.normal(ks[10], (N_LAYERS, D, F), jnp.float32) * w, 'n1': jnp.ones((N_LAYERS, D), jnp.float32), 'n2': jnp.ones((N_LAYERS, D), jnp.float32), 'n3': jnp.ones((N_LAYERS, D), jnp.float32), 'nf': jnp.ones((D,), jnp.float32)}
        return inp
    _L0_xattn_all = _L0_xattn_setup()
    _L0_xattn_in = {k: v for k, v in _L0_xattn_all.items() if k in ('Wqkv', 'bqkv', 'Wo', 'bo', 'Wq_c', 'Wkv_c', 'Wo_c', 'Wg', 'Wu', 'Wd', 'n1', 'n2', 'n3', 'nf')}
    del _L0_xattn_all

    def _L0_attn_setup():
        import jax, jax.numpy as jnp
        import numpy as np
        import math
        DIM = 256
        WINDOW = 16
        NUM_HEADS = 16
        HEAD_DIM = DIM // NUM_HEADS
        SCALE = math.sqrt(HEAD_DIM)
        LN_EPS = 1e-05

        def _gather_window(z, W):
            B, T, H, C = z.shape
            t = jnp.arange(T)[:, None]
            w = jnp.arange(W)[None, :]
            idx = t - 1 - w
            valid = idx >= 0
            idxc = jnp.clip(idx, 0, T - 1)
            nb = z[:, idxc]
            nb = jnp.where(valid[None, :, :, None, None], nb, jnp.zeros((), z.dtype))
            return nb.transpose(0, 1, 3, 2, 4)
        key = jax.random.key(seed)
        k0, k1, k2, k3 = jax.random.split(key, 4)
        B, T, D = (2, 1024, DIM)
        x = jax.random.normal(k0, (B, T, D), dtype=jnp.float32)
        wq = jax.random.normal(k1, (D, D), dtype=jnp.float32) * 0.02
        wkv = jax.random.normal(k2, (2 * D, D), dtype=jnp.float32) * 0.02
        wo = jax.random.normal(k3, (D, D), dtype=jnp.float32) * 0.02
        gamma = jnp.ones((D,), dtype=jnp.float32)
        beta = jnp.zeros((D,), dtype=jnp.float32)
        return {'x': x, 'wq': wq, 'wkv': wkv, 'wo': wo, 'gamma': gamma, 'beta': beta}
    _L0_attn_all = _L0_attn_setup()
    _L0_attn_in = {k: v for k, v in _L0_attn_all.items() if k in ('wq', 'wkv', 'wo', 'gamma', 'beta')}
    del _L0_attn_all

    def _L0_ffn_setup():
        import jax, jax.numpy as jnp
        import numpy as np
        HIDDEN = 256
        INNER = 1024

        def _weight_quant(w):
            scale = 1.0 / jnp.clip(jnp.mean(jnp.abs(w)), 1e-05)
            wq = jnp.clip(jnp.round(w * scale), -1.0, 1.0) / scale
            return w + jax.lax.stop_gradient(wq - w)

        def _act_quant(x):
            scale = 127.0 / jnp.clip(jnp.max(jnp.abs(x), axis=-1, keepdims=True), 1e-05)
            xq = jnp.clip(jnp.round(x * scale), -128.0, 127.0) / scale
            return x + jax.lax.stop_gradient(xq - x)

        def _bitlinear(x, w):
            return jnp.einsum('bsi,oi->bso', _act_quant(x), _weight_quant(w))
        key = jax.random.key(seed)
        k0, k1, k2, k3 = jax.random.split(key, 4)
        x = jax.random.normal(k0, (4, 512, HIDDEN), dtype=jnp.float32)
        w_gate = jax.random.normal(k1, (INNER, HIDDEN), dtype=jnp.float32) / np.sqrt(HIDDEN)
        w_up = jax.random.normal(k2, (INNER, HIDDEN), dtype=jnp.float32) / np.sqrt(HIDDEN)
        w_down = jax.random.normal(k3, (HIDDEN, INNER), dtype=jnp.float32) / np.sqrt(INNER)
        return {'x': x, 'w_gate': w_gate, 'w_up': w_up, 'w_down': w_down}
    _L0_ffn_all = _L0_ffn_setup()
    _L0_ffn_in = {k: v for k, v in _L0_ffn_all.items() if k in ('w_gate', 'w_up', 'w_down')}
    del _L0_ffn_all
    return {'x': x, 'ctx_1024': ctx_1024, 'itok_BxS_0_255': itok_BxS_0_255, 'L0_xattn_Wqkv': _L0_xattn_in['Wqkv'], 'L0_xattn_bqkv': _L0_xattn_in['bqkv'], 'L0_xattn_Wo': _L0_xattn_in['Wo'], 'L0_xattn_bo': _L0_xattn_in['bo'], 'L0_xattn_Wq_c': _L0_xattn_in['Wq_c'], 'L0_xattn_Wkv_c': _L0_xattn_in['Wkv_c'], 'L0_xattn_Wo_c': _L0_xattn_in['Wo_c'], 'L0_xattn_Wg': _L0_xattn_in['Wg'], 'L0_xattn_Wu': _L0_xattn_in['Wu'], 'L0_xattn_Wd': _L0_xattn_in['Wd'], 'L0_xattn_n1': _L0_xattn_in['n1'], 'L0_xattn_n2': _L0_xattn_in['n2'], 'L0_xattn_n3': _L0_xattn_in['n3'], 'L0_xattn_nf': _L0_xattn_in['nf'], 'L0_attn_wq': _L0_attn_in['wq'], 'L0_attn_wkv': _L0_attn_in['wkv'], 'L0_attn_wo': _L0_attn_in['wo'], 'L0_attn_gamma': _L0_attn_in['gamma'], 'L0_attn_beta': _L0_attn_in['beta'], 'L0_ffn_w_gate': _L0_ffn_in['w_gate'], 'L0_ffn_w_up': _L0_ffn_in['w_up'], 'L0_ffn_w_down': _L0_ffn_in['w_down']}

def reference(x, ctx_1024, itok_BxS_0_255, L0_xattn_Wqkv, L0_xattn_bqkv, L0_xattn_Wo, L0_xattn_bo, L0_xattn_Wq_c, L0_xattn_Wkv_c, L0_xattn_Wo_c, L0_xattn_Wg, L0_xattn_Wu, L0_xattn_Wd, L0_xattn_n1, L0_xattn_n2, L0_xattn_n3, L0_xattn_nf, L0_attn_wq, L0_attn_wkv, L0_attn_wo, L0_attn_gamma, L0_attn_beta, L0_ffn_w_gate, L0_ffn_w_up, L0_ffn_w_down):
    import jax
    import jax.numpy as jnp

    def _L0_xattn_ref(x, memory, seg_ids, Wqkv, bqkv, Wo, bo, Wq_c, Wkv_c, Wo_c, Wg, Wu, Wd, n1, n2, n3, nf):
        import jax, jax.numpy as jnp
        import numpy as np
        N_LAYERS = 4
        H = 16
        LOOKBACK = 128
        EPS = 1e-06
        ROPE_BASE = 10000.0
        NEG = jnp.float32(-1e+30)

        def rmsnorm(x, w):
            return x * jax.lax.rsqrt(jnp.mean(x * x, axis=-1, keepdims=True) + EPS) * w

        def rope_cache(L, hd):
            inv = 1.0 / ROPE_BASE ** (jnp.arange(0, hd, 2, dtype=jnp.float32) / hd)
            t = jnp.arange(L, dtype=jnp.float32)
            f = t[:, None] * inv[None, :]
            emb = jnp.concatenate([f, f], axis=-1)
            return (jnp.cos(emb), jnp.sin(emb))

        def apply_rope(x, cos, sin):
            d = x.shape[-1]
            x1, x2 = (x[..., :d // 2], x[..., d // 2:])
            rot = jnp.concatenate([-x2, x1], axis=-1)
            return x * cos + rot * sin

        def split_heads(x, n_heads):
            B, L, D = x.shape
            return x.reshape(B, L, n_heads, D // n_heads).transpose(0, 2, 1, 3)

        def merge_heads(x):
            B, h, L, d = x.shape
            return x.transpose(0, 2, 1, 3).reshape(B, L, h * d)

        def sdpa(q, k, v, bias):
            scale = q.shape[-1] ** (-0.5)
            s = jnp.einsum('bhqd,bhkd->bhqk', q, k) * scale + bias
            p = jax.nn.softmax(s, axis=-1)
            return jnp.einsum('bhqk,bhkd->bhqd', p, v)

        def forward(x, memory, seg_ids, Wqkv, bqkv, Wo, bo, Wq_c, Wkv_c, Wo_c, Wg, Wu, Wd, n1, n2, n3, nf):
            B, L, D = x.shape
            S = memory.shape[1]
            hd = D // H
            cos, sin = rope_cache(L, hd)
            i = jnp.arange(L)
            causal_bias = jnp.where(i[None, :] <= i[:, None], 0.0, NEG)[None, None]
            j = jnp.arange(S)
            allowed = (j[None, None, :] <= seg_ids[:, :, None]) & (j[None, None, :] > seg_ids[:, :, None] - LOOKBACK)
            cross_bias = jnp.where(allowed, 0.0, NEG)[:, None]
            for l in range(N_LAYERS):
                h = rmsnorm(x, n1[l])
                qkv = h @ Wqkv[l].T + bqkv[l]
                q, k, v = jnp.split(qkv, 3, axis=-1)
                q = apply_rope(split_heads(q, H), cos, sin)
                k = apply_rope(split_heads(k, H), cos, sin)
                v = split_heads(v, H)
                o = merge_heads(sdpa(q, k, v, causal_bias)) @ Wo[l].T + bo[l]
                x = x + o
                h2 = rmsnorm(x, n2[l])
                qc = split_heads(h2 @ Wq_c[l].T, H)
                kv = memory @ Wkv_c[l].T
                kc, vc = jnp.split(kv, 2, axis=-1)
                kc, vc = (split_heads(kc, H), split_heads(vc, H))
                oc = merge_heads(sdpa(qc, kc, vc, cross_bias)) @ Wo_c[l].T
                x = x + oc
                h3 = rmsnorm(x, n3[l])
                x = x + jax.nn.silu(h3 @ Wg[l].T) * (h3 @ Wu[l].T) @ Wd[l].T
            return rmsnorm(x, nf)
        return forward(x, memory, seg_ids, Wqkv, bqkv, Wo, bo, Wq_c, Wkv_c, Wo_c, Wg, Wu, Wd, n1, n2, n3, nf)

    def _L0_attn_ref(x, wq, wkv, wo, gamma, beta):
        import jax, jax.numpy as jnp
        import numpy as np
        import math
        DIM = 256
        WINDOW = 16
        NUM_HEADS = 16
        HEAD_DIM = DIM // NUM_HEADS
        SCALE = math.sqrt(HEAD_DIM)
        LN_EPS = 1e-05

        def _gather_window(z, W):
            B, T, H, C = z.shape
            t = jnp.arange(T)[:, None]
            w = jnp.arange(W)[None, :]
            idx = t - 1 - w
            valid = idx >= 0
            idxc = jnp.clip(idx, 0, T - 1)
            nb = z[:, idxc]
            nb = jnp.where(valid[None, :, :, None, None], nb, jnp.zeros((), z.dtype))
            return nb.transpose(0, 1, 3, 2, 4)
        B, T, D = x.shape
        H, HD, W = (NUM_HEADS, HEAD_DIM, WINDOW)
        q = (x @ wq.T).reshape(B, T, H, HD)
        kv = (x @ wkv.T).reshape(B, T, H, 2 * HD)
        nb_kv = _gather_window(kv, W)
        nb_k, nb_v = (nb_kv[..., :HD], nb_kv[..., HD:])
        tau = jax.nn.sigmoid(jnp.einsum('bthd,bthwd->bthw', q, nb_k) / SCALE)
        msg = jnp.einsum('bthw,bthwd->bthd', tau, nb_v)
        y = x + msg.reshape(B, T, D) @ wo.T
        mu = jnp.mean(y, axis=-1, keepdims=True)
        var = jnp.mean((y - mu) ** 2, axis=-1, keepdims=True)
        out = (y - mu) * jax.lax.rsqrt(var + LN_EPS) * gamma + beta
        return out

    def _L0_ffn_ref(x, w_gate, w_up, w_down):
        import jax, jax.numpy as jnp
        import numpy as np
        HIDDEN = 256
        INNER = 1024

        def _weight_quant(w):
            scale = 1.0 / jnp.clip(jnp.mean(jnp.abs(w)), 1e-05)
            wq = jnp.clip(jnp.round(w * scale), -1.0, 1.0) / scale
            return w + jax.lax.stop_gradient(wq - w)

        def _act_quant(x):
            scale = 127.0 / jnp.clip(jnp.max(jnp.abs(x), axis=-1, keepdims=True), 1e-05)
            xq = jnp.clip(jnp.round(x * scale), -128.0, 127.0) / scale
            return x + jax.lax.stop_gradient(xq - x)

        def _bitlinear(x, w):
            return jnp.einsum('bsi,oi->bso', _act_quant(x), _weight_quant(w))
        gate = jax.nn.silu(_bitlinear(x, w_gate))
        up = _bitlinear(x, w_up)
        return _bitlinear(gate * up, w_down)
    x = x + _L0_xattn_ref(_layernorm(x, axis=-1), ctx_1024, itok_BxS_0_255, L0_xattn_Wqkv, L0_xattn_bqkv, L0_xattn_Wo, L0_xattn_bo, L0_xattn_Wq_c, L0_xattn_Wkv_c, L0_xattn_Wo_c, L0_xattn_Wg, L0_xattn_Wu, L0_xattn_Wd, L0_xattn_n1, L0_xattn_n2, L0_xattn_n3, L0_xattn_nf)
    x = x + _L0_attn_ref(_layernorm(x, axis=-1), L0_attn_wq, L0_attn_wkv, L0_attn_wo, L0_attn_gamma, L0_attn_beta)
    x = x + _L0_ffn_ref(_layernorm(x, axis=-1), L0_ffn_w_gate, L0_ffn_w_up, L0_ffn_w_down)
    return x

_drawn_inputs = setup_inputs


def setup_inputs(seed=0):
    import zlib

    import numpy as np

    out = dict(_drawn_inputs(seed))
    spreads = {'L0_xattn_bqkv': (0.0, 0.1),
     'L0_xattn_bo': (0.0, 0.1),
     'L0_xattn_n1': (1.0, 0.6),
     'L0_xattn_n2': (1.0, 0.6),
     'L0_xattn_n3': (1.0, 0.6),
     'L0_xattn_nf': (1.0, 0.2),
     'L0_attn_gamma': (1.0, 0.2),
     'L0_attn_beta': (0.0, 0.1)}
    factors = {'L0_xattn_Wq_c': 8.0, 'L0_attn_wq': 8.0}
    for name, (base, spread) in spreads.items():
        noise = np.random.default_rng([zlib.crc32(name.encode()), seed]).standard_normal(out[name].shape)
        drawn = base * np.exp(spread * noise) if base else spread * noise
        out[name] = jnp.asarray(drawn.astype(out[name].dtype))
    for name, factor in factors.items():
        out[name] = (out[name] * factor).astype(out[name].dtype)
    return out
```

```python
from contextlib import ExitStack

import concourse.bass as bass
from concourse import mybir

F32 = mybir.dt.float32
BF16 = mybir.dt.bfloat16
I32 = mybir.dt.int32
ALU = mybir.AluOpType
ACT = mybir.ActivationFunctionType
AX_X = mybir.AxisListType.X

P = 128
B, L, D = 2, 256, 256
H, HD = 16, 16
NL = 4
S_CTX = 4096
LOOKBACK = 128
F = 1024
QT = L // P
KT = D // P
HT = H // KT
FT = F // P
NBLK = S_CTX // P
RMS_EPS, LN_EPS = 1e-6, 1e-5
NEG = -1e30
NO_MAX = 3e38
MAGIC = 12582912.0
SCALE = HD ** -0.5

WA_QKV, WA_O, WA_N = 0, KT * 3 * D, KT * 4 * D
WB_Q, WB_KV, WB_O, WB_N = 0, KT * D, KT * 3 * D, KT * 4 * D
WC_G, WC_U, WC_D, WC_N = 0, KT * F, 2 * KT * F, 2 * KT * F + FT * D
C_ID, C_CAUSAL, C_HEAD, C_COS, C_SIN, C_IOTA, C_BAND, C_CORNER = 0, 128, 384, 392, 424, 456, 584, 712
C_N = 728

SELF = [(0, 4 * g, 4, P) for g in range(4)] + [(1, 2 * g, 2, 2 * P) for g in range(8)]
NSELF = B * len(SELF)
CROSS = [(b, q, 4 * g) for b in range(B) for q in range(QT) for g in range(4)]
NCROSS = len(CROSS)
WINDOW = [(blk, k, half) for blk in range(QT) for k in range(KT) for half in range(2)] + [("corner", 0, 0)]
NORMS = 3 * B
SBANKS, PBANKS, DBANKS = 3, 2, 2

LAYER_USES = (
    ["n00", "qk00", "qk01", "v0", "n01", "qk10", "qk11", "v1", "tq00", "tq01", "tq10", "tq11",
     "oT0", "wo0", "n10", "qc00", "qc01", "oT1", "wo1", "n11", "qc10", "qc11"]
    + ["coT0", "cwo0", "coT1", "cwo1", "n20"] + [f"gu0{f}" for f in range(FT)]
    + ["n21", "gu10", "gu11", "y0"] + [f"gu1{f}" for f in range(2, FT)] + ["y1"]
)
CROSS_AT = LAYER_USES.index("coT0")
TAIL_USES = (
    [u for b in range(B) for u in (f"an{b}", f"wq0{b}", f"wq1{b}", f"wk{b}", f"wv{b}")] + ["sum"]
    + [u for b in range(B) for u in (f"moT{b}", f"mwo{b}")]
    + [u for b in range(B) for u in (f"fn{b}",)]
    + [f"{w}{t}{j}" for t in range(2 * B) for j in range(2) for w in "gu"]
    + [u for t in range(2 * B) for u in (f"gT{t}", f"d{t}")]
)


def bank_order(uses):
    seen, at = [0] * DBANKS, {}
    for n, u in enumerate(uses):
        at[u] = (n % DBANKS, seen[n % DBANKS])
        seen[n % DBANKS] += 1
    return at, seen


LAYER_AT, LAYER_TOTAL = bank_order(LAYER_USES)
TAIL_AT, _ = bank_order(TAIL_USES)
BEFORE_CROSS = bank_order(LAYER_USES[:CROSS_AT])[1]


def perceiver(nc, x_in, ctx_in, seg_in, wa_in, wb_in, wc_in, nrm_in, bias_in, vec_in, wt_in, wf_in, const_in, out):
    stack = ExitStack()
    with stack:
        def sb(name, shape, dt=F32):
            return stack.enter_context(nc.sbuf_tensor(name, shape, dt))

        def ps(name):
            return stack.enter_context(nc.psum_tensor(name, [P, 512], F32))

        def sem(name):
            return stack.enter_context(nc.semaphore(name))

        X0 = sb("X0", [P, 4, D])
        X = sb("X", [P, 4, D])
        hs = sb("hs", [P, 4, D])
        hT = [sb(f"hT{b}", [P, KT, L]) for b in range(B)]
        WAB = sb("WAB", [P, WA_N + WB_N])
        WA, WB = WAB[:, 0:WA_N], WAB[:, WA_N:WA_N + WB_N]
        WC = sb("WC", [P, WC_N])
        nrm = sb("nrm", [P, 3 * KT])
        bias = sb("bias", [P, 4 * D])
        vec = sb("vec", [P, 3 * D])
        WT = sb("WT", [P, KT * 4 * D])
        const = sb("const", [P, C_N])
        identB = sb("identB", [P, P], BF16)
        causB = sb("causB", [P, 2 * P], BF16)
        HID = [sb(f"HID{b}", [P, 2 * QT * 2 * D]) for b in range(B)]
        QK = [HID[b][:, 0:QT * 2 * D].rearrange("p (t n) -> p t n", t=QT) for b in range(B)]
        QR = [HID[b][:, QT * 2 * D:].rearrange("p (t n) -> p t n", t=QT) for b in range(B)]
        AT = [HID[b][:, :].rearrange("p (f n) -> p f n", f=FT) for b in range(B)]
        V = [sb(f"V{b}", [P, QT, D]) for b in range(B)]
        QM = [sb(f"QM{b}", [P, KT, HT, L]) for b in range(B)]
        kTs = [sb(f"kTs{b}", [P, KT, L]) for b in range(B)]
        Pr = sb("Pr", [P, 3, 512])
        PT = sb("PT", [P, 3, 512])
        ON = sb("ON", [P, B * QT * D])
        On = [ON[:, b * QT * D:(b + 1) * QT * D].rearrange("p (t n) -> p t n", t=QT) for b in range(B)]
        RT = ON[:, :].rearrange("p (t n) -> p t n", t=QT)
        oT = [sb(f"oT{b}", [P, KT, L]) for b in range(B)]
        CT = sb("CT", [P, KT, B, P])
        KC = sb("KC", [P, KT, B, P])
        VC = sb("VC", [P, B, D])
        OR = [sb(f"OR{b}", [P, QT, D]) for b in range(B)]
        SG = sb("SG", [P, 2, L])
        ss = sb("ss", [P, NORMS, QT])
        ms = sb("ms", [P, NORMS, QT])
        rstd = sb("rstd", [P, NORMS, QT])
        mhalf = sb("mhalf", [P, QT])
        segR = sb("segR", [P, 4])
        nms = sb("nms", [P, B, QT * H])
        lS = sb("lS", [P, B, QT * H])
        rl = sb("rl", [P, B, QT * H])
        nmB = sb("nmB", [P, B, QT * H])
        nmN = sb("nmN", [P, B, QT * H])
        nmR = sb("nmR", [P, B, QT * H])
        lB = sb("lB", [P, B, QT * H])
        lR = sb("lR", [P, B, QT * H])
        dm = sb("dm", [P, B, QT * H])
        al = sb("al", [P, B, QT * H])
        segI = sb("segI", [P, 4], I32)
        segF = sb("segF", [P, 4])
        segL = sb("segL", [P, 4])
        rowI = sb("rowI", [1, 4 * P], I32)
        rowF = sb("rowF", [1, 4 * P])
        few = sb("few", [1, 8])
        cnt = sb("cnt", [1, NBLK])
        NB = sb("NB", [1, 1], I32)
        step = sb("step", [P, 4])
        look = sb("look", [P, 4])
        mA = sb("mA", [P, 4, P])
        mB = sb("mB", [P, 4, P])
        maskB = sb("maskB", [P, 4, P], BF16)
        bst = sb("bst", [P, 8, QT, 6])
        mv = sb("mv", [P, 8, QT, 2])
        lve = sb("lve", [P, 8, QT])
        lrs = sb("lrs", [P, 8, QT])
        ones = sb("ones", [P, P])
        asum = sb("asum", [P, 3])
        WF = sb("WF", [P, 3, 2048])
        mw = sb("mw", [P, 3])
        rw = sb("rw", [P, 3])
        WQ = WAB[:, 0:3 * 1024].bitcast(BF16).rearrange("p (w n) -> p w n", w=3)
        xq = mA[:, :, :].rearrange("p t n -> p (t n)").bitcast(BF16).rearrange("p (t n) -> p t n", t=4)
        xqT = [mB[:, 2 * b:2 * b + 2, :].rearrange("p t n -> p (t n)").bitcast(BF16)
               .rearrange("p (k n) -> p k n", k=KT) for b in range(B)]
        am = sb("am", [P, 4, 4])
        am2 = sb("am2", [P, 4, 4])
        sgu = sb("sgu", [P, 4, 3])

        psS = [ps(f"psS{i}") for i in range(SBANKS)]
        psP = [ps(f"psP{i}") for i in range(PBANKS)]
        psO = ps("psO")
        psD = [ps(f"psD{i}") for i in range(DBANKS)]

        c_ld, x_ld, seg_ld, vec_ld = sem("c_ld"), sem("x_ld"), sem("seg_ld"), sem("vec_ld")
        wa_ld, wb_ld, wc_ld, nrm_ld, bias_ld = sem("wa_ld"), sem("wb_ld"), sem("wc_ld"), sem("nrm_ld"), sem("bias_ld")
        wt_ld, wf_ld, ct_ld = sem("wt_ld"), sem("wf_ld"), sem("ct_ld")
        d_full = [sem(f"d_full{i}") for i in range(DBANKS)]
        d_free = [sem(f"d_free{i}") for i in range(DBANKS)]
        consts_set = sem("consts_set")
        nb_set = sem("nb_set")
        few_done = sem("few_done")
        x_first = sem("x_first")
        ss_set, ms_set, rstd_set, h_set = (sem(n) for n in ("ss_set", "ms_set", "rstd_set", "h_set"))
        cos_set, sin_set, qr_set = (sem(n) for n in ("cos_set", "sin_set", "qr_set"))
        xbo_set = sem("xbo_set")
        s_full, s_max, s_exp, t_full, t_copied, pv_done = (
            sem(n) for n in ("s_full", "s_max", "s_exp", "t_full", "t_copied", "pv_done"))
        rl_set, on_set = sem("rl_set"), sem("on_set")
        kc_full, vc_full, kc_set, vc_set = sem("kc_full"), sem("vc_full"), sem("kc_set"), sem("vc_set")
        mask_cmp, mask_set = sem("mask_cmp"), sem("mask_set")
        cs_full, c_bmax, c_max, c_exp, ct_full, ct_copied, cpv_done = (
            sem(n) for n in ("cs_full", "c_bmax", "c_max", "c_exp", "ct_full", "ct_copied", "cpv_done"))
        dm_set, nmr_set, al_set, lr_set, or_scaled, or_added = (
            sem(n) for n in ("dm_set", "nmr_set", "al_set", "lr_set", "or_scaled", "or_added"))
        crl_set, con_set = sem("crl_set"), sem("con_set")
        sg_set = sem("sg_set")
        ln_var, ln_rstd = sem("ln_var"), sem("ln_rstd")
        v_step = sem("v_step")
        an_set = sem("an_set")
        ws_full, sig_set, tau_set, wpv_done = sem("ws_full"), sem("sig_set"), sem("tau_set"), sem("wpv_done")
        mo_set = sem("mo_set")
        asum_set, mw_set, tern_set, sgu_set = sem("asum_set"), sem("mw_set"), sem("tern_set"), sem("sgu_set")
        pool_set, tern_step, mask_rel = sem("pool_set"), sem("tern_step"), sem("mask_rel")
        xq_set, gq_set = sem("xq_set"), sem("gq_set")
        stored = sem("stored")

        ident = const[:, C_ID:C_ID + P]
        headmask = const[:, C_HEAD:C_HEAD + HT]
        cos = const[:, C_COS:C_COS + QT * HD].rearrange("p (t d) -> p t d", t=QT)
        sin = const[:, C_SIN:C_SIN + QT * HD].rearrange("p (t d) -> p t d", t=QT)
        iota = const[:, C_IOTA:C_IOTA + P]
        band = const[:, C_BAND:C_BAND + P]
        corner = const[:, C_CORNER:C_CORNER + HD]
        Wqkv = WA[:, WA_QKV:WA_O].rearrange("p (k n) -> p k n", k=KT)
        Wo = WA[:, WA_O:WA_N].rearrange("p (k n) -> p k n", k=KT)
        Wqc = WB[:, WB_Q:WB_KV].rearrange("p (k n) -> p k n", k=KT)
        Wkv = WB[:, WB_KV:WB_O].rearrange("p (k n) -> p k n", k=KT)
        Woc = WB[:, WB_O:WB_N].rearrange("p (k n) -> p k n", k=KT)
        Wg = WC[:, WC_G:WC_U].rearrange("p (k n) -> p k n", k=KT)
        Wu = WC[:, WC_U:WC_D].rearrange("p (k n) -> p k n", k=KT)
        Wd = WC[:, WC_D:WC_N].rearrange("p (k n) -> p k n", k=FT)
        Wt = WT[:, :].rearrange("p (w k n) -> p w k n", w=4, k=KT)

        def filled(l, use):
            k, n = (LAYER_AT if use in LAYER_AT else TAIL_AT)[use]
            return d_full[k], l * LAYER_TOTAL[k] + n + 1

        def free_for(l, use):
            k, n = (LAYER_AT if use in LAYER_AT else TAIL_AT)[use]
            return d_free[k], l * LAYER_TOTAL[k] + n

        def emptied(l, use):
            k, n = (LAYER_AT if use in LAYER_AT else TAIL_AT)[use]
            return d_free[k], l * LAYER_TOTAL[k] + n + 1

        def bank(use):
            return psD[(LAYER_AT if use in LAYER_AT else TAIL_AT)[use][0]]

        def full(use):
            return d_full[(LAYER_AT if use in LAYER_AT else TAIL_AT)[use][0]]

        def free(use):
            return d_free[(LAYER_AT if use in LAYER_AT else TAIL_AT)[use][0]]

        def heads(ap):
            return ap.rearrange("p t (h d) -> p (t h) d", d=HD)

        def tiles(ap):
            return ap.rearrange("p (a n) -> p a n", a=2)

        def GU(t):
            return QM[t // 2][:, :, :, :].rearrange("p k h n -> p (k h n)")[:, (t % 2) * 2048:(t % 2) * 2048 + F]

        def GR(t):
            return QM[t // 2][:, :, :, :].rearrange("p k h n -> p (k h n)")[:, (t % 2) * 2048 + F:(t % 2) * 2048 + 2 * F]

        def GQ(t):
            return AT[t // 2][:, :, :].rearrange("p f n -> p (f n)").bitcast(BF16)[:, (t % 2) * 2048:(t % 2) * 2048 + F]

        def GQT(t):
            return AT[t // 2][:, :, :].rearrange("p f n -> p (f n)").bitcast(BF16)[:, (t % 2) * 2048 + F:(t % 2) * 2048 + 2 * F]

        block = stack.enter_context(nc.Block())

        @block.sync
        def _(sp):
            sp.dma_start(X0[:, :, :], x_in).then_inc(x_ld, 16)
            sp.dma_start(rowI[:, :], seg_in[4 * P:8 * P].rearrange("(a n) -> a n", a=1)).then_inc(seg_ld, 16)
            sp.dma_start(segI[:, :], seg_in[0:4 * P].rearrange("(p t) -> p t", t=4)).then_inc(seg_ld, 16)
            sp.dma_start(const[:, :], const_in).then_inc(c_ld, 16)
            sp.dma_start(nrm[:, :], nrm_in[0]).then_inc(nrm_ld, 16)
            sp.dma_start(WA, wa_in[0]).then_inc(wa_ld, 16)
            sp.dma_start(bias[:, :], bias_in[0:1, :].broadcast_to([P, 4 * D])).then_inc(bias_ld, 16)
            sp.dma_start(WB, wb_in[0]).then_inc(wb_ld, 16)
            sp.dma_start(WC[:, :], wc_in[0]).then_inc(wc_ld, 16)
            sp.dma_start(vec[:, :], vec_in[0:1, :].broadcast_to([P, 3 * D])).then_inc(vec_ld, 16)
            sp.dma_start(WT[:, :], wt_in).then_inc(wt_ld, 16)
            sp.dma_start(WF[:, :, :], wf_in).then_inc(wf_ld, 16)
            sp.wait_ge(nb_set, 1)
            nb = sp.value_load(NB[0:1, 0:1], min_val=1, max_val=NBLK)

            def context_blocks(l):
                with sp.Fori(0, nb) as kb:
                    sp.wait_ge(vc_full, l * nb + kb)
                    sp.dma_start(CT[:, :, :, :], ctx_in[kb]).then_inc(ct_ld, 16)

            with sp.Fori(0, NL - 1) as l:
                context_blocks(l)
                sp.wait_ge(*emptied(l, "v1"))
                sp.wait_ge(xbo_set, (l + 1) * B)
                sp.dma_start(bias[:, :], bias_in[l + 1].rearrange("(a n) -> a n", a=1).broadcast_to([P, 4 * D])).then_inc(bias_ld, 16)
                sp.wait_ge(*filled(l, "wo1"))
                sp.dma_start(WA, wa_in[l + 1]).then_inc(wa_ld, 16)
                sp.wait_ge(*filled(l, "cwo1"))
                sp.dma_start(WB, wb_in[l + 1]).then_inc(wb_ld, 16)
                sp.wait_ge(*emptied(l, "n21"))
                sp.dma_start(nrm[:, :], nrm_in[l + 1]).then_inc(nrm_ld, 16)
                sp.wait_ge(*filled(l, "y1"))
                sp.dma_start(WC[:, :], wc_in[l + 1]).then_inc(wc_ld, 16)
            context_blocks(NL - 1)
            for t in range(4):
                sp.wait_ge(*emptied(NL, f"d{t}"))
                sp.dma_start(out[t], X[:, t, :]).then_inc(stored, 16)
            sp.wait_ge(stored, 4 * 16)

        @block.tensor
        def _(pe):
            def transposes(l, use, src, b):
                pe.wait_ge(*free_for(l, use))
                for k in range(KT):
                    for t in range(QT):
                        mm = pe.transpose(bank(use)[:, k * L + t * P:k * L + (t + 1) * P],
                                          src[:, t, k * P:(k + 1) * P], ident)
                mm.then_inc(full(use), 1)

            def project(l, use, col, lhs, rhs, n=D):
                for k in range(KT):
                    mm = pe.matmul(bank(use)[:, col:col + n], lhs(k), rhs(k), start=(k == 0), stop=(k == KT - 1))
                return mm

            def norm_T(l, i, b):
                pe.wait_ge(h_set, l * NORMS + i * B + b + 1)
                transposes(l, f"n{i}{b}", hs[:, 2 * b:2 * b + 2, :], b)

            def qkv(l, b):
                pe.wait_ge(*emptied(l, f"n0{b}"))
                pe.wait_ge(wa_ld, l * 16 + 16)
                for t in range(QT):
                    pe.wait_ge(*free_for(l, f"qk{b}{t}"))
                    project(l, f"qk{b}{t}", 0, lambda k: hT[b][:, k, t * P:(t + 1) * P],
                            lambda k: Wqkv[:, k, 0:2 * D], 2 * D).then_inc(full(f"qk{b}{t}"), 1)
                pe.wait_ge(*free_for(l, f"v{b}"))
                for t in range(QT):
                    mm = project(l, f"v{b}", t * D, lambda k: hT[b][:, k, t * P:(t + 1) * P],
                                 lambda k: Wqkv[:, k, 2 * D:3 * D])
                mm.then_inc(full(f"v{b}"), 1)

            def rotated_T(l, b):
                pe.wait_ge(qr_set, l * B + b + 1)
                for k in range(KT):
                    use = f"tq{b}{k}"
                    pe.wait_ge(*free_for(l, use))
                    for w in range(2):
                        for t in range(QT):
                            mm = pe.transpose(bank(use)[:, w * L + t * P:w * L + (t + 1) * P],
                                              QR[b][:, t, w * D + k * P:w * D + (k + 1) * P], ident)
                    mm.then_inc(full(use), 1)

            def self_scores(l, i):
                b, (q, h0, nh, keys) = i // len(SELF), SELF[i % len(SELF)]
                if i % len(SELF) == 0:
                    pe.wait_ge(*emptied(l, f"tq{b}0"))
                    pe.wait_ge(*emptied(l, f"tq{b}1"))
                if i >= SBANKS:
                    pe.wait_ge(s_exp, l * NSELF + i - SBANKS + 1)
                S = psS[i % SBANKS]
                pe.matmul(S[:, :].rearrange("p (h k) -> p h k", h=nh), identB[:, :],
                          causB[:, 2 * P - keys:2 * P].unsqueeze(1).broadcast_to([P, nh, keys]),
                          start=True, stop=False, skip_group_check=True)
                for j in range(nh):
                    h = h0 + j
                    mm = pe.matmul(S[:, j * keys:(j + 1) * keys], QM[b][:, h // HT, h % HT, q * P:(q + 1) * P],
                                   kTs[b][:, h // HT, 0:keys], start=False, stop=True, skip_group_check=True)
                mm.then_inc(s_full, 1)

            def self_probs_T(l, i):
                pe.wait_ge(s_exp, l * NSELF + i + 1)
                if i >= PBANKS:
                    pe.wait_ge(t_copied, l * NSELF + i - PBANKS + 1)
                for j in range(4):
                    mm = pe.transpose(psP[i % PBANKS][:, j * P:(j + 1) * P], Pr[:, i % 3, j * P:(j + 1) * P], ident)
                mm.then_inc(t_full, 1)

            def self_pv(l, i):
                b, (q, h0, nh, keys) = i // len(SELF), SELF[i % len(SELF)]
                first = i % len(SELF) == 0
                if first:
                    pe.wait_ge(*emptied(l, f"v{b}"))
                    if b:
                        pe.wait_ge(on_set, l * B + b)
                pe.wait_ge(t_copied, l * NSELF + i + 1)
                nk = keys // P
                for j in range(nh):
                    h = h0 + j
                    for k in range(nk):
                        mm = pe.matmul(psO[:, q * D + h * HD:q * D + (h + 1) * HD],
                                       PT[:, i % 3, (j * nk + k) * P:(j * nk + k + 1) * P],
                                       V[b][:, k, h * HD:(h + 1) * HD],
                                       start=(first and j == 0 and k == 0), stop=True, skip_group_check=True)
                mm.then_inc(pv_done, 1)

            def out_T(l, b, use, src, ready, value):
                pe.wait_ge(ready, value)
                transposes(l, use, src, b)

            def out_proj(l, b, use, W, source):
                pe.wait_ge(*emptied(l, source))
                pe.wait_ge(*free_for(l, use))
                for t in range(QT):
                    mm = project(l, use, t * D, lambda k: oT[b][:, k, t * P:(t + 1) * P], lambda k: W[:, k, :])
                mm.then_inc(full(use), 1)

            def cross_q(l, b):
                pe.wait_ge(*emptied(l, f"n1{b}"))
                pe.wait_ge(wb_ld, l * 16 + 16)
                for m in range(KT):
                    use = f"qc{b}{m}"
                    pe.wait_ge(*free_for(l, use))
                    project(l, use, 0, lambda k: Wqc[:, k, m * P:(m + 1) * P],
                            lambda k: hT[b][:, k, :]).then_inc(full(use), 1)

            def cross_kv(l, c):
                pe.wait_ge(ct_ld, c * 16 + 16)
                pe.wait_ge(d_free[0], l * LAYER_TOTAL[0] + BEFORE_CROSS[0])
                pe.wait_ge(kc_set, c)
                for m in range(KT):
                    for k in range(KT):
                        mm = pe.matmul(psD[0][:, m * B * P:(m + 1) * B * P], Wkv[:, k, m * P:(m + 1) * P],
                                       CT[:, k, :, :].rearrange("p b n -> p (b n)"), start=(k == 0), stop=(k == KT - 1))
                mm.then_inc(kc_full, 1)
                pe.wait_ge(d_free[1], l * LAYER_TOTAL[1] + BEFORE_CROSS[1])
                pe.wait_ge(vc_set, c)
                for b in range(B):
                    for k in range(KT):
                        mm = pe.matmul(psD[1][:, b * D:(b + 1) * D], CT[:, k, b, :], Wkv[:, k, D:2 * D],
                                       start=(k == 0), stop=(k == KT - 1))
                mm.then_inc(vc_full, 1)

            def cross_scores(l, c, i):
                b, q, h0 = CROSS[i]
                if i == 0:
                    pe.wait_ge(mask_set, c + 1)
                    pe.wait_ge(kc_set, c + 1)
                if i % (NCROSS // B) == 0:
                    pe.wait_ge(*emptied(l, f"qc{b}0"))
                    pe.wait_ge(*emptied(l, f"qc{b}1"))
                if i >= SBANKS:
                    pe.wait_ge(c_exp, c * NCROSS + i - SBANKS + 1)
                S = psS[i % SBANKS]
                pe.matmul(S[:, :].rearrange("p (h k) -> p h k", h=4), identB[:, :],
                          maskB[:, 2 * b + q, :].unsqueeze(1).broadcast_to([P, 4, P]),
                          start=True, stop=False, skip_group_check=True)
                for j in range(4):
                    h = h0 + j
                    mm = pe.matmul(S[:, j * P:(j + 1) * P], QM[b][:, h // HT, h % HT, q * P:(q + 1) * P],
                                   KC[:, h // HT, b, :], start=False, stop=True, skip_group_check=True)
                mm.then_inc(cs_full, 1)

            def cross_probs_T(c, i):
                pe.wait_ge(c_exp, c * NCROSS + i + 1)
                if i >= PBANKS:
                    pe.wait_ge(ct_copied, c * NCROSS + i - PBANKS + 1)
                for j in range(4):
                    mm = pe.transpose(psP[i % PBANKS][:, j * P:(j + 1) * P], Pr[:, i % 3, j * P:(j + 1) * P], ident)
                mm.then_inc(ct_full, 1)

            def cross_pv(c, i):
                b, q, h0 = CROSS[i]
                first = i % (NCROSS // B) == 0
                if i == 0:
                    pe.wait_ge(vc_set, c + 1)
                if first:
                    pe.wait_ge(or_added, c * B + b)
                pe.wait_ge(ct_copied, c * NCROSS + i + 1)
                for j in range(4):
                    h = h0 + j
                    mm = pe.matmul(psO[:, q * D + h * HD:q * D + (h + 1) * HD], PT[:, i % 3, j * P:(j + 1) * P],
                                   VC[:, b, h * HD:(h + 1) * HD], start=(first and j == 0), stop=True,
                                   skip_group_check=True)
                mm.then_inc(cpv_done, 1)

            def gate_up(l, b, f):
                use = f"gu{b}{f}"
                if f == 0:
                    pe.wait_ge(*emptied(l, f"n2{b}"))
                    pe.wait_ge(wc_ld, l * 16 + 16)
                pe.wait_ge(*free_for(l, use))
                for w, W in enumerate((Wg, Wu)):
                    mm = project(l, use, w * L, lambda k: W[:, k, f * P:(f + 1) * P], lambda k: hT[b][:, k, :])
                mm.then_inc(full(use), 1)

            def down(l, b):
                use = f"y{b}"
                pe.wait_ge(*emptied(l, f"gu{b}{FT - 1}"))
                pe.wait_ge(*free_for(l, use))
                for t in range(QT):
                    for f in range(FT):
                        mm = pe.matmul(bank(use)[:, t * D:(t + 1) * D], AT[b][:, f, t * P:(t + 1) * P], Wd[:, f, :],
                                       start=(f == 0), stop=(f == FT - 1))
                mm.then_inc(full(use), 1)

            pe.wait_ge(c_ld, 16)
            pe.wait_ge(consts_set, 2)
            pe.wait_ge(nb_set, 1)
            nb = pe.value_load(NB[0:1, 0:1], min_val=1, max_val=NBLK)
            with pe.Fori(0, NL) as l:
                for b in range(B):
                    norm_T(l, 0, b)
                    qkv(l, b)
                for b in range(B):
                    rotated_T(l, b)
                self_scores(l, 0)
                self_scores(l, 1)
                for i in range(NSELF):
                    if i + 2 < NSELF:
                        self_scores(l, i + 2)
                    self_probs_T(l, i)
                    if i:
                        self_pv(l, i - 1)
                    if i == 14:
                        out_T(l, 0, "oT0", On[0], on_set, l * B + 1)
                    if i == 15:
                        out_proj(l, 0, "wo0", Wo, "oT0")
                    if i == 20:
                        norm_T(l, 1, 0)
                    if i == 22:
                        cross_q(l, 0)
                self_pv(l, NSELF - 1)
                out_T(l, 1, "oT1", On[1], on_set, l * B + 2)
                out_proj(l, 1, "wo1", Wo, "oT1")
                norm_T(l, 1, 1)
                cross_q(l, 1)
                with pe.Fori(0, nb) as kb:
                    c = pe.snap(l * nb + kb)
                    cross_kv(l, c)
                    cross_scores(l, c, 0)
                    cross_scores(l, c, 1)
                    for i in range(NCROSS):
                        if i + 2 < NCROSS:
                            cross_scores(l, c, i + 2)
                        cross_probs_T(c, i)
                        if i:
                            cross_pv(c, i - 1)
                    cross_pv(c, NCROSS - 1)
                for b in range(B):
                    out_T(l, b, f"coT{b}", On[b], con_set, l * B + b + 1)
                    out_proj(l, b, f"cwo{b}", Woc, f"coT{b}")
                norm_T(l, 2, 0)
                for f in range(FT):
                    gate_up(l, 0, f)
                norm_T(l, 2, 1)
                for f in range(FT):
                    gate_up(l, 1, f)
                    if f == 1:
                        down(l, 0)
                down(l, 1)

            pe.wait_ge(wt_ld, 16)
            for b in range(B):
                pe.wait_ge(an_set, b + 1)
                transposes(NL, f"an{b}", hs[:, 2 * b:2 * b + 2, :], b)
                pe.wait_ge(*emptied(NL, f"an{b}"))
                for m in range(KT):
                    pe.wait_ge(*free_for(NL, f"wq{m}{b}"))
                    project(NL, f"wq{m}{b}", 0, lambda k: Wt[:, 0, k, m * P:(m + 1) * P],
                            lambda k: hT[b][:, k, :]).then_inc(full(f"wq{m}{b}"), 1)
                pe.wait_ge(*free_for(NL, f"wk{b}"))
                for m in range(KT):
                    mm = project(NL, f"wk{b}", m * L, lambda k: Wt[:, 1, k, m * P:(m + 1) * P], lambda k: hT[b][:, k, :])
                mm.then_inc(full(f"wk{b}"), 1)
                pe.wait_ge(*free_for(NL, f"wv{b}"))
                for t in range(QT):
                    mm = project(NL, f"wv{b}", t * D, lambda k: hT[b][:, k, t * P:(t + 1) * P], lambda k: Wt[:, 2, k, :])
                mm.then_inc(full(f"wv{b}"), 1)

            pe.wait_ge(asum_set, 3)
            pe.wait_ge(pool_set, 1)
            pe.wait_ge(*free_for(NL, "sum"))
            pe.matmul(bank("sum")[:, 0:3], ones[:, :], asum[:, :], start=True, stop=True).then_inc(full("sum"), 1)

            def window_scores(i):
                b, (blk, k, half) = i // 9, WINDOW[i % 9]
                if i % 9 == 0:
                    for use in (f"wq0{b}", f"wq1{b}", f"wk{b}"):
                        pe.wait_ge(*emptied(NL, use))
                if i >= SBANKS:
                    pe.wait_ge(sig_set, i - SBANKS + 1)
                S = psS[i % SBANKS]
                if blk == "corner":
                    for k in range(KT):
                        mm = pe.matmul(S[:, k * P:(k + 1) * P].rearrange("p (h q) -> p h q", h=HT), kTs[b][:, k, 0:P],
                                       QM[b][:, k, :, P:P + HD], start=(k == 0), stop=True, skip_group_check=True)
                else:
                    mm = pe.matmul(S[:, :].rearrange("p (h q) -> p h q", h=4), kTs[b][:, k, blk * P:(blk + 1) * P],
                                   QM[b][:, k, 4 * half:4 * half + 4, blk * P:(blk + 1) * P], start=True, stop=True)
                mm.then_inc(ws_full, 1)

            def window_pv(i):
                b, (blk, k, half) = i // 9, WINDOW[i % 9]
                if i % 9 == 0:
                    pe.wait_ge(*emptied(NL, f"wv{b}"))
                    if b:
                        pe.wait_ge(mo_set, b)
                pe.wait_ge(tau_set, i + 1)
                T = PT[:, i % 3, :]
                if blk == "corner":
                    for h in range(H):
                        mm = pe.matmul(psO[0:HD, D + h * HD:D + (h + 1) * HD], T[:, h * HD:(h + 1) * HD],
                                       V[b][:, 0, h * HD:(h + 1) * HD], start=False, stop=True, skip_group_check=True)
                else:
                    for j in range(4):
                        h = k * HT + 4 * half + j
                        mm = pe.matmul(psO[:, blk * D + h * HD:blk * D + (h + 1) * HD], T[:, j * P:(j + 1) * P],
                                       V[b][:, blk, h * HD:(h + 1) * HD], start=(i % 9 == 0 and j == 0), stop=True,
                                       skip_group_check=True)
                mm.then_inc(wpv_done, 1)

            window_scores(0)
            window_scores(1)
            for i in range(18):
                if i + 2 < 18:
                    window_scores(i + 2)
                window_pv(i)
            for b in range(B):
                out_T(NL, b, f"moT{b}", On[b], mo_set, b + 1)
                out_proj(NL, b, f"mwo{b}", Wt[:, 3, :, :], f"moT{b}")

            for b in range(B):
                pe.wait_ge(xq_set, 2 * b + 2)
                pe.wait_ge(*free_for(NL, f"fn{b}"))
                for k in range(KT):
                    for t in range(QT):
                        mm = pe.transpose(bank(f"fn{b}")[:, :].bitcast(BF16)[:, k * L + t * P:k * L + (t + 1) * P],
                                          xq[:, 2 * b + t, k * P:(k + 1) * P], identB[:, :])
                mm.then_inc(full(f"fn{b}"), 1)
            pe.wait_ge(tern_set, 3)
            for t in range(4):
                pe.wait_ge(*emptied(NL, f"fn{t // 2}"))
                for j in range(2):
                    for w in range(2):
                        use = f"{'gu'[w]}{t}{j}"
                        pe.wait_ge(*free_for(NL, use))
                        Wx = WQ[:, w, :].rearrange("p (k n) -> p k n", k=KT)
                        for k in range(KT):
                            mm = pe.matmul(bank(use)[:, :], xqT[t // 2][:, k, (t % 2) * P:(t % 2 + 1) * P],
                                           Wx[:, k, j * 512:(j + 1) * 512], start=(k == 0), stop=(k == KT - 1))
                        mm.then_inc(full(use), 1)
            WDq = WQ[:, 2, :].rearrange("p (f n) -> p f n", f=FT)
            for t in range(4):
                pe.wait_ge(gq_set, t + 1)
                pe.wait_ge(*free_for(NL, f"gT{t}"))
                for f in range(FT):
                    mm = pe.transpose(bank(f"gT{t}")[:, :].bitcast(BF16)[:, f * P:(f + 1) * P],
                                      GQ(t)[:, f * P:(f + 1) * P], identB[:, :])
                mm.then_inc(full(f"gT{t}"), 1)
                pe.wait_ge(*emptied(NL, f"gT{t}"))
                pe.wait_ge(*free_for(NL, f"d{t}"))
                for f in range(FT):
                    mm = pe.matmul(bank(f"d{t}")[:, 0:D], GQT(t)[:, f * P:(f + 1) * P], WDq[:, f, :],
                                   start=(f == 0), stop=(f == FT - 1))
                mm.then_inc(full(f"d{t}"), 1)

        @block.scalar
        def _(act):
            def squares(i, b, ready, value):
                act.wait_ge(ready, value)
                for t in range(QT):
                    a = nc.scalar.activation(hs[:, 2 * b + t, :], X[:, 2 * b + t, :], ACT.Square,
                                             accum_out=ss[:, i * B + b, t:t + 1])
                a.then_inc(ss_set, 1)

            def masked_q(src, b, k):
                for h in range(HT):
                    a = nc.scalar.activation(QM[b][:, k, h, :], src, ACT.Copy, scale=headmask[:, h:h + 1])
                return a

            def self_qk(l, b):
                use = f"tq{b}1"
                act.wait_ge(*filled(l, use))
                nc.scalar.activation(kTs[b][:, 1, :], bank(use)[:, L:2 * L], ACT.Copy)
                a = masked_q(bank(use)[:, 0:L], b, 1)
                a.then_inc(free(use), 1)

            def self_exp(l, i):
                b, (q, h0, nh, keys) = i // len(SELF), SELF[i % len(SELF)]
                act.wait_ge(s_max, l * NSELF + i + 1)
                if i >= 3:
                    act.wait_ge(t_full, l * NSELF + i - 2)
                for j in range(nh):
                    s = q * H + h0 + j
                    a = nc.scalar.activation(Pr[:, i % 3, j * keys:(j + 1) * keys],
                                             psS[i % SBANKS][:, j * keys:(j + 1) * keys], ACT.Exp,
                                             bias=nms[:, b, s:s + 1], accum_out=lS[:, b, s:s + 1])
                a.then_inc(s_exp, 1)

            def copy_oT(l, b, use):
                act.wait_ge(*filled(l, use))
                a = nc.scalar.activation(oT[b][:, :, :].rearrange("p k n -> p (k n)"), bank(use)[:, :], ACT.Copy)
                a.then_inc(free(use), 1)

            def cross_qm(l, b):
                use = f"qc{b}1"
                act.wait_ge(*filled(l, use))
                a = masked_q(bank(use)[:, 0:L], b, 1)
                a.then_inc(free(use), 1)

            def cross_exp(c, i):
                b, q, h0 = CROSS[i]
                act.wait_ge(c_max, c * NCROSS + i + 1)
                if i >= 3:
                    act.wait_ge(ct_full, c * NCROSS + i - 2)
                if i % (NCROSS // B) == 0:
                    act.wait_ge(or_scaled, c * B)
                for j in range(4):
                    s = q * H + h0 + j
                    a = nc.scalar.activation(Pr[:, i % 3, j * P:(j + 1) * P], psS[i % SBANKS][:, j * P:(j + 1) * P],
                                             ACT.Exp, bias=nmN[:, b, s:s + 1], accum_out=lB[:, b, s:s + 1])
                a.then_inc(c_exp, 1)

            def alpha(c, b):
                act.wait_ge(dm_set, c * B + b + 1)
                act.wait_ge(or_scaled, c * B + b)
                nc.scalar.activation(al[:, b, :], dm[:, b, :], ACT.Exp).then_inc(al_set, 1)

            def gate(l, b, f):
                use, n = f"gu{b}{f}", b * FT + f
                act.wait_ge(*filled(l, use))
                if n >= 2:
                    act.wait_ge(*emptied(l, f"gu{(n - 2) // FT}{(n - 2) % FT}"))
                nc.scalar.activation(SG[:, n % 2, :], bank(use)[:, 0:L], ACT.Silu).then_inc(sg_set, 1)

            act.wait_ge(c_ld, 16)
            act.wait_ge(nb_set, 1)
            nb = act.value_load(NB[0:1, 0:1], min_val=1, max_val=NBLK)
            for b in range(B):
                squares(0, b, x_first, b + 1)
            with act.Fori(0, NL) as l:
                for b in range(B):
                    self_qk(l, b)
                for i in range(NSELF):
                    self_exp(l, i)
                    if i == 15:
                        copy_oT(l, 0, "oT0")
                    if i == 17:
                        squares(1, 0, *emptied(l, "wo0"))
                cross_qm(l, 0)
                copy_oT(l, 1, "oT1")
                squares(1, 1, *emptied(l, "wo1"))
                cross_qm(l, 1)
                with act.Fori(0, nb) as kb:
                    c = act.snap(l * nb + kb)
                    act.wait_ge(vc_full, c + 1)
                    act.wait_ge(cpv_done, c * NCROSS)
                    nc.scalar.activation(VC[:, :, :].rearrange("p b n -> p (b n)"), psD[1][:, :], ACT.Copy)\
                        .then_inc(vc_set, 1)
                    for i in range(NCROSS):
                        cross_exp(c, i)
                        if i == NCROSS // B + 1:
                            alpha(c, 0)
                    alpha(c, 1)
                for b in range(B):
                    copy_oT(l, b, f"coT{b}")
                    squares(2, b, *emptied(l, f"cwo{b}"))
                for b in range(B):
                    for f in range(FT):
                        gate(l, b, f)
                for b in range(B):
                    squares(0, b, *emptied(l, f"y{b}"))

            act.wait_ge(wf_ld, 16)
            for w in range(3):
                if w:
                    act.wait_ge(asum_set, w)
                nc.scalar.activation(AT[0][:, :, :].rearrange("p f n -> p (f n)"), WF[:, w, :],
                                     ACT.Abs, accum_out=asum[:, w:w + 1]).then_inc(asum_set, 1)

            for b in range(B):
                act.wait_ge(*filled(NL, f"wq1{b}"))
                a = masked_q(bank(f"wq1{b}")[:, 0:L], b, 1)
                a.then_inc(free(f"wq1{b}"), 1)
                act.wait_ge(*filled(NL, f"wv{b}"))
                a = nc.scalar.activation(V[b][:, :, :].rearrange("p t n -> p (t n)"), bank(f"wv{b}")[:, :], ACT.Copy)
                a.then_inc(free(f"wv{b}"), 1)
            for i in range(18):
                n = 2 * P if WINDOW[i % 9][0] == "corner" else 512
                act.wait_ge(ws_full, i + 1)
                if i >= 3:
                    act.wait_ge(tau_set, i - 2)
                nc.scalar.activation(Pr[:, i % 3, 0:n], psS[i % SBANKS][:, 0:n], ACT.Sigmoid).then_inc(sig_set, 1)
            for b in range(B):
                act.wait_ge(*filled(NL, f"moT{b}"))
                a = nc.scalar.activation(oT[b][:, :, :].rearrange("p k n -> p (k n)"), bank(f"moT{b}")[:, :], ACT.Copy)
                a.then_inc(free(f"moT{b}"), 1)
            for t in range(4):
                act.wait_ge(sgu_set, 2)
                for j in range(2):
                    use = f"g{t}{j}"
                    act.wait_ge(*filled(NL, use))
                    a = nc.scalar.activation(GR(t)[:, j * 512:(j + 1) * 512], bank(use)[:, :], ACT.Silu,
                                             scale=sgu[:, t, 0:1])
                    a.then_inc(free(use), 1)
            for t in range(4):
                act.wait_ge(*filled(NL, f"gT{t}"))
                a = nc.scalar.activation(GQT(t), bank(f"gT{t}")[:, :].bitcast(BF16), ACT.Copy)
                a.then_inc(free(f"gT{t}"), 1)

        @block.vector
        def _(dve):
            steps = [0]

            def done(ins):
                steps[0] += 1
                ins.then_inc(v_step, 1)
                dve.wait_ge(v_step, steps[0])

            def mean_square(l, i, b):
                dve.wait_ge(ss_set, l * NORMS + i * B + b + 1)
                dve.tensor_scalar(ms[:, i * B + b, :], ss[:, i * B + b, :], 1.0 / D, RMS_EPS, ALU.mult, ALU.add)\
                   .then_inc(ms_set, 1)

            def normalise(l, i, b):
                dve.wait_ge(rstd_set, l * NORMS + i * B + b + 1)
                for t in range(QT):
                    v = dve.tensor_scalar(hs[:, 2 * b + t, :], X[:, 2 * b + t, :], rstd[:, i * B + b, t:t + 1], None,
                                          ALU.mult)
                v.then_inc(h_set, 1)

            def weigh_T(l, i, b):
                use = f"n{i}{b}"
                dve.wait_ge(nrm_ld, l * 16 + 16)
                dve.wait_ge(*filled(l, use))
                for k in range(KT):
                    v = dve.tensor_scalar(hT[b][:, k, :], bank(use)[:, k * L:(k + 1) * L],
                                          nrm[:, i * KT + k:i * KT + k + 1], None, ALU.mult)
                v.then_inc(free(use), 1)

            def biased_qkv(l, b):
                dve.wait_ge(bias_ld, l * 16 + 16)
                for t in range(QT):
                    use = f"qk{b}{t}"
                    dve.wait_ge(*filled(l, use))
                    v = dve.tensor_tensor(QK[b][:, t, :], bank(use)[:, :], bias[:, 0:2 * D], ALU.add)
                    v.then_inc(free(use), 1)
                dve.wait_ge(*filled(l, f"v{b}"))
                v = dve.tensor_tensor(V[b][:, :, :], tiles(bank(f"v{b}")[:, :]),
                                      bias[:, 2 * D:3 * D].unsqueeze(1).broadcast_to([P, QT, D]), ALU.add)
                v.then_inc(free(f"v{b}"), 1)

            def cosines(l, b):
                for t in range(QT):
                    dve.wait_ge(*emptied(l, f"qk{b}{t}"))
                dve.tensor_tensor(QR[b][:, :, :].rearrange("p t (h d) -> p t h d", d=HD),
                                  QK[b][:, :, :].rearrange("p t (h d) -> p t h d", d=HD),
                                  cos.unsqueeze(2).broadcast_to([P, QT, 2 * H, HD]), ALU.mult).then_inc(cos_set, 1)

            def add_sines(l, b):
                dve.wait_ge(cos_set, l * B + b + 1)
                dve.wait_ge(sin_set, l * B + b + 1)
                dve.tensor_tensor(QR[b][:, :, :], QR[b][:, :, :], RT[:, :, :], ALU.add).then_inc(qr_set, 1)

            def masked_q(src, b):
                return dve.tensor_tensor(QM[b][:, 0, :, :], src.unsqueeze(1).broadcast_to([P, HT, L]),
                                         headmask.unsqueeze(2).broadcast_to([P, HT, L]), ALU.mult)

            def self_qk(l, b):
                use = f"tq{b}0"
                dve.wait_ge(*filled(l, use))
                dve.tensor_copy(kTs[b][:, 0, :], bank(use)[:, L:2 * L])
                v = masked_q(bank(use)[:, 0:L], b)
                v.then_inc(free(use), 1)

            def self_max(l, i):
                b, (q, h0, nh, keys) = i // len(SELF), SELF[i % len(SELF)]
                s = q * H + h0
                dve.wait_ge(s_full, l * NSELF + i + 1)
                dve.tensor_reduce(nms[:, b, s:s + nh], psS[i % SBANKS][:, :].rearrange("p (h k) -> p h k", h=nh),
                                  AX_X, ALU.max, negate=True).then_inc(s_max, 1)

            def self_copy_T(l, i):
                dve.wait_ge(t_full, l * NSELF + i + 1)
                if i >= 3:
                    dve.wait_ge(pv_done, l * NSELF + i - 2)
                dve.tensor_copy(PT[:, i % 3, :], psP[i % PBANKS][:, :]).then_inc(t_copied, 1)

            def divide(src, denominator, b, step_set, step_value, out_set):
                dve.reciprocal(rl[:, b, :], denominator).then_inc(step_set, 1)
                dve.wait_ge(step_set, step_value)
                dve.tensor_tensor(heads(On[b][:, :, :]), src,
                                  rl[:, b, :].unsqueeze(2).broadcast_to([P, QT * H, HD]), ALU.mult).then_inc(out_set, 1)

            def self_out(l, b):
                dve.wait_ge(pv_done, l * NSELF + (b + 1) * len(SELF))
                divide(psO[:, :].rearrange("p (h d) -> p h d", d=HD), lS[:, b, :], b, rl_set, l * B + b + 1, on_set)

            def residual(l, b, use):
                dve.wait_ge(*filled(l, use))
                x = X[:, 2 * b:2 * b + 2, :]
                v = dve.tensor_tensor(x, x, tiles(bank(use)[:, :]), ALU.add)
                v.then_inc(free(use), 1)

            def cross_qm(l, b):
                use = f"qc{b}0"
                dve.wait_ge(*filled(l, use))
                v = masked_q(bank(use)[:, 0:L], b)
                v.then_inc(free(use), 1)

            def cross_max(l, c, i):
                b, q, h0 = CROSS[i]
                s = q * H + h0
                dve.wait_ge(cs_full, c * NCROSS + i + 1)
                dve.tensor_reduce(nmB[:, b, s:s + 4], psS[i % SBANKS][:, :].rearrange("p (h k) -> p h k", h=4),
                                  AX_X, ALU.max, negate=True).then_inc(c_bmax, 1)
                dve.wait_ge(c_bmax, c * NCROSS + i + 1)
                if i == 0:
                    dve.wait_ge(nmr_set, l + 1 + c * B)
                dve.tensor_tensor(nmN[:, b, s:s + 4], nmR[:, b, s:s + 4], nmB[:, b, s:s + 4], ALU.min)\
                   .then_inc(c_max, 1)

            def block_mask(l, c):
                dve.wait_ge(mask_rel, 2 * (c + l) + 2)
                for t in range(4):
                    dve.tensor_scalar(mA[:, t, :], iota, segR[:, t:t + 1], NEG, ALU.is_gt, ALU.mult)
                    v = dve.tensor_scalar(mB[:, t, :], iota, segL[:, t:t + 1], NEG, ALU.is_le, ALU.mult)
                v.then_inc(mask_cmp, 1)
                dve.wait_ge(mask_cmp, c + 1)
                dve.wait_ge(cs_full, c * NCROSS)
                dve.tensor_tensor(maskB[:, :, :], mA[:, :, :], mB[:, :, :], ALU.add).then_inc(mask_set, 1)

            def cross_copy_T(c, i):
                dve.wait_ge(ct_full, c * NCROSS + i + 1)
                if i >= 3:
                    dve.wait_ge(cpv_done, c * NCROSS + i - 2)
                dve.tensor_copy(PT[:, i % 3, :], psP[i % PBANKS][:, :]).then_inc(ct_copied, 1)

            def add_block(c, b):
                dve.wait_ge(cpv_done, c * NCROSS + (b + 1) * (NCROSS // B))
                dve.wait_ge(or_scaled, c * B + b + 1)
                o = OR[b][:, :, :].rearrange("p t n -> p (t n)")
                dve.tensor_tensor(o, o, psO[:, :], ALU.add).then_inc(or_added, 1)

            def hidden(l, b, f):
                use, n = f"gu{b}{f}", b * FT + f
                dve.wait_ge(sg_set, l * B * FT + n + 1)
                v = dve.tensor_tensor(AT[b][:, f, :], SG[:, n % 2, :], bank(use)[:, L:2 * L], ALU.mult)
                v.then_inc(free(use), 1)

            def layernorm(n, b, src, dst, last):
                for t in range(QT):
                    v = dve.bn_stats(bst[:, n, t, :], src[:, 2 * b + t, :])
                done(v)
                for t in range(QT):
                    v = dve.bn_aggr(mv[:, n, t, :], bst[:, n, t, :])
                done(v)
                dve.tensor_scalar(lve[:, n, :], mv[:, n, :, 1], LN_EPS, None, ALU.add).then_inc(ln_var, 1)
                dve.wait_ge(ln_rstd, n + 1)
                for t in range(QT):
                    v = dve.tensor_scalar(dst[:, 2 * b + t, :], src[:, 2 * b + t, :], mv[:, n, t, 0:1],
                                          lrs[:, n, t:t + 1], ALU.subtract, ALU.mult)
                last(v)

            def quantise_scales(t, n, src, which):
                a = (am, am2)[which]
                done(dve.tensor_reduce(a[:, t:t + n, 0], src, AX_X, ALU.max, apply_absolute_value=True))
                done(dve.tensor_scalar(a[:, t:t + n, 1], a[:, t:t + n, 0], 1e-5, None, ALU.max))
                done(dve.reciprocal(a[:, t:t + n, 2], a[:, t:t + n, 1]))
                dve.tensor_scalar(a[:, t:t + n, 3], a[:, t:t + n, 1], 1.0 / 127.0, None, ALU.mult)
                done(dve.tensor_scalar(a[:, t:t + n, 2], a[:, t:t + n, 2], 127.0, None, ALU.mult))

            def round_tile(src, t, which, dst, done_set):
                a = (am, am2)[which]
                done(dve.tensor_scalar(src, src, a[:, t, 2:3], MAGIC, ALU.mult, ALU.add))
                done(dve.tensor_scalar(src, src, MAGIC, 127.0, ALU.subtract, ALU.min))
                dve.tensor_scalar(dst, src, -128.0, None, ALU.max).then_inc(done_set, 1)

            dve.wait_ge(seg_ld, 32)
            done(dve.tensor_copy(rowF[:, :], rowI[:, :]))
            dve.tensor_reduce(few[:, 1:2], rowF[:, :], AX_X, ALU.min)
            done(dve.tensor_reduce(few[:, 0:1], rowF[:, :], AX_X, ALU.max))
            dve.wait_ge(c_ld, 16)
            dve.tensor_scalar(few[:, 3:4], few[:, 1:2], 0.0, float(NBLK), ALU.is_lt, ALU.mult)
            done(dve.tensor_scalar(cnt[:, :], iota[0:1, 0:NBLK], float(P), None, ALU.mult))
            done(dve.tensor_scalar(cnt[:, :], cnt[:, :], few[:, 0:1], None, ALU.is_le))
            done(dve.tensor_reduce(few[:, 2:3], cnt[:, :], AX_X, ALU.add))
            dve.tensor_tensor(NB[:, :], few[:, 2:3], few[:, 3:4], ALU.max).then_inc(nb_set, 1)
            dve.tensor_copy(segF[:, :], segI[:, :]).then_inc(consts_set, 1)
            dve.tensor_copy(identB[:, :], ident)
            dve.tensor_copy(causB[:, :], const[:, C_CAUSAL:C_CAUSAL + 2 * P]).then_inc(consts_set, 1)
            dve.wait_ge(x_ld, 16)
            for b in range(B):
                layernorm(b, b, X0, X, lambda v: v.then_inc(x_first, 1))

            dve.wait_ge(nb_set, 1)
            nb = dve.value_load(NB[0:1, 0:1], min_val=1, max_val=NBLK)
            with dve.Fori(0, NL) as l:
                for b in range(B):
                    mean_square(l, 0, b)
                    normalise(l, 0, b)
                weigh_T(l, 0, 0)
                biased_qkv(l, 0)
                weigh_T(l, 0, 1)
                cosines(l, 0)
                biased_qkv(l, 1)
                add_sines(l, 0)
                cosines(l, 1)
                add_sines(l, 1)
                for b in range(B):
                    self_qk(l, b)
                self_max(l, 0)
                self_max(l, 1)
                for i in range(NSELF):
                    if i + 2 < NSELF:
                        self_max(l, i + 2)
                    self_copy_T(l, i)
                    if i == 12:
                        self_out(l, 0)
                    if i == 16:
                        dve.wait_ge(xbo_set, l * B + 1)
                        residual(l, 0, "wo0")
                    if i == 18:
                        mean_square(l, 1, 0)
                    if i == 19:
                        normalise(l, 1, 0)
                    if i == 21:
                        weigh_T(l, 1, 0)
                cross_qm(l, 0)
                self_out(l, 1)
                dve.wait_ge(xbo_set, l * B + 2)
                residual(l, 1, "wo1")
                mean_square(l, 1, 1)
                normalise(l, 1, 1)
                weigh_T(l, 1, 1)
                cross_qm(l, 1)
                with dve.Fori(0, nb) as kb:
                    c = dve.snap(l * nb + kb)
                    block_mask(l, c)
                    dve.wait_ge(kc_full, c + 1)
                    dve.tensor_copy(KC[:, :, :, :].rearrange("p k b n -> p (k b n)"), psD[0][:, :]).then_inc(kc_set, 1)
                    cross_max(l, c, 0)
                    cross_max(l, c, 1)
                    for i in range(NCROSS):
                        if i + 2 < NCROSS:
                            cross_max(l, c, i + 2)
                        cross_copy_T(c, i)
                        if i == NCROSS // B:
                            add_block(c, 0)
                    add_block(c, 1)
                for b in range(B):
                    dve.wait_ge(or_added, (l + 1) * nb * B)
                    divide(heads(OR[b][:, :, :]), lR[:, b, :], b, crl_set, l * B + b + 1, con_set)
                for b in range(B):
                    residual(l, b, f"cwo{b}")
                    mean_square(l, 2, b)
                    normalise(l, 2, b)
                weigh_T(l, 2, 0)
                for f in range(FT):
                    hidden(l, 0, f)
                weigh_T(l, 2, 1)
                for f in range(2):
                    hidden(l, 1, f)
                residual(l, 0, "y0")
                for f in range(2, FT):
                    hidden(l, 1, f)
                residual(l, 1, "y1")

            dve.wait_ge(vec_ld, 16)
            for b in range(B):
                mean_square(NL, 0, b)
                dve.wait_ge(rstd_set, NL * NORMS + b + 1)
                for t in range(QT):
                    v = dve.scalar_tensor_tensor(hs[:, 2 * b + t, :], X[:, 2 * b + t, :], rstd[:, b, t:t + 1],
                                                 vec[:, 0:D], ALU.mult, ALU.mult)
                done(v)
                x = X0[:, 2 * b:2 * b + 2, :]
                done(dve.tensor_tensor(x, x, hs[:, 2 * b:2 * b + 2, :], ALU.add))
                layernorm(2 + b, b, X0, hs, lambda v: v.then_inc(an_set, 1))
            for b in range(B):
                dve.wait_ge(*filled(NL, f"an{b}"))
                v = dve.tensor_copy(hT[b][:, :, :].rearrange("p k n -> p (k n)"), bank(f"an{b}")[:, :])
                v.then_inc(free(f"an{b}"), 1)
                dve.wait_ge(*filled(NL, f"wq0{b}"))
                v = masked_q(bank(f"wq0{b}")[:, 0:L], b)
                v.then_inc(free(f"wq0{b}"), 1)
                dve.wait_ge(*filled(NL, f"wk{b}"))
                v = dve.tensor_copy(kTs[b][:, :, :].rearrange("p k n -> p (k n)"), bank(f"wk{b}")[:, :])
                v.then_inc(free(f"wk{b}"), 1)
            dve.wait_ge(*filled(NL, "sum"))
            v = dve.tensor_scalar(mw[:, :], bank("sum")[:, 0:3], 1.0 / (F * D), 1e-5, ALU.mult, ALU.max)
            v.then_inc(free("sum"), 1)
            dve.wait_ge(*emptied(NL, "sum"))
            dve.reciprocal(rw[:, :], mw[:, :]).then_inc(mw_set, 1)

            for i in range(18):
                dve.wait_ge(sig_set, i + 1)
                if i >= 3:
                    dve.wait_ge(wpv_done, i - 2)
                if WINDOW[i % 9][0] == "corner":
                    o, p, m = PT[:, i % 3, 0:2 * P], Pr[:, i % 3, 0:2 * P], corner
                else:
                    o, p, m = PT[:, i % 3, :], Pr[:, i % 3, :], band
                n = m.shape[1]
                h = o.shape[1] // n
                dve.tensor_tensor(o.rearrange("p (h q) -> p h q", q=n), p.rearrange("p (h q) -> p h q", q=n),
                                  m.unsqueeze(1).broadcast_to([P, h, n]), ALU.mult).then_inc(tau_set, 1)
                if i == 9:
                    dve.wait_ge(wpv_done, 9)
                    dve.tensor_copy(On[0][:, :, :].rearrange("p t n -> p (t n)"), psO[:, :]).then_inc(mo_set, 1)
            dve.wait_ge(wpv_done, 18)
            dve.tensor_copy(On[1][:, :, :].rearrange("p t n -> p (t n)"), psO[:, :]).then_inc(mo_set, 1)
            for b in range(B):
                x, y, z = (a[:, 2 * b:2 * b + 2, :] for a in (X0, X, hs))
                dve.wait_ge(*filled(NL, f"mwo{b}"))
                v = dve.tensor_tensor(y, z, tiles(bank(f"mwo{b}")[:, :]), ALU.add)
                v.then_inc(free(f"mwo{b}"), 1)
                dve.wait_ge(*emptied(NL, f"mwo{b}"))
                layernorm(4 + 2 * b, b, X, hs, done)
                done(dve.tensor_tensor(z, z, vec[:, D:2 * D].unsqueeze(1).broadcast_to([P, QT, D]), ALU.mult))
                done(dve.tensor_tensor(z, z, vec[:, 2 * D:3 * D].unsqueeze(1).broadcast_to([P, QT, D]), ALU.add))
                done(dve.tensor_tensor(x, x, z, ALU.add))
                layernorm(5 + 2 * b, b, X0, hs, done)
                quantise_scales(b * 2, 2, z, 0)
                for t in (2 * b, 2 * b + 1):
                    round_tile(hs[:, t, :], t, 0, xq[:, t, :], xq_set)
            for w in range(2):
                dve.tensor_scalar(sgu[:, :, w], am[:, :, 3], mw[:, w:w + 1], None, ALU.mult).then_inc(sgu_set, 1)
            for b in range(B):
                dve.wait_ge(*filled(NL, f"fn{b}"))
                v = dve.tensor_copy(xqT[b][:, :, :].rearrange("p k n -> p (k n)"),
                                    bank(f"fn{b}")[:, :].bitcast(BF16)[:, 0:KT * L])
                v.then_inc(free(f"fn{b}"), 1)
            dve.wait_ge(sgu_set, 2)
            for t in range(4):
                for j in range(2):
                    dve.wait_ge(*filled(NL, f"u{t}{j}"))
                    dve.wait_ge(*emptied(NL, f"g{t}{j}"))
                    v = dve.scalar_tensor_tensor(GU(t)[:, j * 512:(j + 1) * 512], bank(f"u{t}{j}")[:, :],
                                                 sgu[:, t, 1:2], GR(t)[:, j * 512:(j + 1) * 512], ALU.mult, ALU.mult)
                    v.then_inc(free(f"u{t}{j}"), 1)
                for j in range(2):
                    dve.wait_ge(*emptied(NL, f"u{t}{j}"))
                quantise_scales(t, 1, GU(t).unsqueeze(1), 1)
                round_tile(GU(t), t, 1, GQ(t), gq_set)
            done(dve.tensor_scalar(sgu[:, :, 2], am2[:, :, 3], mw[:, 2:3], None, ALU.mult))
            for t in range(4):
                dve.wait_ge(*filled(NL, f"d{t}"))
                v = dve.scalar_tensor_tensor(X[:, t, :], bank(f"d{t}")[:, 0:D], sgu[:, t, 2:3], X0[:, t, :],
                                             ALU.mult, ALU.add)
                v.then_inc(free(f"d{t}"), 1)

        @block.gpsimd
        def _(pool):
            pool.memset(mhalf[:, :], -0.5)
            pool.memset(step[:, :], float(P))
            pool.memset(look[:, :], float(LOOKBACK))
            pool.memset(ones[:, :], 1.0).then_inc(pool_set, 1)

            def rsqrt(l, i, b):
                pool.wait_ge(ms_set, l * NORMS + i * B + b + 1)
                nc.gpsimd.tensor_tensor(rstd[:, i * B + b, :], ms[:, i * B + b, :], mhalf[:, :], ALU.pow)\
                    .then_inc(rstd_set, 1)

            def ln_rsqrt(n):
                pool.wait_ge(ln_var, n + 1)
                nc.gpsimd.tensor_tensor(lrs[:, n, :], lve[:, n, :], mhalf[:, :], ALU.pow).then_inc(ln_rstd, 1)

            def sines(l, b):
                for t in range(QT):
                    pool.wait_ge(*emptied(l, f"qk{b}{t}"))
                pool.wait_ge(qr_set, l * B + b)
                q = QK[b][:, :, :].rearrange("p t (h d) -> p t h d", d=HD)
                r = RT[:, :, :].rearrange("p t (h d) -> p t h d", d=HD)
                for to, of in ((0, HD // 2), (HD // 2, 0)):
                    g = nc.gpsimd.tensor_tensor(r[:, :, :, to:to + HD // 2], q[:, :, :, of:of + HD // 2],
                                                sin[:, :, to:to + HD // 2].unsqueeze(2)
                                                .broadcast_to([P, QT, 2 * H, HD // 2]), ALU.mult)
                g.then_inc(sin_set, 1)

            def add_bo(l, b):
                pool.wait_ge(h_set, l * NORMS + b + 1)
                pool.wait_ge(bias_ld, l * 16 + 16)
                x = X[:, 2 * b:2 * b + 2, :]
                nc.gpsimd.tensor_tensor(x, x, bias[:, 3 * D:4 * D].unsqueeze(1).broadcast_to([P, QT, D]), ALU.add)\
                    .then_inc(xbo_set, 1)

            def clear_running():
                for b in range(B):
                    pool.memset(OR[b][:, :, :], 0.0)
                pool.memset(lR[:, :, :], 0.0)
                pool.memset(nmR[:, :, :], NO_MAX).then_inc(nmr_set, 1)

            def rescale(c, b):
                n = (b + 1) * (NCROSS // B)
                pool.wait_ge(c_max, c * NCROSS + n)
                nc.gpsimd.tensor_tensor(dm[:, b, :], nmN[:, b, :], nmR[:, b, :], ALU.subtract).then_inc(dm_set, 1)
                pool.wait_ge(dm_set, c * B + b + 1)
                nc.gpsimd.tensor_tensor(nmR[:, b, :], nmN[:, b, :], ones[:, 0:QT * H], ALU.mult).then_inc(nmr_set, 1)
                pool.wait_ge(al_set, c * B + b + 1)
                nc.gpsimd.tensor_tensor(lR[:, b, :], lR[:, b, :], al[:, b, :], ALU.mult).then_inc(lr_set, 1)
                pool.wait_ge(lr_set, c * B + b + 1)
                pool.wait_ge(c_exp, c * NCROSS + n)
                nc.gpsimd.tensor_tensor(lR[:, b, :], lR[:, b, :], lB[:, b, :], ALU.add)
                pool.wait_ge(or_added, c * B)
                nc.gpsimd.tensor_tensor(heads(OR[b][:, :, :]), heads(OR[b][:, :, :]),
                                        al[:, b, :].unsqueeze(2).broadcast_to([P, QT * H, HD]), ALU.mult)\
                    .then_inc(or_scaled, 1)

            clear_running()
            pool.wait_ge(nmr_set, 1)
            for n in range(B):
                ln_rsqrt(n)
            pool.wait_ge(consts_set, 2)
            pool.wait_ge(nb_set, 1)
            nb = pool.value_load(NB[0:1, 0:1], min_val=1, max_val=NBLK)
            with pool.Fori(0, NL) as l:
                for b in range(B):
                    rsqrt(l, 0, b)
                for b in range(B):
                    add_bo(l, b)
                    sines(l, b)
                for b in range(B):
                    rsqrt(l, 1, b)
                nc.gpsimd.tensor_tensor(segR[:, :], segF[:, :], ones[:, 0:4], ALU.mult).then_inc(mask_rel, 1)
                nc.gpsimd.tensor_tensor(segL[:, :], segF[:, :], look[:, :], ALU.subtract).then_inc(mask_rel, 1)
                with pool.Fori(0, nb) as kb:
                    c = pool.snap(l * nb + kb)
                    pool.wait_ge(mask_set, c + 1)
                    nc.gpsimd.tensor_tensor(segR[:, :], segR[:, :], step[:, :], ALU.subtract).then_inc(mask_rel, 1)
                    nc.gpsimd.tensor_tensor(segL[:, :], segL[:, :], step[:, :], ALU.subtract).then_inc(mask_rel, 1)
                    for b in range(B):
                        rescale(c, b)
                for b in range(B):
                    rsqrt(l, 2, b)
                clear_running()

            for b in range(B):
                rsqrt(NL, 0, b)
                ln_rsqrt(2 + b)
            pool.wait_ge(wf_ld, 16)
            pool.wait_ge(mw_set, 1)
            for w in range(3):
                nc.gpsimd.tensor_scalar(WF[:, w, :], WF[:, w, :], rw[:, w:w + 1], MAGIC, ALU.mult, ALU.add)\
                    .then_inc(tern_step, 1)
                pool.wait_ge(tern_step, 2 * w + 1)
                nc.gpsimd.tensor_scalar(WF[:, w, :], WF[:, w, :], MAGIC, 1.0, ALU.subtract, ALU.min)\
                    .then_inc(tern_step, 1)
                pool.wait_ge(tern_step, 2 * w + 2)
                nc.gpsimd.tensor_scalar(WQ[:, w, :], WF[:, w, :], -1.0, None, ALU.max).then_inc(tern_set, 1)
            for b in range(B):
                ln_rsqrt(4 + 2 * b)
                ln_rsqrt(5 + 2 * b)


def constants():
    import numpy as np

    c = np.zeros((P, C_N), np.float32)
    p = np.arange(P)
    c[:, C_ID:C_ID + P] = np.eye(P, dtype=np.float32)
    c[:, C_CAUSAL + P:C_CAUSAL + 2 * P] = np.where(p[None, :] > p[:, None], NEG, 0.0)
    c[:, C_HEAD:C_HEAD + HT] = np.where(p[:, None] // HD == np.arange(HT)[None, :], SCALE, 0.0)
    inv = (np.float32(1.0) / np.float32(10000.0) ** (np.arange(0, HD, 2, dtype=np.float32) / np.float32(HD))).astype(np.float32)
    f = (np.arange(L, dtype=np.float32)[:, None] * inv[None, :]).astype(np.float32)
    cos, sin = np.cos(f), np.sin(f)
    cos = np.concatenate([cos, cos], 1).reshape(QT, P, HD).transpose(1, 0, 2)
    sin = np.concatenate([-sin, sin], 1).reshape(QT, P, HD).transpose(1, 0, 2)
    c[:, C_COS:C_COS + QT * HD] = cos.reshape(P, -1)
    c[:, C_SIN:C_SIN + QT * HD] = sin.reshape(P, -1)
    c[:, C_IOTA:C_IOTA + P] = p[None, :]
    back = p[None, :] - p[:, None]
    c[:, C_BAND:C_BAND + P] = (back >= 1) & (back <= HD)
    back = P + np.arange(HD)[None, :] - p[:, None]
    c[:, C_CORNER:C_CORNER + HD] = (back >= 1) & (back <= HD)
    return c


def rows_on_partitions(w):
    import numpy as np

    w = np.swapaxes(w, -1, -2)
    lead, (n_in, n_out) = w.shape[:-2], w.shape[-2:]
    w = w.reshape(*lead, n_in // P, P, n_out)
    return np.moveaxis(w, -2, -3).reshape(*lead, P, -1)


def kernel(**inputs):
    import numpy as np
    import concourse.bacc as bacc
    from concourse.bass_utils import run_bass_kernel_spmd as run

    a = {k: np.asarray(v) for k, v in inputs.items()}
    X, A, G = "L0_xattn_", "L0_attn_", "L0_ffn_"
    x = a["x"].reshape(4, P, D).transpose(1, 0, 2)
    ctx = a["ctx_1024"].reshape(B, NBLK, P, KT, P).transpose(1, 4, 3, 0, 2)
    seg = a["itok_BxS_0_255"].reshape(4, P)
    seg = np.concatenate([seg.T.ravel(), seg.ravel()])
    wa = np.concatenate([rows_on_partitions(a[X + "Wqkv"]), rows_on_partitions(a[X + "Wo"])], -1)
    wb = np.concatenate([rows_on_partitions(a[X + n]) for n in ("Wq_c", "Wkv_c", "Wo_c")], -1)
    wc = np.concatenate([rows_on_partitions(a[X + n]) for n in ("Wg", "Wu", "Wd")], -1)
    nrm = np.stack([a[X + n] for n in ("n1", "n2", "n3")], 1).reshape(NL, 3, KT, P).transpose(0, 3, 1, 2).reshape(NL, P, -1)
    bias = np.concatenate([a[X + "bqkv"], a[X + "bo"]], -1)
    vec = np.concatenate([a[X + "nf"], a[A + "gamma"], a[A + "beta"]])[None, :]
    wkv = a[A + "wkv"].reshape(H, 2, HD, D)
    wt = np.concatenate([rows_on_partitions(w) for w in (a[A + "wq"], wkv[:, 0].reshape(D, D), wkv[:, 1].reshape(D, D), a[A + "wo"])], -1)
    wf = np.stack([rows_on_partitions(a[G + n]) for n in ("w_gate", "w_up", "w_down")], 1)
    arrays = {"x": x, "ctx": ctx, "seg": seg, "wa": wa, "wb": wb, "wc": wc, "nrm": nrm, "bias": bias, "vec": vec,
              "wt": wt, "wf": wf, "const": constants()}
    arrays = {k: np.ascontiguousarray(v) for k, v in arrays.items()}
    nc = bacc.Bacc("TRN2", target_bir_lowering=False, num_devices=1)
    args = [nc.dram_tensor(f"in_{k}", v.shape, mybir.dt.from_np(v.dtype), kind="ExternalInput").ap() for k, v in arrays.items()]
    out = nc.dram_tensor("out_x", (4, P, D), F32, kind="ExternalOutput").ap()
    perceiver(nc, *args, out)
    r = run(nc, [{f"in_{k}": v for k, v in arrays.items()}], core_ids=[0])
    return r.results[0]["out_x"].reshape(B, L, D)
```

```python
from contextlib import ExitStack

import concourse.bass as bass
from concourse import mybir

F32 = mybir.dt.float32
BF16 = mybir.dt.bfloat16
I32 = mybir.dt.int32
ALU = mybir.AluOpType
ACT = mybir.ActivationFunctionType
AX_X = mybir.AxisListType.X

P = 128
B, L, D = 2, 256, 256
H, HD = 16, 16
NL = 4
S_CTX = 4096
LOOKBACK = 128
F = 1024
QT = L // P
KT = D // P
HT = H // KT
FT = F // P
NBLK = S_CTX // P
RMS_EPS, LN_EPS = 1e-6, 1e-5
NEG = -1e30
NO_MAX = 3e38
MAGIC = 12582912.0
SCALE = HD ** -0.5

WA_QKV, WA_O, WA_N = 0, KT * 3 * D, KT * 4 * D
WB_Q, WB_KV, WB_O, WB_N = 0, KT * D, KT * 3 * D, KT * 4 * D
WC_G, WC_U, WC_D, WC_N = 0, KT * F, 2 * KT * F, 2 * KT * F + FT * D
C_ID, C_CAUSAL, C_HEAD, C_COS, C_SIN, C_IOTA, C_BAND, C_CORNER = 0, 128, 384, 392, 424, 456, 584, 712
C_N = 728

SELF = [(0, 4 * g, 4, P) for g in range(4)] + [(1, 2 * g, 2, 2 * P) for g in range(8)]
CROSS = [(q, 4 * g, 4, P) for q in range(QT) for g in range(4)]
NSELF, NCROSS = len(SELF), len(CROSS)
GROUPS = [(0, b, *g) for b in range(B) for g in SELF] + [(1, b, *g) for b in range(B) for g in CROSS]
NG = len(GROUPS)
S0, S1, C0, C1 = 0, NSELF, B * NSELF, B * NSELF + NCROSS
WINDOW = [(blk, k, half) for blk in range(QT) for k in range(KT) for half in range(2)] + [("corner", 0, 0)]
NORMS = 3 * B
SBANKS, PBANKS, DBANKS = 3, 2, 2

LAYER_USES = (
    [u for b in range(B) for u in (f"n0{b}", f"qk{b}0", f"qk{b}1", f"v{b}", f"tq{b}0", f"tq{b}1")]
    + [u for b in range(B) for u in (f"oT{b}", f"wo{b}", f"n1{b}", f"kv{b}", f"qc{b}0", f"qc{b}1")]
    + [u for b in range(B) for u in (f"coT{b}", f"cwo{b}", f"n2{b}")]
)
TAIL_USES = (
    [u for b in range(B) for u in (f"an{b}", f"wq0{b}", f"wq1{b}", f"wk{b}", f"wv{b}")] + ["sum"]
    + [u for b in range(B) for u in (f"moT{b}", f"mwo{b}")]
    + [u for b in range(B) for u in (f"fn{b}",)]
    + [f"{w}{t}{j}" for t in range(2 * B) for j in range(2) for w in "gu"]
    + [u for t in range(2 * B) for u in (f"gT{t}", f"d{t}")]
)


def bank_order(uses):
    seen, at = [0] * DBANKS, {}
    for n, u in enumerate(uses):
        at[u] = (n % DBANKS, seen[n % DBANKS])
        seen[n % DBANKS] += 1
    return at, seen


LAYER_AT, LAYER_TOTAL = bank_order(LAYER_USES)
TAIL_AT, _ = bank_order(TAIL_USES)


def perceiver(nc, x_in, ctx_in, seg_in, wa_in, wb_in, wc_in, nrm_in, bias_in, vec_in, wt_in, wf_in, const_in, out):
    stack = ExitStack()
    with stack:
        def sb(name, shape, dt=F32):
            return stack.enter_context(nc.sbuf_tensor(name, shape, dt))

        def ps(name):
            return stack.enter_context(nc.psum_tensor(name, [P, 512], F32))

        def sem(name):
            return stack.enter_context(nc.semaphore(name))

        X0 = sb("X0", [P, 4, D])
        X = sb("X", [P, 4, D])
        hs = sb("hs", [P, 4, D])
        hT = [sb(f"hT{b}", [P, KT, L]) for b in range(B)]
        WAB = sb("WAB", [P, WA_N + WB_N])
        WA, WB = WAB[:, 0:WA_N], WAB[:, WA_N:WA_N + WB_N]
        WC = sb("WC", [P, WC_N])
        nrm = sb("nrm", [P, 3 * KT])
        bias = sb("bias", [P, 4 * D])
        vec = sb("vec", [P, 3 * D])
        WT = sb("WT", [P, KT * 4 * D])
        const = sb("const", [P, C_N])
        identB = sb("identB", [P, P], BF16)
        causB = sb("causB", [P, 2 * P], BF16)
        HID = [sb(f"HID{b}", [P, 2 * QT * 2 * D]) for b in range(B)]
        QK = [HID[b][:, 0:QT * 2 * D].rearrange("p (t n) -> p t n", t=QT) for b in range(B)]
        QR = [HID[b][:, QT * 2 * D:].rearrange("p (t n) -> p t n", t=QT) for b in range(B)]
        AT = [HID[b][:, :].rearrange("p (f n) -> p f n", f=FT) for b in range(B)]
        V = [sb(f"V{b}", [P, QT, D]) for b in range(B)]
        QM = [sb(f"QM{b}", [P, KT, HT, L]) for b in range(B)]
        kTs = [sb(f"kTs{b}", [P, KT, L]) for b in range(B)]
        Pr = sb("Pr", [P, 3, 512])
        PT = sb("PT", [P, 3, 512])
        ON = sb("ON", [P, B * QT * D])
        On = [ON[:, b * QT * D:(b + 1) * QT * D].rearrange("p (t n) -> p t n", t=QT) for b in range(B)]
        RT = ON[:, :].rearrange("p (t n) -> p t n", t=QT)
        oT = [sb(f"oT{b}", [P, KT, L]) for b in range(B)]
        CT = sb("CT", [P, KT, B, P])
        CTg = sb("CTg", [P, KT, P])
        KV = [sb(f"KV{b}", [P, 2 * D]) for b in range(B)]
        KC = [KV[b][:, 0:D].rearrange("p (k n) -> p k n", k=KT) for b in range(B)]
        VC = [KV[b][:, D:2 * D] for b in range(B)]
        OR = [sb(f"OR{b}", [P, QT, D]) for b in range(B)]
        SG = sb("SG", [P, 2, L])
        ss = sb("ss", [P, NORMS, QT])
        ms = sb("ms", [P, NORMS, QT])
        rstd = sb("rstd", [P, NORMS, QT])
        mhalf = sb("mhalf", [P, QT])
        segR = sb("segR", [P, 4])
        nms = sb("nms", [P, B, QT * H])
        lS = sb("lS", [P, B, QT * H])
        rl = sb("rl", [P, B, QT * H])
        nmB = sb("nmB", [P, B, QT * H])
        nmN = sb("nmN", [P, B, QT * H])
        nmR = sb("nmR", [P, B, QT * H])
        lB = sb("lB", [P, B, QT * H])
        lR = sb("lR", [P, B, QT * H])
        dm = sb("dm", [P, B, QT * H])
        al = sb("al", [P, B, QT * H])
        segI = sb("segI", [P, 4], I32)
        segF = sb("segF", [P, 4])
        segL = sb("segL", [P, 4])
        rowI = sb("rowI", [1, 4 * P], I32)
        rowF = sb("rowF", [1, 4 * P])
        few = sb("few", [1, 8])
        cnt = sb("cnt", [1, NBLK - 1])
        NX = sb("NX", [1, 1], I32)
        step = sb("step", [P, 4])
        look = sb("look", [P, 4])
        mA = sb("mA", [P, 4, P])
        mB = sb("mB", [P, 4, P])
        maskB = sb("maskB", [P, 4, P], BF16)
        maskG = sb("maskG", [P, QT, P], BF16)
        bst = sb("bst", [P, 8, QT, 6])
        mv = sb("mv", [P, 8, QT, 2])
        lve = sb("lve", [P, 8, QT])
        lrs = sb("lrs", [P, 8, QT])
        ones = sb("ones", [P, P])
        asum = sb("asum", [P, 3])
        WF = sb("WF", [P, 3, 2048])
        mw = sb("mw", [P, 3])
        rw = sb("rw", [P, 3])
        WQ = WAB[:, 0:3 * 1024].bitcast(BF16).rearrange("p (w n) -> p w n", w=3)
        xq = mA[:, :, :].rearrange("p t n -> p (t n)").bitcast(BF16).rearrange("p (t n) -> p t n", t=4)
        xqT = [mB[:, 2 * b:2 * b + 2, :].rearrange("p t n -> p (t n)").bitcast(BF16)
               .rearrange("p (k n) -> p k n", k=KT) for b in range(B)]
        am = sb("am", [P, 4, 4])
        am2 = sb("am2", [P, 4, 4])
        sgu = sb("sgu", [P, 4, 3])

        psS = [ps(f"psS{i}") for i in range(SBANKS)]
        psP = [ps(f"psP{i}") for i in range(PBANKS)]
        psO = ps("psO")
        psD = [ps(f"psD{i}") for i in range(DBANKS)]

        c_ld, x_ld, seg_ld, vec_ld = sem("c_ld"), sem("x_ld"), sem("seg_ld"), sem("vec_ld")
        wa_ld, wb_ld, wc_ld, nrm_ld, bias_ld = sem("wa_ld"), sem("wb_ld"), sem("wc_ld"), sem("nrm_ld"), sem("bias_ld")
        wt_ld, wf_ld, ct_ld, g_ct_ld = sem("wt_ld"), sem("wf_ld"), sem("ct_ld"), sem("g_ct_ld")
        d_full = [sem(f"d_full{i}") for i in range(DBANKS)]
        d_free = [sem(f"d_free{i}") for i in range(DBANKS)]
        consts_set = sem("consts_set")
        nb_set = sem("nb_set")
        few_done = sem("few_done")
        x_first = sem("x_first")
        ss_set, ms_set, rstd_set, h_set = (sem(n) for n in ("ss_set", "ms_set", "rstd_set", "h_set"))
        cos_set, sin_set, qr_set = (sem(n) for n in ("cos_set", "sin_set", "qr_set"))
        xbo_set = sem("xbo_set")
        s_full, s_max, s_exp, t_full, t_copied, pv_done = (
            sem(n) for n in ("s_full", "s_max", "s_exp", "t_full", "t_copied", "pv_done"))
        rl_set, on_set = sem("rl_set"), sem("on_set")
        mask_cmp, mask_set = sem("mask_cmp"), sem("mask_set")
        or_copied, crl_set, con_set = sem("or_copied"), sem("crl_set"), sem("con_set")
        gu_full, hid_set, y_full, y_free = sem("gu_full"), sem("hid_set"), sem("y_full"), sem("y_free")
        g_rel, g_cmp, g_mask, g_kv_full, g_kv_set = (
            sem(n) for n in ("g_rel", "g_cmp", "g_mask", "g_kv_full", "g_kv_set"))
        g_s_full, g_bmax, g_max, g_exp, g_t_full, g_t_copied, g_pv_done = (
            sem(n) for n in ("g_s_full", "g_bmax", "g_max", "g_exp", "g_t_full", "g_t_copied", "g_pv_done"))
        g_dm, g_nmr, g_al, g_lr, g_scaled, g_added = (
            sem(n) for n in ("g_dm", "g_nmr", "g_al", "g_lr", "g_scaled", "g_added"))
        sg_set = sem("sg_set")
        ln_var, ln_rstd = sem("ln_var"), sem("ln_rstd")
        v_step = sem("v_step")
        an_set = sem("an_set")
        ws_full, sig_set, tau_set, wpv_done = sem("ws_full"), sem("sig_set"), sem("tau_set"), sem("wpv_done")
        mo_set = sem("mo_set")
        asum_set, mw_set, tern_set, sgu_set = sem("asum_set"), sem("mw_set"), sem("tern_set"), sem("sgu_set")
        pool_set, tern_step = sem("pool_set"), sem("tern_step")
        xq_set, gq_set = sem("xq_set"), sem("gq_set")
        stored = sem("stored")

        ident = const[:, C_ID:C_ID + P]
        headmask = const[:, C_HEAD:C_HEAD + HT]
        cos = const[:, C_COS:C_COS + QT * HD].rearrange("p (t d) -> p t d", t=QT)
        sin = const[:, C_SIN:C_SIN + QT * HD].rearrange("p (t d) -> p t d", t=QT)
        iota = const[:, C_IOTA:C_IOTA + P]
        band = const[:, C_BAND:C_BAND + P]
        corner = const[:, C_CORNER:C_CORNER + HD]
        Wqkv = WA[:, WA_QKV:WA_O].rearrange("p (k n) -> p k n", k=KT)
        Wo = WA[:, WA_O:WA_N].rearrange("p (k n) -> p k n", k=KT)
        Wqc = WB[:, WB_Q:WB_KV].rearrange("p (k n) -> p k n", k=KT)
        Wkv = WB[:, WB_KV:WB_O].rearrange("p (k n) -> p k n", k=KT)
        Woc = WB[:, WB_O:WB_N].rearrange("p (k n) -> p k n", k=KT)
        Wg = WC[:, WC_G:WC_U].rearrange("p (k n) -> p k n", k=KT)
        Wu = WC[:, WC_U:WC_D].rearrange("p (k n) -> p k n", k=KT)
        Wd = WC[:, WC_D:WC_N].rearrange("p (k n) -> p k n", k=FT)
        Wt = WT[:, :].rearrange("p (w k n) -> p w k n", w=4, k=KT)

        def filled(l, use):
            k, n = (LAYER_AT if use in LAYER_AT else TAIL_AT)[use]
            return d_full[k], l * LAYER_TOTAL[k] + n + 1

        def free_for(l, use):
            k, n = (LAYER_AT if use in LAYER_AT else TAIL_AT)[use]
            return d_free[k], l * LAYER_TOTAL[k] + n + 1

        def emptied(l, use):
            k, n = (LAYER_AT if use in LAYER_AT else TAIL_AT)[use]
            return d_free[k], l * LAYER_TOTAL[k] + n + 2

        def bank(use):
            return psD[(LAYER_AT if use in LAYER_AT else TAIL_AT)[use][0]]

        def full(use):
            return d_full[(LAYER_AT if use in LAYER_AT else TAIL_AT)[use][0]]

        def free(use):
            return d_free[(LAYER_AT if use in LAYER_AT else TAIL_AT)[use][0]]

        def heads(ap):
            return ap.rearrange("p t (h d) -> p (t h) d", d=HD)

        def tiles(ap):
            return ap.rearrange("p (a n) -> p a n", a=2)

        def GU(t):
            return QM[t // 2][:, :, :, :].rearrange("p k h n -> p (k h n)")[:, (t % 2) * 2048:(t % 2) * 2048 + F]

        def GR(t):
            return QM[t // 2][:, :, :, :].rearrange("p k h n -> p (k h n)")[:, (t % 2) * 2048 + F:(t % 2) * 2048 + 2 * F]

        def GQ(t):
            return AT[t // 2][:, :, :].rearrange("p f n -> p (f n)").bitcast(BF16)[:, (t % 2) * 2048:(t % 2) * 2048 + F]

        def GQT(t):
            return AT[t // 2][:, :, :].rearrange("p f n -> p (f n)").bitcast(BF16)[:, (t % 2) * 2048 + F:(t % 2) * 2048 + 2 * F]

        block = stack.enter_context(nc.Block())

        @block.sync
        def _(sp):
            sp.dma_start(X0[:, :, :], x_in).then_inc(x_ld, 16)
            sp.dma_start(const[:, :], const_in).then_inc(c_ld, 16)
            sp.dma_start(nrm[:, :], nrm_in[0]).then_inc(nrm_ld, 16)
            sp.dma_start(WA, wa_in[0]).then_inc(wa_ld, 16)
            sp.dma_start(bias[:, :], bias_in[0:1, :].broadcast_to([P, 4 * D])).then_inc(bias_ld, 16)
            sp.dma_start(rowI[:, :], seg_in[4 * P:8 * P].rearrange("(a n) -> a n", a=1)).then_inc(seg_ld, 16)
            sp.dma_start(segI[:, :], seg_in[0:4 * P].rearrange("(p t) -> p t", t=4)).then_inc(seg_ld, 16)
            sp.dma_start(CT[:, :, :, :], ctx_in[0]).then_inc(ct_ld, 16)
            sp.dma_start(WB, wb_in[0]).then_inc(wb_ld, 16)
            sp.dma_start(WC[:, :], wc_in[0]).then_inc(wc_ld, 16)
            sp.dma_start(vec[:, :], vec_in[0:1, :].broadcast_to([P, 3 * D])).then_inc(vec_ld, 16)
            sp.dma_start(WT[:, :], wt_in).then_inc(wt_ld, 16)
            sp.dma_start(WF[:, :, :], wf_in).then_inc(wf_ld, 16)
            sp.wait_ge(nb_set, 1)
            nx = sp.value_load(NX[0:1, 0:1], min_val=0, max_val=NBLK - 1)

            def further_blocks(l, b):
                with sp.If(nx > 0):
                    with sp.Fori(0, nx) as j:
                        sp.wait_ge(g_kv_full, (l * B + b) * nx + j + 1)
                        sp.dma_start(CTg[:, :, :], ctx_in[j + 1][:, :, b, :]).then_inc(g_ct_ld, 16)

            with sp.Fori(0, NL - 1) as l:
                sp.wait_ge(*emptied(l, "v1"))
                sp.wait_ge(xbo_set, (l + 1) * B)
                sp.dma_start(bias[:, :], bias_in[l + 1].rearrange("(a n) -> a n", a=1).broadcast_to([P, 4 * D])).then_inc(bias_ld, 16)
                sp.wait_ge(*filled(l, "wo1"))
                sp.dma_start(WA, wa_in[l + 1]).then_inc(wa_ld, 16)
                for b in range(B):
                    further_blocks(l, b)
                sp.wait_ge(*filled(l, "cwo1"))
                sp.dma_start(WB, wb_in[l + 1]).then_inc(wb_ld, 16)
                sp.wait_ge(*emptied(l, "n21"))
                sp.dma_start(nrm[:, :], nrm_in[l + 1]).then_inc(nrm_ld, 16)
                sp.wait_ge(y_full, l * B + 2)
                sp.dma_start(WC[:, :], wc_in[l + 1]).then_inc(wc_ld, 16)
            for b in range(B):
                further_blocks(NL - 1, b)
            for t in range(4):
                sp.wait_ge(*emptied(NL, f"d{t}"))
                sp.dma_start(out[t], X[:, t, :]).then_inc(stored, 16)
            sp.wait_ge(stored, 4 * 16)

        @block.tensor
        def _(pe):
            def transposes(l, use, src, b):
                pe.wait_ge(*free_for(l, use))
                for k in range(KT):
                    for t in range(QT):
                        mm = pe.transpose(bank(use)[:, k * L + t * P:k * L + (t + 1) * P],
                                          src[:, t, k * P:(k + 1) * P], ident)
                mm.then_inc(full(use), 1)

            def project(l, use, col, lhs, rhs, n=D):
                for k in range(KT):
                    mm = pe.matmul(bank(use)[:, col:col + n], lhs(k), rhs(k), start=(k == 0), stop=(k == KT - 1))
                return mm

            def norm_T(l, i, b):
                pe.wait_ge(h_set, l * NORMS + i * B + b + 1)
                transposes(l, f"n{i}{b}", hs[:, 2 * b:2 * b + 2, :], b)

            def qkv(l, b, part):
                if part == 0:
                    pe.wait_ge(*emptied(l, f"n0{b}"))
                    pe.wait_ge(wa_ld, l * 16 + 16)
                if part < QT:
                    use = f"qk{b}{part}"
                    pe.wait_ge(*free_for(l, use))
                    mm = project(l, use, 0, lambda k: hT[b][:, k, part * P:(part + 1) * P],
                                 lambda k: Wqkv[:, k, 0:2 * D], 2 * D)
                else:
                    use = f"v{b}"
                    pe.wait_ge(*free_for(l, use))
                    for t in range(QT):
                        mm = project(l, use, t * D, lambda k: hT[b][:, k, t * P:(t + 1) * P],
                                     lambda k: Wqkv[:, k, 2 * D:3 * D])
                mm.then_inc(full(use), 1)

            def rotated_T(l, b, k):
                pe.wait_ge(qr_set, l * B + b + 1)
                use = f"tq{b}{k}"
                pe.wait_ge(*free_for(l, use))
                for w in range(2):
                    for t in range(QT):
                        mm = pe.transpose(bank(use)[:, w * L + t * P:w * L + (t + 1) * P],
                                          QR[b][:, t, w * D + k * P:w * D + (k + 1) * P], ident)
                mm.then_inc(full(use), 1)

            def masked_scores(S, b, q, h0, nh, keys, mask, keysT):
                pe.matmul(S[:, :].rearrange("p (h k) -> p h k", h=nh), identB[:, :],
                          mask.unsqueeze(1).broadcast_to([P, nh, keys]), start=True, stop=False, skip_group_check=True)
                for j in range(nh):
                    h = h0 + j
                    mm = pe.matmul(S[:, j * keys:(j + 1) * keys], QM[b][:, h // HT, h % HT, q * P:(q + 1) * P],
                                   keysT[:, h // HT, 0:keys], start=False, stop=True, skip_group_check=True)
                return mm

            def scores(l, i):
                cross, b, q, h0, nh, keys = GROUPS[i]
                if i in (S0, S1):
                    pe.wait_ge(*emptied(l, f"tq{b}0"))
                    pe.wait_ge(*emptied(l, f"tq{b}1"))
                if i in (C0, C1):
                    pe.wait_ge(mask_set, 1)
                    pe.wait_ge(*emptied(l, f"kv{b}"))
                    pe.wait_ge(*emptied(l, f"qc{b}0"))
                    pe.wait_ge(*emptied(l, f"qc{b}1"))
                if i >= SBANKS:
                    pe.wait_ge(s_exp, l * NG + i - SBANKS + 1)
                mask = maskB[:, 2 * b + q, :] if cross else causB[:, 2 * P - keys:2 * P]
                masked_scores(psS[i % SBANKS], b, q, h0, nh, keys, mask, KC[b] if cross else kTs[b])\
                    .then_inc(s_full, 1)

            def probs_T(l, i):
                pe.wait_ge(s_exp, l * NG + i + 1)
                if i >= PBANKS:
                    pe.wait_ge(t_copied, l * NG + i - PBANKS + 1)
                for j in range(4):
                    mm = pe.transpose(psP[i % PBANKS][:, j * P:(j + 1) * P], Pr[:, i % 3, j * P:(j + 1) * P], ident)
                mm.then_inc(t_full, 1)

            def pv(l, i):
                cross, b, q, h0, nh, keys = GROUPS[i]
                first = i in (S0, S1, C0, C1)
                if i == S0:
                    pe.wait_ge(*emptied(l, "v0"))
                    pe.wait_ge(y_free, l * B + 1)
                if i == S1:
                    pe.wait_ge(*emptied(l, "v1"))
                    pe.wait_ge(on_set, l * B + 1)
                if i == C0:
                    pe.wait_ge(on_set, l * B + 2)
                if i == C1:
                    pe.wait_ge(or_copied, l * B + 1)
                pe.wait_ge(t_copied, l * NG + i + 1)
                nk = keys // P
                for j in range(nh):
                    h = h0 + j
                    for k in range(nk):
                        values = VC[b] if cross else V[b][:, k, :]
                        mm = pe.matmul(psO[:, q * D + h * HD:q * D + (h + 1) * HD],
                                       PT[:, i % 3, (j * nk + k) * P:(j * nk + k + 1) * P],
                                       values[:, h * HD:(h + 1) * HD],
                                       start=(first and j == 0 and k == 0), stop=True, skip_group_check=True)
                mm.then_inc(pv_done, 1)

            def out_T(l, b, use, src, ready, value):
                pe.wait_ge(ready, value)
                transposes(l, use, src, b)

            def out_proj(l, b, use, W, source):
                pe.wait_ge(*emptied(l, source))
                pe.wait_ge(*free_for(l, use))
                for t in range(QT):
                    mm = project(l, use, t * D, lambda k: oT[b][:, k, t * P:(t + 1) * P], lambda k: W[:, k, :])
                mm.then_inc(full(use), 1)

            def cross_q(l, b):
                pe.wait_ge(*emptied(l, f"n1{b}"))
                pe.wait_ge(wb_ld, l * 16 + 16)
                for m in range(KT):
                    use = f"qc{b}{m}"
                    pe.wait_ge(*free_for(l, use))
                    project(l, use, 0, lambda k: Wqc[:, k, m * P:(m + 1) * P],
                            lambda k: hT[b][:, k, :]).then_inc(full(use), 1)

            def keys_values(P_bank, b, CTb):
                for m in range(KT):
                    for k in range(KT):
                        pe.matmul(P_bank[:, m * P:(m + 1) * P], Wkv[:, k, m * P:(m + 1) * P], CTb[:, k, :],
                                  start=(k == 0), stop=(k == KT - 1))
                for k in range(KT):
                    mm = pe.matmul(P_bank[:, D:2 * D], CTb[:, k, :], Wkv[:, k, D:2 * D],
                                   start=(k == 0), stop=(k == KT - 1))
                return mm

            def cross_kv(l, b):
                pe.wait_ge(ct_ld, 16)
                pe.wait_ge(wb_ld, l * 16 + 16)
                pe.wait_ge(*free_for(l, f"kv{b}"))
                keys_values(bank(f"kv{b}"), b, CT[:, :, b, :]).then_inc(full(f"kv{b}"), 1)

            def further_blocks(l, b, nx):
                with pe.If(nx > 0):
                    with pe.Fori(0, nx) as j:
                        c = pe.snap((l * B + b) * nx + j)
                        pe.wait_ge(g_ct_ld, c * 16 + 16)
                        keys_values(psS[2], b, CTg).then_inc(g_kv_full, 1)
                        pe.wait_ge(g_mask, c + 1)
                        pe.wait_ge(g_kv_set, c + 1)
                        pe.wait_ge(or_copied, l * B + b + 1)
                        for i in range(NCROSS + 2):
                            if i < NCROSS:
                                q, h0, nh, keys = CROSS[i]
                                if i >= 2:
                                    pe.wait_ge(g_exp, c * NCROSS + i - 1)
                                masked_scores(psS[i % 2], b, q, h0, nh, keys, maskG[:, q, :], KC[b])\
                                    .then_inc(g_s_full, 1)
                            if 1 <= i <= NCROSS:
                                n = i - 1
                                pe.wait_ge(g_exp, c * NCROSS + n + 1)
                                if n >= 2:
                                    pe.wait_ge(g_t_copied, c * NCROSS + n - 1)
                                for m in range(4):
                                    mm = pe.transpose(psP[n % 2][:, m * P:(m + 1) * P],
                                                      Pr[:, n % 3, m * P:(m + 1) * P], ident)
                                mm.then_inc(g_t_full, 1)
                            if i >= 2:
                                n = i - 2
                                q, h0, nh, keys = CROSS[n]
                                pe.wait_ge(g_t_copied, c * NCROSS + n + 1)
                                for m in range(4):
                                    h = h0 + m
                                    mm = pe.matmul(psO[:, q * D + h * HD:q * D + (h + 1) * HD],
                                                   PT[:, n % 3, m * P:(m + 1) * P], VC[b][:, h * HD:(h + 1) * HD],
                                                   start=(n == 0 and m == 0), stop=True, skip_group_check=True)
                                mm.then_inc(g_pv_done, 1)
                        pe.wait_ge(g_added, c + 1)

            def gate_up(l, b, f):
                n = b * FT + f
                if f == 0:
                    pe.wait_ge(*emptied(l, f"n2{b}"))
                    pe.wait_ge(wc_ld, l * 16 + 16)
                if n >= SBANKS:
                    pe.wait_ge(hid_set, l * B * FT + n - SBANKS + 1)
                for w, W in enumerate((Wg, Wu)):
                    for k in range(KT):
                        mm = pe.matmul(psS[n % SBANKS][:, w * L:(w + 1) * L], W[:, k, f * P:(f + 1) * P],
                                       hT[b][:, k, :], start=(k == 0), stop=(k == KT - 1))
                mm.then_inc(gu_full, 1)

            def down(l, b):
                pe.wait_ge(hid_set, l * B * FT + (b + 1) * FT)
                if b == 0:
                    pe.wait_ge(or_copied, l * B + B)
                else:
                    pe.wait_ge(y_free, l * B + 2)
                for t in range(QT):
                    for f in range(FT):
                        mm = pe.matmul(psO[:, t * D:(t + 1) * D], AT[b][:, f, t * P:(t + 1) * P], Wd[:, f, :],
                                       start=(f == 0), stop=(f == FT - 1))
                mm.then_inc(y_full, 1)

            def attention(l, nx):
                between = {
                    2: lambda: norm_T(l, 0, 1), 3: lambda: qkv(l, 1, 0), 4: lambda: qkv(l, 1, 1),
                    5: lambda: qkv(l, 1, 2), 7: lambda: rotated_T(l, 1, 0), 8: lambda: rotated_T(l, 1, 1),
                    S1 + 1: lambda: out_T(l, 0, "oT0", On[0], on_set, l * B + 1),
                    S1 + 2: lambda: out_proj(l, 0, "wo0", Wo, "oT0"),
                    S1 + 6: lambda: (norm_T(l, 1, 0), cross_kv(l, 0)), S1 + 7: lambda: cross_q(l, 0),
                    C0 + 1: lambda: out_T(l, 1, "oT1", On[1], on_set, l * B + 2),
                    C0 + 2: lambda: out_proj(l, 1, "wo1", Wo, "oT1"),
                    C0 + 5: lambda: (norm_T(l, 1, 1), cross_kv(l, 1)), C0 + 6: lambda: cross_q(l, 1),
                    C1 + 1: lambda: out_T(l, 0, "coT0", On[0], con_set, l * B + 1),
                    C1 + 2: lambda: out_proj(l, 0, "cwo0", Woc, "coT0"), C1 + 5: lambda: norm_T(l, 2, 0),
                }
                for first, end in ((S0, C1), (C1, NG)):
                    scores(l, first)
                    scores(l, first + 1)
                    for i in range(first, end):
                        if i + 2 < end:
                            scores(l, i + 2)
                        between.get(i, lambda: None)()
                        probs_T(l, i)
                        if i > first:
                            pv(l, i - 1)
                    pv(l, end - 1)
                    further_blocks(l, int(first == C1), nx)

            def hidden_0(l):
                for f in range(FT):
                    gate_up(l, 0, f)
                    if f == 1:
                        out_T(l, 1, "coT1", On[1], con_set, l * B + 2)
                    if f == 2:
                        out_proj(l, 1, "cwo1", Woc, "coT1")
                    if f == 6:
                        norm_T(l, 2, 1)

            pe.wait_ge(c_ld, 16)
            norm_T(0, 0, 0)
            for part in range(3):
                qkv(0, 0, part)
            pe.wait_ge(consts_set, 2)
            for k in range(KT):
                rotated_T(0, 0, k)
            pe.wait_ge(nb_set, 1)
            nx = pe.value_load(NX[0:1, 0:1], min_val=0, max_val=NBLK - 1)
            with pe.Fori(0, NL - 1) as l:
                attention(l, nx)
                hidden_0(l)
                for f in range(FT):
                    gate_up(l, 1, f)
                    if f == 0:
                        down(l, 0)
                    if f == 3:
                        norm_T(l + 1, 0, 0)
                    if f == 4:
                        qkv(l + 1, 0, 0)
                        qkv(l + 1, 0, 1)
                    if f == 5:
                        qkv(l + 1, 0, 2)
                for k in range(KT):
                    rotated_T(l + 1, 0, k)
                down(l, 1)
            attention(NL - 1, nx)
            hidden_0(NL - 1)
            for f in range(FT):
                gate_up(NL - 1, 1, f)
                if f == 0:
                    down(NL - 1, 0)
            down(NL - 1, 1)

            pe.wait_ge(wt_ld, 16)
            for b in range(B):
                pe.wait_ge(an_set, b + 1)
                transposes(NL, f"an{b}", hs[:, 2 * b:2 * b + 2, :], b)
                pe.wait_ge(*emptied(NL, f"an{b}"))
                for m in range(KT):
                    pe.wait_ge(*free_for(NL, f"wq{m}{b}"))
                    project(NL, f"wq{m}{b}", 0, lambda k: Wt[:, 0, k, m * P:(m + 1) * P],
                            lambda k: hT[b][:, k, :]).then_inc(full(f"wq{m}{b}"), 1)
                pe.wait_ge(*free_for(NL, f"wk{b}"))
                for m in range(KT):
                    mm = project(NL, f"wk{b}", m * L, lambda k: Wt[:, 1, k, m * P:(m + 1) * P], lambda k: hT[b][:, k, :])
                mm.then_inc(full(f"wk{b}"), 1)
                pe.wait_ge(*free_for(NL, f"wv{b}"))
                for t in range(QT):
                    mm = project(NL, f"wv{b}", t * D, lambda k: hT[b][:, k, t * P:(t + 1) * P], lambda k: Wt[:, 2, k, :])
                mm.then_inc(full(f"wv{b}"), 1)

            pe.wait_ge(asum_set, 3)
            pe.wait_ge(pool_set, 1)
            pe.wait_ge(*free_for(NL, "sum"))
            pe.matmul(bank("sum")[:, 0:3], ones[:, :], asum[:, :], start=True, stop=True).then_inc(full("sum"), 1)

            def window_scores(i):
                b, (blk, k, half) = i // 9, WINDOW[i % 9]
                if i % 9 == 0:
                    for use in (f"wq0{b}", f"wq1{b}", f"wk{b}"):
                        pe.wait_ge(*emptied(NL, use))
                if i >= SBANKS:
                    pe.wait_ge(sig_set, i - SBANKS + 1)
                S = psS[i % SBANKS]
                if blk == "corner":
                    for k in range(KT):
                        mm = pe.matmul(S[:, k * P:(k + 1) * P].rearrange("p (h q) -> p h q", h=HT), kTs[b][:, k, 0:P],
                                       QM[b][:, k, :, P:P + HD], start=(k == 0), stop=True, skip_group_check=True)
                else:
                    mm = pe.matmul(S[:, :].rearrange("p (h q) -> p h q", h=4), kTs[b][:, k, blk * P:(blk + 1) * P],
                                   QM[b][:, k, 4 * half:4 * half + 4, blk * P:(blk + 1) * P], start=True, stop=True)
                mm.then_inc(ws_full, 1)

            def window_pv(i):
                b, (blk, k, half) = i // 9, WINDOW[i % 9]
                if i % 9 == 0:
                    pe.wait_ge(*emptied(NL, f"wv{b}"))
                    if b:
                        pe.wait_ge(mo_set, b)
                pe.wait_ge(tau_set, i + 1)
                T = PT[:, i % 3, :]
                if blk == "corner":
                    for h in range(H):
                        mm = pe.matmul(psO[0:HD, D + h * HD:D + (h + 1) * HD], T[:, h * HD:(h + 1) * HD],
                                       V[b][:, 0, h * HD:(h + 1) * HD], start=False, stop=True, skip_group_check=True)
                else:
                    for j in range(4):
                        h = k * HT + 4 * half + j
                        mm = pe.matmul(psO[:, blk * D + h * HD:blk * D + (h + 1) * HD], T[:, j * P:(j + 1) * P],
                                       V[b][:, blk, h * HD:(h + 1) * HD], start=(i % 9 == 0 and j == 0), stop=True,
                                       skip_group_check=True)
                mm.then_inc(wpv_done, 1)

            window_scores(0)
            window_scores(1)
            for i in range(18):
                if i + 2 < 18:
                    window_scores(i + 2)
                window_pv(i)
            for b in range(B):
                out_T(NL, b, f"moT{b}", On[b], mo_set, b + 1)
                out_proj(NL, b, f"mwo{b}", Wt[:, 3, :, :], f"moT{b}")

            for b in range(B):
                pe.wait_ge(xq_set, 2 * b + 2)
                pe.wait_ge(*free_for(NL, f"fn{b}"))
                for k in range(KT):
                    for t in range(QT):
                        mm = pe.transpose(bank(f"fn{b}")[:, :].bitcast(BF16)[:, k * L + t * P:k * L + (t + 1) * P],
                                          xq[:, 2 * b + t, k * P:(k + 1) * P], identB[:, :])
                mm.then_inc(full(f"fn{b}"), 1)
            pe.wait_ge(tern_set, 3)
            for t in range(4):
                pe.wait_ge(*emptied(NL, f"fn{t // 2}"))
                for j in range(2):
                    for w in range(2):
                        use = f"{'gu'[w]}{t}{j}"
                        pe.wait_ge(*free_for(NL, use))
                        Wx = WQ[:, w, :].rearrange("p (k n) -> p k n", k=KT)
                        for k in range(KT):
                            mm = pe.matmul(bank(use)[:, :], xqT[t // 2][:, k, (t % 2) * P:(t % 2 + 1) * P],
                                           Wx[:, k, j * 512:(j + 1) * 512], start=(k == 0), stop=(k == KT - 1))
                        mm.then_inc(full(use), 1)
            WDq = WQ[:, 2, :].rearrange("p (f n) -> p f n", f=FT)
            for t in range(4):
                pe.wait_ge(gq_set, t + 1)
                pe.wait_ge(*free_for(NL, f"gT{t}"))
                for f in range(FT):
                    mm = pe.transpose(bank(f"gT{t}")[:, :].bitcast(BF16)[:, f * P:(f + 1) * P],
                                      GQ(t)[:, f * P:(f + 1) * P], identB[:, :])
                mm.then_inc(full(f"gT{t}"), 1)
                pe.wait_ge(*emptied(NL, f"gT{t}"))
                pe.wait_ge(*free_for(NL, f"d{t}"))
                for f in range(FT):
                    mm = pe.matmul(bank(f"d{t}")[:, 0:D], GQT(t)[:, f * P:(f + 1) * P], WDq[:, f, :],
                                   start=(f == 0), stop=(f == FT - 1))
                mm.then_inc(full(f"d{t}"), 1)

        @block.scalar
        def _(act):
            def squares(i, b, ready, value):
                act.wait_ge(ready, value)
                for t in range(QT):
                    a = nc.scalar.activation(hs[:, 2 * b + t, :], X[:, 2 * b + t, :], ACT.Square,
                                             accum_out=ss[:, i * B + b, t:t + 1])
                a.then_inc(ss_set, 1)

            def masked_q(src, b, k, heads_of=range(HT)):
                for h in heads_of:
                    a = nc.scalar.activation(QM[b][:, k, h, :], src, ACT.Copy, scale=headmask[:, h:h + 1])
                return a

            def self_qk(l, b, half):
                use = f"tq{b}1"
                if half == 0:
                    act.wait_ge(*filled(l, use))
                    nc.scalar.activation(kTs[b][:, 1, :], bank(use)[:, L:2 * L], ACT.Copy)
                    masked_q(bank(use)[:, 0:L], b, 1, range(HT // 2))
                else:
                    masked_q(bank(use)[:, 0:L], b, 1, range(HT // 2, HT)).then_inc(free(use), 1)

            def exp(l, i):
                cross, b, q, h0, nh, keys = GROUPS[i]
                nm, total = (nmR, lR) if cross else (nms, lS)
                act.wait_ge(s_max, l * NG + i + 1)
                if i >= 3:
                    act.wait_ge(t_full, l * NG + i - 2)
                for j in range(nh):
                    s = q * H + h0 + j
                    a = nc.scalar.activation(Pr[:, i % 3, j * keys:(j + 1) * keys],
                                             psS[i % SBANKS][:, j * keys:(j + 1) * keys], ACT.Exp,
                                             bias=nm[:, b, s:s + 1], accum_out=total[:, b, s:s + 1])
                a.then_inc(s_exp, 1)

            def copy_oT(l, b, use):
                act.wait_ge(*filled(l, use))
                a = nc.scalar.activation(oT[b][:, :, :].rearrange("p k n -> p (k n)"), bank(use)[:, :], ACT.Copy)
                a.then_inc(free(use), 1)

            def cross_qm(l, b, half):
                use = f"qc{b}1"
                if half == 0:
                    act.wait_ge(*filled(l, use))
                    masked_q(bank(use)[:, 0:L], b, 1, range(HT // 2))
                else:
                    masked_q(bank(use)[:, 0:L], b, 1, range(HT // 2, HT)).then_inc(free(use), 1)

            def cross_outputs(l, b):
                act.wait_ge(pv_done, l * NG + (C1 if b == 0 else NG))
                nc.scalar.activation(OR[b][:, :, :].rearrange("p t n -> p (t n)"), psO[:, :], ACT.Copy)\
                    .then_inc(or_copied, 1)

            def further_blocks(l, b, nx):
                with act.If(nx > 0):
                    with act.Fori(0, nx) as j:
                        c = act.snap((l * B + b) * nx + j)
                        for i, (q, h0, nh, keys) in enumerate(CROSS):
                            act.wait_ge(g_max, c * NCROSS + i + 1)
                            if i >= 3:
                                act.wait_ge(g_t_full, c * NCROSS + i - 2)
                            for m in range(nh):
                                s = q * H + h0 + m
                                a = nc.scalar.activation(Pr[:, i % 3, m * P:(m + 1) * P],
                                                         psS[i % 2][:, m * P:(m + 1) * P], ACT.Exp,
                                                         bias=nmN[:, b, s:s + 1], accum_out=lB[:, b, s:s + 1])
                            a.then_inc(g_exp, 1)
                        act.wait_ge(g_dm, c + 1)
                        nc.scalar.activation(al[:, b, :], dm[:, b, :], ACT.Exp).then_inc(g_al, 1)
                        act.wait_ge(g_added, c + 1)

            def gate(l, b, f):
                n = b * FT + f
                act.wait_ge(gu_full, l * B * FT + n + 1)
                if n >= 2:
                    act.wait_ge(hid_set, l * B * FT + n - 1)
                nc.scalar.activation(SG[:, n % 2, :], psS[n % SBANKS][:, 0:L], ACT.Silu).then_inc(sg_set, 1)

            def attention(l, nx):
                between = {
                    8: lambda: self_qk(l, 1, 0), 9: lambda: self_qk(l, 1, 1),
                    S1 + 1: lambda: copy_oT(l, 0, "oT0"), S1 + 3: lambda: squares(1, 0, *emptied(l, "wo0")),
                    S1 + 7: lambda: cross_qm(l, 0, 0), S1 + 8: lambda: cross_qm(l, 0, 1),
                    C0 + 1: lambda: copy_oT(l, 1, "oT1"), C0 + 2: lambda: squares(1, 1, *emptied(l, "wo1")),
                    C0 + 6: lambda: cross_qm(l, 1, 0), C0 + 7: lambda: cross_qm(l, 1, 1),
                    C1 + 1: lambda: copy_oT(l, 0, "coT0"), C1 + 2: lambda: squares(2, 0, *emptied(l, "cwo0")),
                }
                for first, end in ((S0, C1), (C1, NG)):
                    for i in range(first, end):
                        exp(l, i)
                        between.get(i, lambda: None)()
                    b = int(first == C1)
                    cross_outputs(l, b)
                    further_blocks(l, b, nx)

            def hidden_0(l):
                for f in range(FT):
                    gate(l, 0, f)
                    if f == 1:
                        copy_oT(l, 1, "coT1")
                    if f == 3:
                        squares(2, 1, *emptied(l, "cwo1"))

            act.wait_ge(c_ld, 16)
            for b in range(B):
                squares(0, b, x_first, b + 1)
            for half in range(2):
                self_qk(0, 0, half)
            act.wait_ge(nb_set, 1)
            nx = act.value_load(NX[0:1, 0:1], min_val=0, max_val=NBLK - 1)
            with act.Fori(0, NL - 1) as l:
                attention(l, nx)
                hidden_0(l)
                for f in range(FT):
                    gate(l, 1, f)
                    if f == 0:
                        squares(0, 0, y_free, l * B + 2)
                for half in range(2):
                    self_qk(l + 1, 0, half)
                squares(0, 1, y_free, l * B + 3)
            attention(NL - 1, nx)
            hidden_0(NL - 1)
            for f in range(FT):
                gate(NL - 1, 1, f)
                if f == 0:
                    squares(0, 0, y_free, (NL - 1) * B + 2)
            squares(0, 1, y_free, (NL - 1) * B + 3)

            act.wait_ge(wf_ld, 16)
            for w in range(3):
                if w:
                    act.wait_ge(asum_set, w)
                nc.scalar.activation(AT[0][:, :, :].rearrange("p f n -> p (f n)"), WF[:, w, :],
                                     ACT.Abs, accum_out=asum[:, w:w + 1]).then_inc(asum_set, 1)

            for b in range(B):
                act.wait_ge(*filled(NL, f"wq1{b}"))
                a = masked_q(bank(f"wq1{b}")[:, 0:L], b, 1)
                a.then_inc(free(f"wq1{b}"), 1)
                act.wait_ge(*filled(NL, f"wv{b}"))
                a = nc.scalar.activation(V[b][:, :, :].rearrange("p t n -> p (t n)"), bank(f"wv{b}")[:, :], ACT.Copy)
                a.then_inc(free(f"wv{b}"), 1)
            for i in range(18):
                n = 2 * P if WINDOW[i % 9][0] == "corner" else 512
                act.wait_ge(ws_full, i + 1)
                if i >= 3:
                    act.wait_ge(tau_set, i - 2)
                nc.scalar.activation(Pr[:, i % 3, 0:n], psS[i % SBANKS][:, 0:n], ACT.Sigmoid).then_inc(sig_set, 1)
            for b in range(B):
                act.wait_ge(*filled(NL, f"moT{b}"))
                a = nc.scalar.activation(oT[b][:, :, :].rearrange("p k n -> p (k n)"), bank(f"moT{b}")[:, :], ACT.Copy)
                a.then_inc(free(f"moT{b}"), 1)
            for t in range(4):
                act.wait_ge(sgu_set, 2)
                for j in range(2):
                    use = f"g{t}{j}"
                    act.wait_ge(*filled(NL, use))
                    a = nc.scalar.activation(GR(t)[:, j * 512:(j + 1) * 512], bank(use)[:, :], ACT.Silu,
                                             scale=sgu[:, t, 0:1])
                    a.then_inc(free(use), 1)
            for t in range(4):
                act.wait_ge(*filled(NL, f"gT{t}"))
                a = nc.scalar.activation(GQT(t), bank(f"gT{t}")[:, :].bitcast(BF16), ACT.Copy)
                a.then_inc(free(f"gT{t}"), 1)

        @block.vector
        def _(dve):
            steps = [0]

            def done(ins):
                steps[0] += 1
                ins.then_inc(v_step, 1)
                dve.wait_ge(v_step, steps[0])

            def mean_square(l, i, b):
                dve.wait_ge(ss_set, l * NORMS + i * B + b + 1)
                dve.tensor_scalar(ms[:, i * B + b, :], ss[:, i * B + b, :], 1.0 / D, RMS_EPS, ALU.mult, ALU.add)\
                   .then_inc(ms_set, 1)

            def normalise(l, i, b):
                dve.wait_ge(rstd_set, l * NORMS + i * B + b + 1)
                for t in range(QT):
                    v = dve.tensor_scalar(hs[:, 2 * b + t, :], X[:, 2 * b + t, :], rstd[:, i * B + b, t:t + 1], None,
                                          ALU.mult)
                v.then_inc(h_set, 1)

            def weigh_T(l, i, b):
                use = f"n{i}{b}"
                dve.wait_ge(nrm_ld, l * 16 + 16)
                dve.wait_ge(*filled(l, use))
                for k in range(KT):
                    v = dve.tensor_scalar(hT[b][:, k, :], bank(use)[:, k * L:(k + 1) * L],
                                          nrm[:, i * KT + k:i * KT + k + 1], None, ALU.mult)
                v.then_inc(free(use), 1)

            def biased_qkv(l, b, part):
                if part == 0:
                    dve.wait_ge(bias_ld, l * 16 + 16)
                if part < QT:
                    use = f"qk{b}{part}"
                    dve.wait_ge(*filled(l, use))
                    v = dve.tensor_tensor(QK[b][:, part, :], bank(use)[:, :], bias[:, 0:2 * D], ALU.add)
                else:
                    use = f"v{b}"
                    dve.wait_ge(*filled(l, use))
                    v = dve.tensor_tensor(V[b][:, :, :], tiles(bank(use)[:, :]),
                                          bias[:, 2 * D:3 * D].unsqueeze(1).broadcast_to([P, QT, D]), ALU.add)
                v.then_inc(free(use), 1)

            def cosines(l, b):
                for t in range(QT):
                    dve.wait_ge(*emptied(l, f"qk{b}{t}"))
                dve.tensor_tensor(QR[b][:, :, :].rearrange("p t (h d) -> p t h d", d=HD),
                                  QK[b][:, :, :].rearrange("p t (h d) -> p t h d", d=HD),
                                  cos.unsqueeze(2).broadcast_to([P, QT, 2 * H, HD]), ALU.mult).then_inc(cos_set, 1)

            def add_sines(l, b):
                dve.wait_ge(cos_set, l * B + b + 1)
                dve.wait_ge(sin_set, l * B + b + 1)
                dve.tensor_tensor(QR[b][:, :, :], QR[b][:, :, :], RT[:, :, :], ALU.add).then_inc(qr_set, 1)

            def masked_q(src, b, n=HT, h0=0):
                return dve.tensor_tensor(QM[b][:, 0, h0:h0 + n, :], src.unsqueeze(1).broadcast_to([P, n, L]),
                                         headmask[:, h0:h0 + n].unsqueeze(2).broadcast_to([P, n, L]), ALU.mult)

            def self_qk(l, b, half):
                use = f"tq{b}0"
                if half == 0:
                    dve.wait_ge(*filled(l, use))
                    dve.tensor_copy(kTs[b][:, 0, :], bank(use)[:, L:2 * L])
                    masked_q(bank(use)[:, 0:L], b, HT // 2)
                else:
                    masked_q(bank(use)[:, 0:L], b, HT // 2, HT // 2).then_inc(free(use), 1)

            def max_(l, i):
                cross, b, q, h0, nh, keys = GROUPS[i]
                s = q * H + h0
                dve.wait_ge(s_full, l * NG + i + 1)
                dve.tensor_reduce((nmR if cross else nms)[:, b, s:s + nh],
                                  psS[i % SBANKS][:, :].rearrange("p (h k) -> p h k", h=nh),
                                  AX_X, ALU.max, negate=True).then_inc(s_max, 1)

            def copy_T(l, i):
                dve.wait_ge(t_full, l * NG + i + 1)
                if i >= 3:
                    dve.wait_ge(pv_done, l * NG + i - 2)
                dve.tensor_copy(PT[:, i % 3, :], psP[i % PBANKS][:, :]).then_inc(t_copied, 1)

            def divide(src, denominator, b, step_set, step_value, out_set):
                dve.reciprocal(rl[:, b, :], denominator).then_inc(step_set, 1)
                dve.wait_ge(step_set, step_value)
                dve.tensor_tensor(heads(On[b][:, :, :]), src,
                                  rl[:, b, :].unsqueeze(2).broadcast_to([P, QT * H, HD]), ALU.mult).then_inc(out_set, 1)

            def self_out(l, b):
                dve.wait_ge(pv_done, l * NG + (b + 1) * NSELF)
                divide(psO[:, :].rearrange("p (h d) -> p h d", d=HD), lS[:, b, :], b, rl_set, l * B + b + 1, on_set)

            def residual(l, b, use):
                dve.wait_ge(*filled(l, use))
                x = X[:, 2 * b:2 * b + 2, :]
                v = dve.tensor_tensor(x, x, tiles(bank(use)[:, :]), ALU.add)
                v.then_inc(free(use), 1)

            def down_residual(l, b):
                dve.wait_ge(y_full, l * B + b + 1)
                x = X[:, 2 * b:2 * b + 2, :]
                dve.tensor_tensor(x, x, tiles(psO[:, :]), ALU.add).then_inc(y_free, 1)

            def cross_qm(l, b, half):
                use = f"qc{b}0"
                if half == 0:
                    dve.wait_ge(*filled(l, use))
                    masked_q(bank(use)[:, 0:L], b, HT // 2)
                else:
                    masked_q(bank(use)[:, 0:L], b, HT // 2, HT // 2).then_inc(free(use), 1)

            def cross_kv(l, b):
                use = f"kv{b}"
                dve.wait_ge(*filled(l, use))
                dve.tensor_copy(KV[b][:, :], bank(use)[:, :]).then_inc(free(use), 1)

            def cross_out(l, b):
                dve.wait_ge(or_copied, l * B + b + 1)
                divide(heads(OR[b][:, :, :]), lR[:, b, :], b, crl_set, l * B + b + 1, con_set)

            def compare(t0, n, low, high):
                for t in range(t0, t0 + n):
                    dve.tensor_scalar(mA[:, t - t0, :], iota, high[:, t:t + 1], NEG, ALU.is_gt, ALU.mult)
                    v = dve.tensor_scalar(mB[:, t - t0, :], iota, low[:, t:t + 1], NEG, ALU.is_le, ALU.mult)
                return v

            def further_blocks(l, b, nx):
                with dve.If(nx > 0):
                    with dve.Fori(0, nx) as j:
                        c = dve.snap((l * B + b) * nx + j)
                        dve.wait_ge(g_rel, 2 * (c + l * B + b) + 2)
                        compare(2 * b, QT, segL, segR).then_inc(g_cmp, 1)
                        dve.wait_ge(g_cmp, c + 1)
                        dve.tensor_tensor(maskG[:, :, :], mA[:, 0:QT, :], mB[:, 0:QT, :], ALU.add).then_inc(g_mask, 1)
                        dve.wait_ge(g_kv_full, c + 2)
                        dve.tensor_copy(KV[b][:, :], psS[2][:, :]).then_inc(g_kv_set, 1)
                        for i in range(NCROSS + 1):
                            if i < NCROSS:
                                q, h0, nh, keys = CROSS[i]
                                s = q * H + h0
                                dve.wait_ge(g_s_full, c * NCROSS + i + 1)
                                dve.tensor_reduce(nmB[:, b, s:s + 4], psS[i % 2][:, :].rearrange("p (h k) -> p h k", h=4),
                                                  AX_X, ALU.max, negate=True).then_inc(g_bmax, 1)
                                dve.wait_ge(g_bmax, c * NCROSS + i + 1)
                                dve.tensor_tensor(nmN[:, b, s:s + 4], nmR[:, b, s:s + 4], nmB[:, b, s:s + 4], ALU.min)\
                                   .then_inc(g_max, 1)
                            if i >= 1:
                                n = i - 1
                                dve.wait_ge(g_t_full, c * NCROSS + n + 1)
                                if n >= 3:
                                    dve.wait_ge(g_pv_done, c * NCROSS + n - 2)
                                dve.tensor_copy(PT[:, n % 3, :], psP[n % 2][:, :]).then_inc(g_t_copied, 1)
                        dve.wait_ge(g_pv_done, (c + 1) * NCROSS)
                        dve.wait_ge(g_scaled, c + 1)
                        o = OR[b][:, :, :].rearrange("p t n -> p (t n)")
                        dve.tensor_tensor(o, o, psO[:, :], ALU.add).then_inc(g_added, 1)
                        dve.wait_ge(g_added, c + 1)

            def hidden(l, b, f):
                n = b * FT + f
                dve.wait_ge(sg_set, l * B * FT + n + 1)
                dve.tensor_tensor(AT[b][:, f, :], SG[:, n % 2, :], psS[n % SBANKS][:, L:2 * L], ALU.mult)\
                   .then_inc(hid_set, 1)

            def layernorm(n, b, src, dst, last):
                for t in range(QT):
                    v = dve.bn_stats(bst[:, n, t, :], src[:, 2 * b + t, :])
                done(v)
                for t in range(QT):
                    v = dve.bn_aggr(mv[:, n, t, :], bst[:, n, t, :])
                done(v)
                dve.tensor_scalar(lve[:, n, :], mv[:, n, :, 1], LN_EPS, None, ALU.add).then_inc(ln_var, 1)
                dve.wait_ge(ln_rstd, n + 1)
                for t in range(QT):
                    v = dve.tensor_scalar(dst[:, 2 * b + t, :], src[:, 2 * b + t, :], mv[:, n, t, 0:1],
                                          lrs[:, n, t:t + 1], ALU.subtract, ALU.mult)
                last(v)

            def quantise_scales(t, n, src, which):
                a = (am, am2)[which]
                done(dve.tensor_reduce(a[:, t:t + n, 0], src, AX_X, ALU.max, apply_absolute_value=True))
                done(dve.tensor_scalar(a[:, t:t + n, 1], a[:, t:t + n, 0], 1e-5, None, ALU.max))
                done(dve.reciprocal(a[:, t:t + n, 2], a[:, t:t + n, 1]))
                dve.tensor_scalar(a[:, t:t + n, 3], a[:, t:t + n, 1], 1.0 / 127.0, None, ALU.mult)
                done(dve.tensor_scalar(a[:, t:t + n, 2], a[:, t:t + n, 2], 127.0, None, ALU.mult))

            def round_tile(src, t, which, dst, done_set):
                a = (am, am2)[which]
                done(dve.tensor_scalar(src, src, a[:, t, 2:3], MAGIC, ALU.mult, ALU.add))
                done(dve.tensor_scalar(src, src, MAGIC, 127.0, ALU.subtract, ALU.min))
                dve.tensor_scalar(dst, src, -128.0, None, ALU.max).then_inc(done_set, 1)

            def attention(l, nx):
                between = {
                    0: lambda: mean_square(l, 0, 1), 1: lambda: normalise(l, 0, 1), 2: lambda: weigh_T(l, 0, 1),
                    3: lambda: biased_qkv(l, 1, 0), 4: lambda: biased_qkv(l, 1, 1),
                    5: lambda: (biased_qkv(l, 1, 2), cosines(l, 1)), 6: lambda: add_sines(l, 1),
                    7: lambda: self_qk(l, 1, 0), 8: lambda: self_qk(l, 1, 1),
                    S1: lambda: self_out(l, 0),
                    S1 + 2: lambda: (dve.wait_ge(xbo_set, l * B + 1), residual(l, 0, "wo0")),
                    S1 + 4: lambda: mean_square(l, 1, 0), S1 + 5: lambda: normalise(l, 1, 0),
                    S1 + 6: lambda: (weigh_T(l, 1, 0), cross_kv(l, 0)),
                    S1 + 7: lambda: cross_qm(l, 0, 0), S1 + 8: lambda: cross_qm(l, 0, 1),
                    C0: lambda: self_out(l, 1),
                    C0 + 2: lambda: (dve.wait_ge(xbo_set, l * B + 2), residual(l, 1, "wo1")),
                    C0 + 3: lambda: mean_square(l, 1, 1), C0 + 4: lambda: normalise(l, 1, 1),
                    C0 + 5: lambda: (weigh_T(l, 1, 1), cross_kv(l, 1)),
                    C0 + 6: lambda: cross_qm(l, 1, 0), C0 + 7: lambda: cross_qm(l, 1, 1),
                    C1: lambda: cross_out(l, 0), C1 + 2: lambda: residual(l, 0, "cwo0"),
                    C1 + 3: lambda: mean_square(l, 2, 0), C1 + 4: lambda: normalise(l, 2, 0),
                    C1 + 5: lambda: weigh_T(l, 2, 0),
                }
                for first, end in ((S0, C1), (C1, NG)):
                    max_(l, first)
                    max_(l, first + 1)
                    for i in range(first, end):
                        if i + 2 < end:
                            max_(l, i + 2)
                        copy_T(l, i)
                        between.get(i, lambda: None)()
                    further_blocks(l, int(first == C1), nx)

            def hidden_0(l):
                cross_out(l, 1)
                for f in range(FT):
                    hidden(l, 0, f)
                    if f == 2:
                        residual(l, 1, "cwo1")
                    if f == 4:
                        mean_square(l, 2, 1)
                    if f == 5:
                        normalise(l, 2, 1)
                    if f == 6:
                        weigh_T(l, 2, 1)

            dve.sem_inc(d_free[0], 1)
            dve.sem_inc(d_free[1], 1)
            dve.sem_inc(y_free, 1)
            dve.sem_inc(g_kv_full, 1)
            dve.wait_ge(x_ld, 16)
            layernorm(0, 0, X0, X, lambda v: v.then_inc(x_first, 1))
            mean_square(0, 0, 0)
            layernorm(1, 1, X0, X, lambda v: v.then_inc(x_first, 1))
            normalise(0, 0, 0)
            weigh_T(0, 0, 0)
            dve.wait_ge(seg_ld, 32)
            done(dve.tensor_copy(rowF[:, :], rowI[:, :]))
            dve.tensor_reduce(few[:, 1:2], rowF[:, :], AX_X, ALU.min)
            done(dve.tensor_reduce(few[:, 0:1], rowF[:, :], AX_X, ALU.max))
            dve.tensor_scalar(few[:, 3:4], few[:, 1:2], 0.0, float(NBLK - 1), ALU.is_lt, ALU.mult)
            done(dve.tensor_scalar(cnt[:, :], iota[0:1, 1:NBLK], float(P), None, ALU.mult))
            done(dve.tensor_scalar(cnt[:, :], cnt[:, :], few[:, 0:1], None, ALU.is_le))
            done(dve.tensor_reduce(few[:, 2:3], cnt[:, :], AX_X, ALU.add))
            dve.tensor_tensor(NX[:, :], few[:, 2:3], few[:, 3:4], ALU.max).then_inc(nb_set, 1)
            dve.tensor_copy(segF[:, :], segI[:, :]).then_inc(consts_set, 1)
            dve.tensor_copy(identB[:, :], ident)
            dve.tensor_copy(causB[:, :], const[:, C_CAUSAL:C_CAUSAL + 2 * P]).then_inc(consts_set, 1)
            dve.wait_ge(consts_set, 2)
            done(dve.tensor_scalar(segL[:, :], segF[:, :], float(LOOKBACK), None, ALU.subtract))
            for part in range(3):
                biased_qkv(0, 0, part)
            cosines(0, 0)
            compare(0, 4, segL, segF).then_inc(mask_cmp, 1)
            dve.wait_ge(mask_cmp, 1)
            dve.tensor_tensor(maskB[:, :, :], mA[:, :, :], mB[:, :, :], ALU.add).then_inc(mask_set, 1)
            add_sines(0, 0)
            for half in range(2):
                self_qk(0, 0, half)

            dve.wait_ge(nb_set, 1)
            nx = dve.value_load(NX[0:1, 0:1], min_val=0, max_val=NBLK - 1)
            with dve.Fori(0, NL - 1) as l:
                attention(l, nx)
                hidden_0(l)
                hidden(l, 1, 0)
                down_residual(l, 0)
                hidden(l, 1, 1)
                mean_square(l + 1, 0, 0)
                hidden(l, 1, 2)
                normalise(l + 1, 0, 0)
                hidden(l, 1, 3)
                weigh_T(l + 1, 0, 0)
                hidden(l, 1, 4)
                biased_qkv(l + 1, 0, 0)
                biased_qkv(l + 1, 0, 1)
                hidden(l, 1, 5)
                cosines(l + 1, 0)
                biased_qkv(l + 1, 0, 2)
                hidden(l, 1, 6)
                add_sines(l + 1, 0)
                hidden(l, 1, 7)
                for half in range(2):
                    self_qk(l + 1, 0, half)
                down_residual(l, 1)
            attention(NL - 1, nx)
            hidden_0(NL - 1)
            for f in range(FT):
                hidden(NL - 1, 1, f)
                if f == 0:
                    down_residual(NL - 1, 0)
            down_residual(NL - 1, 1)

            dve.wait_ge(vec_ld, 16)
            for b in range(B):
                mean_square(NL, 0, b)
                dve.wait_ge(rstd_set, NL * NORMS + b + 1)
                for t in range(QT):
                    v = dve.scalar_tensor_tensor(hs[:, 2 * b + t, :], X[:, 2 * b + t, :], rstd[:, b, t:t + 1],
                                                 vec[:, 0:D], ALU.mult, ALU.mult)
                done(v)
                x = X0[:, 2 * b:2 * b + 2, :]
                done(dve.tensor_tensor(x, x, hs[:, 2 * b:2 * b + 2, :], ALU.add))
                layernorm(2 + b, b, X0, hs, lambda v: v.then_inc(an_set, 1))
            for b in range(B):
                dve.wait_ge(*filled(NL, f"an{b}"))
                v = dve.tensor_copy(hT[b][:, :, :].rearrange("p k n -> p (k n)"), bank(f"an{b}")[:, :])
                v.then_inc(free(f"an{b}"), 1)
                dve.wait_ge(*filled(NL, f"wq0{b}"))
                v = masked_q(bank(f"wq0{b}")[:, 0:L], b)
                v.then_inc(free(f"wq0{b}"), 1)
                dve.wait_ge(*filled(NL, f"wk{b}"))
                v = dve.tensor_copy(kTs[b][:, :, :].rearrange("p k n -> p (k n)"), bank(f"wk{b}")[:, :])
                v.then_inc(free(f"wk{b}"), 1)
            dve.wait_ge(*filled(NL, "sum"))
            v = dve.tensor_scalar(mw[:, :], bank("sum")[:, 0:3], 1.0 / (F * D), 1e-5, ALU.mult, ALU.max)
            v.then_inc(free("sum"), 1)
            dve.wait_ge(*emptied(NL, "sum"))
            dve.reciprocal(rw[:, :], mw[:, :]).then_inc(mw_set, 1)

            for i in range(18):
                dve.wait_ge(sig_set, i + 1)
                if i >= 3:
                    dve.wait_ge(wpv_done, i - 2)
                if WINDOW[i % 9][0] == "corner":
                    o, p, m = PT[:, i % 3, 0:2 * P], Pr[:, i % 3, 0:2 * P], corner
                else:
                    o, p, m = PT[:, i % 3, :], Pr[:, i % 3, :], band
                n = m.shape[1]
                h = o.shape[1] // n
                dve.tensor_tensor(o.rearrange("p (h q) -> p h q", q=n), p.rearrange("p (h q) -> p h q", q=n),
                                  m.unsqueeze(1).broadcast_to([P, h, n]), ALU.mult).then_inc(tau_set, 1)
                if i == 9:
                    dve.wait_ge(wpv_done, 9)
                    dve.tensor_copy(On[0][:, :, :].rearrange("p t n -> p (t n)"), psO[:, :]).then_inc(mo_set, 1)
            dve.wait_ge(wpv_done, 18)
            dve.tensor_copy(On[1][:, :, :].rearrange("p t n -> p (t n)"), psO[:, :]).then_inc(mo_set, 1)
            for b in range(B):
                x, y, z = (a[:, 2 * b:2 * b + 2, :] for a in (X0, X, hs))
                dve.wait_ge(*filled(NL, f"mwo{b}"))
                v = dve.tensor_tensor(y, z, tiles(bank(f"mwo{b}")[:, :]), ALU.add)
                v.then_inc(free(f"mwo{b}"), 1)
                dve.wait_ge(*emptied(NL, f"mwo{b}"))
                layernorm(4 + 2 * b, b, X, hs, done)
                done(dve.tensor_tensor(z, z, vec[:, D:2 * D].unsqueeze(1).broadcast_to([P, QT, D]), ALU.mult))
                done(dve.tensor_tensor(z, z, vec[:, 2 * D:3 * D].unsqueeze(1).broadcast_to([P, QT, D]), ALU.add))
                done(dve.tensor_tensor(x, x, z, ALU.add))
                layernorm(5 + 2 * b, b, X0, hs, done)
                quantise_scales(b * 2, 2, z, 0)
                for t in (2 * b, 2 * b + 1):
                    round_tile(hs[:, t, :], t, 0, xq[:, t, :], xq_set)
            for w in range(2):
                dve.tensor_scalar(sgu[:, :, w], am[:, :, 3], mw[:, w:w + 1], None, ALU.mult).then_inc(sgu_set, 1)
            for b in range(B):
                dve.wait_ge(*filled(NL, f"fn{b}"))
                v = dve.tensor_copy(xqT[b][:, :, :].rearrange("p k n -> p (k n)"),
                                    bank(f"fn{b}")[:, :].bitcast(BF16)[:, 0:KT * L])
                v.then_inc(free(f"fn{b}"), 1)
            dve.wait_ge(sgu_set, 2)
            for t in range(4):
                for j in range(2):
                    dve.wait_ge(*filled(NL, f"u{t}{j}"))
                    dve.wait_ge(*emptied(NL, f"g{t}{j}"))
                    v = dve.scalar_tensor_tensor(GU(t)[:, j * 512:(j + 1) * 512], bank(f"u{t}{j}")[:, :],
                                                 sgu[:, t, 1:2], GR(t)[:, j * 512:(j + 1) * 512], ALU.mult, ALU.mult)
                    v.then_inc(free(f"u{t}{j}"), 1)
                for j in range(2):
                    dve.wait_ge(*emptied(NL, f"u{t}{j}"))
                quantise_scales(t, 1, GU(t).unsqueeze(1), 1)
                round_tile(GU(t), t, 1, GQ(t), gq_set)
            done(dve.tensor_scalar(sgu[:, :, 2], am2[:, :, 3], mw[:, 2:3], None, ALU.mult))
            for t in range(4):
                dve.wait_ge(*filled(NL, f"d{t}"))
                v = dve.scalar_tensor_tensor(X[:, t, :], bank(f"d{t}")[:, 0:D], sgu[:, t, 2:3], X0[:, t, :],
                                             ALU.mult, ALU.add)
                v.then_inc(free(f"d{t}"), 1)

        @block.gpsimd
        def _(pool):
            pool.memset(mhalf[:, :], -0.5)
            pool.memset(step[:, :], float(P))
            pool.memset(look[:, :], float(LOOKBACK))
            pool.memset(ones[:, :], 1.0).then_inc(pool_set, 1)

            def rsqrt(l, i, b):
                pool.wait_ge(ms_set, l * NORMS + i * B + b + 1)
                nc.gpsimd.tensor_tensor(rstd[:, i * B + b, :], ms[:, i * B + b, :], mhalf[:, :], ALU.pow)\
                    .then_inc(rstd_set, 1)

            def ln_rsqrt(n):
                pool.wait_ge(ln_var, n + 1)
                nc.gpsimd.tensor_tensor(lrs[:, n, :], lve[:, n, :], mhalf[:, :], ALU.pow).then_inc(ln_rstd, 1)

            def sines(l, b, first=False):
                for t in range(QT):
                    pool.wait_ge(*emptied(l, f"qk{b}{t}"))
                if not first:
                    pool.wait_ge(qr_set, l * B + b)
                    if b == 0:
                        pool.wait_ge(*filled(l - 1, "coT1"))
                q = QK[b][:, :, :].rearrange("p t (h d) -> p t h d", d=HD)
                r = RT[:, :, :].rearrange("p t (h d) -> p t h d", d=HD)
                for to, of in ((0, HD // 2), (HD // 2, 0)):
                    g = nc.gpsimd.tensor_tensor(r[:, :, :, to:to + HD // 2], q[:, :, :, of:of + HD // 2],
                                                sin[:, :, to:to + HD // 2].unsqueeze(2)
                                                .broadcast_to([P, QT, 2 * H, HD // 2]), ALU.mult)
                g.then_inc(sin_set, 1)

            def add_bo(l, b):
                pool.wait_ge(h_set, l * NORMS + b + 1)
                pool.wait_ge(bias_ld, l * 16 + 16)
                x = X[:, 2 * b:2 * b + 2, :]
                nc.gpsimd.tensor_tensor(x, x, bias[:, 3 * D:4 * D].unsqueeze(1).broadcast_to([P, QT, D]), ALU.add)\
                    .then_inc(xbo_set, 1)

            def further_blocks(l, b, nx):
                with pool.If(nx > 0):
                    nc.gpsimd.tensor_tensor(segR[:, :], segF[:, :], step[:, :], ALU.subtract).then_inc(g_rel, 1)
                    pool.wait_ge(g_rel, 2 * (l * B + b) * (nx + 1) + 1)
                    nc.gpsimd.tensor_tensor(segL[:, :], segR[:, :], look[:, :], ALU.subtract).then_inc(g_rel, 1)
                    with pool.Fori(0, nx) as j:
                        c = pool.snap((l * B + b) * nx + j)
                        pool.wait_ge(g_mask, c + 1)
                        nc.gpsimd.tensor_tensor(segR[:, :], segR[:, :], step[:, :], ALU.subtract).then_inc(g_rel, 1)
                        nc.gpsimd.tensor_tensor(segL[:, :], segL[:, :], step[:, :], ALU.subtract).then_inc(g_rel, 1)
                        pool.wait_ge(or_copied, l * B + b + 1)
                        pool.wait_ge(g_max, (c + 1) * NCROSS)
                        nc.gpsimd.tensor_tensor(dm[:, b, :], nmN[:, b, :], nmR[:, b, :], ALU.subtract).then_inc(g_dm, 1)
                        pool.wait_ge(g_dm, c + 1)
                        nc.gpsimd.tensor_tensor(nmR[:, b, :], nmN[:, b, :], ones[:, 0:QT * H], ALU.mult).then_inc(g_nmr, 1)
                        pool.wait_ge(g_al, c + 1)
                        nc.gpsimd.tensor_tensor(lR[:, b, :], lR[:, b, :], al[:, b, :], ALU.mult).then_inc(g_lr, 1)
                        pool.wait_ge(g_lr, c + 1)
                        pool.wait_ge(g_exp, (c + 1) * NCROSS)
                        nc.gpsimd.tensor_tensor(lR[:, b, :], lR[:, b, :], lB[:, b, :], ALU.add)
                        nc.gpsimd.tensor_tensor(heads(OR[b][:, :, :]), heads(OR[b][:, :, :]),
                                                al[:, b, :].unsqueeze(2).broadcast_to([P, QT * H, HD]), ALU.mult)\
                            .then_inc(g_scaled, 1)
                        pool.wait_ge(g_added, c + 1)

            def attention(l, nx):
                rsqrt(l, 0, 1)
                add_bo(l, 1)
                sines(l, 1)
                rsqrt(l, 1, 0)
                rsqrt(l, 1, 1)
                further_blocks(l, 0, nx)
                rsqrt(l, 2, 0)
                further_blocks(l, 1, nx)
                rsqrt(l, 2, 1)

            pool.wait_ge(pool_set, 1)
            ln_rsqrt(0)
            rsqrt(0, 0, 0)
            ln_rsqrt(1)
            pool.wait_ge(c_ld, 16)
            add_bo(0, 0)
            sines(0, 0, first=True)
            pool.wait_ge(nb_set, 1)
            nx = pool.value_load(NX[0:1, 0:1], min_val=0, max_val=NBLK - 1)
            pool.wait_ge(consts_set, 2)
            with pool.Fori(0, NL - 1) as l:
                attention(l, nx)
                rsqrt(l + 1, 0, 0)
                add_bo(l + 1, 0)
                sines(l + 1, 0)
            attention(NL - 1, nx)

            for b in range(B):
                rsqrt(NL, 0, b)
                ln_rsqrt(2 + b)
            pool.wait_ge(wf_ld, 16)
            pool.wait_ge(mw_set, 1)
            for w in range(3):
                nc.gpsimd.tensor_scalar(WF[:, w, :], WF[:, w, :], rw[:, w:w + 1], MAGIC, ALU.mult, ALU.add)\
                    .then_inc(tern_step, 1)
                pool.wait_ge(tern_step, 2 * w + 1)
                nc.gpsimd.tensor_scalar(WF[:, w, :], WF[:, w, :], MAGIC, 1.0, ALU.subtract, ALU.min)\
                    .then_inc(tern_step, 1)
                pool.wait_ge(tern_step, 2 * w + 2)
                nc.gpsimd.tensor_scalar(WQ[:, w, :], WF[:, w, :], -1.0, None, ALU.max).then_inc(tern_set, 1)
            for b in range(B):
                ln_rsqrt(4 + 2 * b)
                ln_rsqrt(5 + 2 * b)


def constants():
    import numpy as np

    c = np.zeros((P, C_N), np.float32)
    p = np.arange(P)
    c[:, C_ID:C_ID + P] = np.eye(P, dtype=np.float32)
    c[:, C_CAUSAL + P:C_CAUSAL + 2 * P] = np.where(p[None, :] > p[:, None], NEG, 0.0)
    c[:, C_HEAD:C_HEAD + HT] = np.where(p[:, None] // HD == np.arange(HT)[None, :], SCALE, 0.0)
    inv = (np.float32(1.0) / np.float32(10000.0) ** (np.arange(0, HD, 2, dtype=np.float32) / np.float32(HD))).astype(np.float32)
    f = (np.arange(L, dtype=np.float32)[:, None] * inv[None, :]).astype(np.float32)
    cos, sin = np.cos(f), np.sin(f)
    cos = np.concatenate([cos, cos], 1).reshape(QT, P, HD).transpose(1, 0, 2)
    sin = np.concatenate([-sin, sin], 1).reshape(QT, P, HD).transpose(1, 0, 2)
    c[:, C_COS:C_COS + QT * HD] = cos.reshape(P, -1)
    c[:, C_SIN:C_SIN + QT * HD] = sin.reshape(P, -1)
    c[:, C_IOTA:C_IOTA + P] = p[None, :]
    back = p[None, :] - p[:, None]
    c[:, C_BAND:C_BAND + P] = (back >= 1) & (back <= HD)
    back = P + np.arange(HD)[None, :] - p[:, None]
    c[:, C_CORNER:C_CORNER + HD] = (back >= 1) & (back <= HD)
    return c


def rows_on_partitions(w):
    import numpy as np

    w = np.swapaxes(w, -1, -2)
    lead, (n_in, n_out) = w.shape[:-2], w.shape[-2:]
    w = w.reshape(*lead, n_in // P, P, n_out)
    return np.moveaxis(w, -2, -3).reshape(*lead, P, -1)


def kernel(**inputs):
    import numpy as np
    import concourse.bacc as bacc
    from concourse.bass_utils import run_bass_kernel_spmd as run

    a = {k: np.asarray(v) for k, v in inputs.items()}
    X, A, G = "L0_xattn_", "L0_attn_", "L0_ffn_"
    x = a["x"].reshape(4, P, D).transpose(1, 0, 2)
    ctx = a["ctx_1024"].reshape(B, NBLK, P, KT, P).transpose(1, 4, 3, 0, 2)
    seg = a["itok_BxS_0_255"].reshape(4, P)
    seg = np.concatenate([seg.T.ravel(), seg.ravel()])
    wa = np.concatenate([rows_on_partitions(a[X + "Wqkv"]), rows_on_partitions(a[X + "Wo"])], -1)
    wb = np.concatenate([rows_on_partitions(a[X + n]) for n in ("Wq_c", "Wkv_c", "Wo_c")], -1)
    wc = np.concatenate([rows_on_partitions(a[X + n]) for n in ("Wg", "Wu", "Wd")], -1)
    nrm = np.stack([a[X + n] for n in ("n1", "n2", "n3")], 1).reshape(NL, 3, KT, P).transpose(0, 3, 1, 2).reshape(NL, P, -1)
    bias = np.concatenate([a[X + "bqkv"], a[X + "bo"]], -1)
    vec = np.concatenate([a[X + "nf"], a[A + "gamma"], a[A + "beta"]])[None, :]
    wkv = a[A + "wkv"].reshape(H, 2, HD, D)
    wt = np.concatenate([rows_on_partitions(w) for w in (a[A + "wq"], wkv[:, 0].reshape(D, D), wkv[:, 1].reshape(D, D), a[A + "wo"])], -1)
    wf = np.stack([rows_on_partitions(a[G + n]) for n in ("w_gate", "w_up", "w_down")], 1)
    arrays = {"x": x, "ctx": ctx, "seg": seg, "wa": wa, "wb": wb, "wc": wc, "nrm": nrm, "bias": bias, "vec": vec,
              "wt": wt, "wf": wf, "const": constants()}
    arrays = {k: np.ascontiguousarray(v) for k, v in arrays.items()}
    nc = bacc.Bacc("TRN2", target_bir_lowering=False, num_devices=1)
    args = [nc.dram_tensor(f"in_{k}", v.shape, mybir.dt.from_np(v.dtype), kind="ExternalInput").ap() for k, v in arrays.items()]
    out = nc.dram_tensor("out_x", (4, P, D), F32, kind="ExternalOutput").ap()
    perceiver(nc, *args, out)
    r = run(nc, [{f"in_{k}": v for k, v in arrays.items()}], core_ids=[0])
    return r.results[0]["out_x"].reshape(B, L, D)
```

```python
from contextlib import ExitStack

import concourse.bass as bass
from concourse import mybir

F32 = mybir.dt.float32
F32R = mybir.dt.float32r
BF16 = mybir.dt.bfloat16
I32 = mybir.dt.int32
ALU = mybir.AluOpType
ACT = mybir.ActivationFunctionType
AX_X = mybir.AxisListType.X

P = 128
B, L, D = 2, 256, 256
H, HD = 16, 16
NL = 4
S_CTX = 4096
LOOKBACK = 128
F = 1024
QT = L // P
KT = D // P
HT = H // KT
FT = F // P
NBLK = S_CTX // P
RMS_EPS, LN_EPS = 1e-6, 1e-5
NEG = -1e30
NO_MAX = 3e38
MAGIC = 12582912.0
SCALE = HD ** -0.5

WA_QKV, WA_O, WA_N = 0, KT * 3 * D, KT * 4 * D
WB_Q, WB_KV, WB_O, WB_N = 0, KT * D, KT * 3 * D, KT * 4 * D
WC_G, WC_U, WC_D, WC_N = 0, KT * F, 2 * KT * F, 2 * KT * F + FT * D
C_ID, C_CAUSAL, C_HEAD, C_COS, C_SIN, C_IOTA, C_BAND, C_CORNER = 0, 128, 256, 264, 296, 328, 456, 584
C_N = 600

SELF = [(0, 4 * g, 4, P) for g in range(4)] + [(1, 2 * g, 2, 2 * P) for g in range(8)]
CROSS = [(q, 4 * g, 4, P) for q in range(QT) for g in range(4)]
NSELF, NCROSS = len(SELF), len(CROSS)
GROUPS = [(0, b, *g) for b in range(B) for g in SELF] + [(1, b, *g) for b in range(B) for g in CROSS]
NG = len(GROUPS)
S0, S1, C0, C1 = 0, NSELF, B * NSELF, B * NSELF + NCROSS
WINDOW = [(blk, k, half) for blk in range(QT) for k in range(KT) for half in range(2)] + [("corner", 0, 0)]
NORMS = 3 * B
SBANKS, PBANKS, DBANKS = 3, 2, 2

LAYER_USES = (
    [u for b in range(B) for u in (f"n0{b}", f"qk{b}0", f"qk{b}1", f"v{b}", f"tq{b}0", f"tq{b}1")]
    + [u for b in range(B) for u in (f"oT{b}", f"wo{b}", f"n1{b}", f"kv{b}", f"qc{b}0", f"qc{b}1")]
    + [u for b in range(B) for u in (f"coT{b}", f"cwo{b}", f"n2{b}")]
)
TAIL_USES = (
    ["sum"] + [u for b in range(B) for u in (f"an{b}", f"wq0{b}", f"wq1{b}", f"wk{b}", f"wv{b}")]
    + ["moT0", "mwo0", "fn0", "moT1", "mwo1", "fn1", "gT0", "d0"] + [u for t in range(1, 4) for u in (f"gT{t}", f"d{t}")]
)
KV_BANK = ("qc11", "n20")
GU_FIRST = (NG - 2) % 3
NW = len(WINDOW)
RING = 3
ABS_CHUNKS = 4
ABS_AT = [1, 2, 3, 4, 5, 6, 7, 10, S1 + 5, S1 + 9, S1 + 10, S1 + 11]


def bank_order(uses):
    seen, at = [0] * DBANKS, {}
    for n, u in enumerate(uses):
        at[u] = (n % DBANKS, seen[n % DBANKS])
        seen[n % DBANKS] += 1
    return at, seen


LAYER_AT, LAYER_TOTAL = bank_order(LAYER_USES)
TAIL_AT, _ = bank_order(TAIL_USES)


def perceiver(nc, x_in, ctx_in, seg_in, wa_in, wb_in, wc_in, nrm_in, bias_in, vec_in, wt_in, wf_in, const_in, out):
    stack = ExitStack()
    with stack:
        def sb(name, shape, dt=F32):
            return stack.enter_context(nc.sbuf_tensor(name, shape, dt))

        def ps(name):
            return stack.enter_context(nc.psum_tensor(name, [P, 512], F32))

        def sem(name):
            return stack.enter_context(nc.semaphore(name))

        X0 = sb("X0", [P, 4, D])
        X = sb("X", [P, 4, D])
        hs = sb("hs", [P, 4, D])
        hT = [sb(f"hT{b}", [P, KT, L]) for b in range(B)]
        WAB = sb("WAB", [P, WA_N + WB_N])
        WA, WB = WAB[:, 0:WA_N], WAB[:, WA_N:WA_N + WB_N]
        WC = sb("WC", [P, WC_N])
        nrm = sb("nrm", [P, 3 * KT])
        bias = sb("bias", [P, 4 * D])
        vec = sb("vec", [P, 3 * D])
        WT = WAB[:, 0:KT * 4 * D]
        WFH = sb("WFH", [P, RING, 2 * KT * P], F32R)
        WFL = sb("WFL", [P, RING, 2 * KT * P], F32R)
        HH = sb("HH", [P, KT, L], F32R)
        HL = sb("HL", [P, KT, L], F32R)
        const = sb("const", [P, C_N])
        identB = sb("identB", [P, P], BF16)
        causB = sb("causB", [P, P], BF16)
        HID = [sb(f"HID{b}", [P, 2 * QT * 2 * D]) for b in range(B)]
        QK = [HID[b][:, 0:QT * 2 * D].rearrange("p (t n) -> p t n", t=QT) for b in range(B)]
        QR = [HID[b][:, QT * 2 * D:].rearrange("p (t n) -> p t n", t=QT) for b in range(B)]
        AT = [HID[b][:, :].rearrange("p (f n) -> p f n", f=FT) for b in range(B)]
        V = [sb(f"V{b}", [P, QT, D]) for b in range(B)]
        QM = [sb(f"QM{b}", [P, KT, HT, L]) for b in range(B)]
        kTs = [sb(f"kTs{b}", [P, KT, L]) for b in range(B)]
        Pr = sb("Pr", [P, 3, 512])
        PT = sb("PT", [P, 3, 512])
        ON = sb("ON", [P, B * QT * D])
        On = [ON[:, b * QT * D:(b + 1) * QT * D].rearrange("p (t n) -> p t n", t=QT) for b in range(B)]
        RT = ON[:, :].rearrange("p (t n) -> p t n", t=QT)
        oT = [sb(f"oT{b}", [P, KT, L]) for b in range(B)]
        CT = sb("CT", [P, KT, B, P])
        CTg = sb("CTg", [P, KT, P])
        KV = [sb(f"KV{b}", [P, 2 * D]) for b in range(B)]
        KC = [KV[b][:, 0:D].rearrange("p (k n) -> p k n", k=KT) for b in range(B)]
        VC = [KV[b][:, D:2 * D] for b in range(B)]
        OR = [HID[b][:, 0:QT * D].rearrange("p (t n) -> p t n", t=QT) for b in range(B)]
        SG = sb("SG", [P, 2, L])
        ss = sb("ss", [P, NORMS, QT])
        ms = sb("ms", [P, NORMS, QT])
        rstd = sb("rstd", [P, NORMS, QT])
        mhalf = sb("mhalf", [P, QT])
        segR = sb("segR", [P, 4])
        nms = sb("nms", [P, B, QT * H])
        lS = sb("lS", [P, B, QT * H])
        rl = sb("rl", [P, B, QT * H])
        nmB = sb("nmB", [P, B, QT * H])
        nmN = sb("nmN", [P, B, QT * H])
        nmR = sb("nmR", [P, B, QT * H])
        lB = sb("lB", [P, B, QT * H])
        lR = sb("lR", [P, B, QT * H])
        dm = sb("dm", [P, B, QT * H])
        al = sb("al", [P, B, QT * H])
        segI = sb("segI", [P, 4], I32)
        segF = sb("segF", [P, 4])
        segL = sb("segL", [P, 4])
        rowI = sb("rowI", [1, 4 * P], I32)
        rowF = sb("rowF", [1, 4 * P])
        few = sb("few", [1, 8])
        cnt = sb("cnt", [1, NBLK - 1])
        NX = sb("NX", [1, 1], I32)
        step = sb("step", [P, 4])
        look = sb("look", [P, 4])
        mA, mB = (HID[0][:, at * P:(at + 4) * P].rearrange("p (t n) -> p t n", t=4) for at in (4, 8))
        maskB = sb("maskB", [P, 4, P], BF16)
        maskG = sb("maskG", [P, QT, P], BF16)
        bst = sb("bst", [P, 8, QT, 6])
        mv = sb("mv", [P, 8, QT, 2])
        lve = sb("lve", [P, 8, QT])
        lrs = sb("lrs", [P, 8, QT])
        ones = sb("ones", [P, P])
        asum = sb("asum", [P, 3 * ABS_CHUNKS])
        awsum = sb("awsum", [P, 3])
        negmagic = sb("negmagic", [P, 1])
        WF = sb("WF", [P, 3, 2048])
        mw = sb("mw", [P, 3])
        rw = sb("rw", [P, 3])
        WQ = ([WAB[:, (2 + w) * 1024:(3 + w) * 1024].bitcast(BF16) for w in range(2)]
              + [WC[:, 0:1024].bitcast(BF16)])
        xq = KV[0][:, :].bitcast(BF16).rearrange("p (t n) -> p t n", t=4)
        xqT = [KV[1][:, b * 256:(b + 1) * 256].bitcast(BF16).rearrange("p (k n) -> p k n", k=KT) for b in range(B)]
        am = sb("am", [P, 4, 4])
        am2 = sb("am2", [P, 4, 4])
        sgu = sb("sgu", [P, 4, 3])

        psS = [ps(f"psS{i}") for i in range(SBANKS)]
        psP = [ps(f"psP{i}") for i in range(PBANKS)]
        psO = ps("psO")
        psD = [ps(f"psD{i}") for i in range(DBANKS)]
        QB = [psP, psS[0:2]]

        c_ld, x_ld, seg_ld, vec_ld = sem("c_ld"), sem("x_ld"), sem("seg_ld"), sem("vec_ld")
        wa_ld, wb_ld, wc_ld, nrm_ld, bias_ld = sem("wa_ld"), sem("wb_ld"), sem("wc_ld"), sem("nrm_ld"), sem("bias_ld")
        wt_ld, wf_ld, ct_ld, g_ct_ld = sem("wt_ld"), sem("wf_ld"), sem("ct_ld"), sem("g_ct_ld")
        d_full = [sem(f"d_full{i}") for i in range(DBANKS)]
        d_free = [sem(f"d_free{i}") for i in range(DBANKS)]
        consts_set = sem("consts_set")
        nb_set = sem("nb_set")
        x_first = sem("x_first")
        ss_set, ms_set, rstd_set, h_set = (sem(n) for n in ("ss_set", "ms_set", "rstd_set", "h_set"))
        cos_set, sin_set, qr_set = (sem(n) for n in ("cos_set", "sin_set", "qr_set"))
        xbo_set = sem("xbo_set")
        s_full, s_max, s_exp, t_full, t_copied, pv_done = (
            sem(n) for n in ("s_full", "s_max", "s_exp", "t_full", "t_copied", "pv_done"))
        rl_set, on_set = sem("rl_set"), sem("on_set")
        mask_cmp, mask_set = sem("mask_cmp"), sem("mask_set")
        or_copied, crl_set, con_set = sem("or_copied"), sem("crl_set"), sem("con_set")
        wh_set, wl_set, hh_set, hx_set = (sem(n) for n in ("wh_set", "wl_set", "hh_set", "hx_set"))
        gu_full, hid_set, y_full, y_free = sem("gu_full"), sem("hid_set"), sem("y_full"), sem("y_free")
        g_rel, g_cmp, g_mask, g_kv_full, g_kv_set = (
            sem(n) for n in ("g_rel", "g_cmp", "g_mask", "g_kv_full", "g_kv_set"))
        g_s_full, g_bmax, g_max, g_exp, g_t_full, g_t_copied, g_pv_done = (
            sem(n) for n in ("g_s_full", "g_bmax", "g_max", "g_exp", "g_t_full", "g_t_copied", "g_pv_done"))
        g_dm, g_nmr, g_al, g_lr, g_scaled, g_added = (
            sem(n) for n in ("g_dm", "g_nmr", "g_al", "g_lr", "g_scaled", "g_added"))
        sg_set = sem("sg_set")
        ln_var, ln_rstd = sem("ln_var"), sem("ln_rstd")
        v_step = sem("v_step")
        an_set = sem("an_set")
        ws_full, sig_set, tau_set, wpv_done = sem("ws_full"), sem("sig_set"), sem("tau_set"), sem("wpv_done")
        mo_set = sem("mo_set")
        qg_full, qg_free, qu_full, qu_free = sem("qg_full"), sem("qg_free"), sem("qu_full"), sem("qu_free")
        gq_scale_set, gq_scaled, gq_clamped = sem("gq_scale_set"), sem("gq_scaled"), sem("gq_clamped")
        asum_set, mw_set, tern_set, sgu_set = sem("asum_set"), sem("mw_set"), sem("tern_set"), sem("sgu_set")
        pool_set, tern_step = sem("pool_set"), sem("tern_step")
        xq_set, gq_set = sem("xq_set"), sem("gq_set")
        stored = sem("stored")

        ident = const[:, C_ID:C_ID + P]
        headmask = const[:, C_HEAD:C_HEAD + HT]
        cos = const[:, C_COS:C_COS + QT * HD].rearrange("p (t d) -> p t d", t=QT)
        sin = const[:, C_SIN:C_SIN + QT * HD].rearrange("p (t d) -> p t d", t=QT)
        iota = const[:, C_IOTA:C_IOTA + P]
        band = const[:, C_BAND:C_BAND + P]
        corner = const[:, C_CORNER:C_CORNER + HD]
        Wqkv = WA[:, WA_QKV:WA_O].rearrange("p (k n) -> p k n", k=KT)
        Wo = WA[:, WA_O:WA_N].rearrange("p (k n) -> p k n", k=KT)
        Wqc = WB[:, WB_Q:WB_KV].rearrange("p (k n) -> p k n", k=KT)
        Wkv = WB[:, WB_KV:WB_O].rearrange("p (k n) -> p k n", k=KT)
        Woc = WB[:, WB_O:WB_N].rearrange("p (k n) -> p k n", k=KT)
        Wd = WC[:, WC_D:WC_N].rearrange("p (k n) -> p k n", k=FT)
        Wt = WT.rearrange("p (w k n) -> p w k n", w=4, k=KT)

        WCt = WC[:, WC_G:WC_D].rearrange("p (m n) -> p m n", m=2 * KT)

        def w_high(n):
            return WFH[:, n % RING, :].rearrange("p (m n) -> p m n", m=2 * KT)

        def w_low(n):
            return WFL[:, n % RING, :].rearrange("p (m n) -> p m n", m=2 * KT)

        def filled(l, use):
            k, n = (LAYER_AT if use in LAYER_AT else TAIL_AT)[use]
            return d_full[k], l * LAYER_TOTAL[k] + n + 1

        def free_for(l, use):
            k, n = (LAYER_AT if use in LAYER_AT else TAIL_AT)[use]
            return d_free[k], l * LAYER_TOTAL[k] + n + 1

        def emptied(l, use):
            k, n = (LAYER_AT if use in LAYER_AT else TAIL_AT)[use]
            return d_free[k], l * LAYER_TOTAL[k] + n + 2

        def bank(use):
            return psD[(LAYER_AT if use in LAYER_AT else TAIL_AT)[use][0]]

        def full(use):
            return d_full[(LAYER_AT if use in LAYER_AT else TAIL_AT)[use][0]]

        def free(use):
            return d_free[(LAYER_AT if use in LAYER_AT else TAIL_AT)[use][0]]

        def heads(ap):
            return ap.rearrange("p t (h d) -> p (t h) d", d=HD)

        def tiles(ap):
            return ap.rearrange("p (a n) -> p a n", a=2)

        def GU(t):
            return QM[t // 2][:, :, :, :].rearrange("p k h n -> p (k h n)")[:, (t % 2) * 2048:(t % 2) * 2048 + F]

        def GR(t):
            return QM[t // 2][:, :, :, :].rearrange("p k h n -> p (k h n)")[:, (t % 2) * 2048 + F:(t % 2) * 2048 + 2 * F]

        def GQ(t):
            return AT[t // 2][:, :, :].rearrange("p f n -> p (f n)").bitcast(BF16)[:, (t % 2) * 2048:(t % 2) * 2048 + F]

        def GQT(t):
            return AT[t // 2][:, :, :].rearrange("p f n -> p (f n)").bitcast(BF16)[:, (t % 2) * 2048 + F:(t % 2) * 2048 + 2 * F]

        block = stack.enter_context(nc.Block())

        @block.sync
        def _(sp):
            sp.dma_start(X0[:, :, :], x_in).then_inc(x_ld, 16)
            sp.dma_start(const[:, :], const_in).then_inc(c_ld, 16)
            sp.dma_start(nrm[:, :], nrm_in[0]).then_inc(nrm_ld, 16)
            sp.dma_start(WA, wa_in[0]).then_inc(wa_ld, 16)
            sp.dma_start(bias[:, :], bias_in[0:1, :].broadcast_to([P, 4 * D])).then_inc(bias_ld, 16)
            sp.dma_start(rowI[:, :], seg_in[4 * P:8 * P].rearrange("(a n) -> a n", a=1)).then_inc(seg_ld, 16)
            sp.dma_start(segI[:, :], seg_in[0:4 * P].rearrange("(p t) -> p t", t=4)).then_inc(seg_ld, 16)
            sp.dma_start(CT[:, :, :, :], ctx_in[0]).then_inc(ct_ld, 16)
            sp.dma_start(WB, wb_in[0]).then_inc(wb_ld, 16)
            sp.dma_start(WC[:, :], wc_in[0]).then_inc(wc_ld, 16)
            sp.dma_start(vec[:, :], vec_in[0:1, :].broadcast_to([P, 3 * D])).then_inc(vec_ld, 16)
            sp.dma_start(WF[:, :, :], wf_in).then_inc(wf_ld, 16)
            sp.wait_ge(nb_set, 1)
            nx = sp.value_load(NX[0:1, 0:1], min_val=0, max_val=NBLK - 1)

            def further_blocks(l, b):
                with sp.If(nx > 0):
                    with sp.Fori(0, nx) as j:
                        sp.wait_ge(g_kv_full, (l * B + b) * nx + j + 1)
                        sp.dma_start(CTg[:, :, :], ctx_in[j + 1][:, :, b, :]).then_inc(g_ct_ld, 16)

            with sp.Fori(0, NL - 1) as l:
                sp.wait_ge(*emptied(l, "v1"))
                sp.wait_ge(xbo_set, (l + 1) * B)
                sp.dma_start(bias[:, :], bias_in[l + 1].rearrange("(a n) -> a n", a=1).broadcast_to([P, 4 * D])).then_inc(bias_ld, 16)
                sp.wait_ge(*filled(l, "wo1"))
                sp.dma_start(WA, wa_in[l + 1]).then_inc(wa_ld, 16)
                for b in range(B):
                    further_blocks(l, b)
                sp.wait_ge(*filled(l, "cwo1"))
                sp.dma_start(WB, wb_in[l + 1]).then_inc(wb_ld, 16)
                sp.wait_ge(*emptied(l, "n21"))
                sp.dma_start(nrm[:, :], nrm_in[l + 1]).then_inc(nrm_ld, 16)
                sp.wait_ge(y_full, l * B + 2)
                sp.dma_start(WC[:, :], wc_in[l + 1]).then_inc(wc_ld, 16)
            sp.wait_ge(*filled(NL - 1, "wo1"))
            sp.dma_start(WT, wt_in).then_inc(wt_ld, 16)
            for b in range(B):
                further_blocks(NL - 1, b)
            for t in range(4):
                sp.wait_ge(*emptied(NL, f"d{t}"))
                sp.dma_start(out[t], X[:, t, :]).then_inc(stored, 16)
            sp.wait_ge(stored, 4 * 16)

        @block.tensor
        def _(pe):
            def transposes(l, use, src, b):
                pe.wait_ge(*free_for(l, use))
                for k in range(KT):
                    for t in range(QT):
                        mm = pe.transpose(bank(use)[:, k * L + t * P:k * L + (t + 1) * P],
                                          src[:, t, k * P:(k + 1) * P], ident)
                mm.then_inc(full(use), 1)

            def project(l, use, col, lhs, rhs, n=D):
                for k in range(KT):
                    mm = pe.matmul(bank(use)[:, col:col + n], lhs(k), rhs(k), start=(k == 0), stop=(k == KT - 1))
                return mm

            def norm_T(l, i, b):
                pe.wait_ge(h_set, l * NORMS + i * B + b + 1)
                transposes(l, f"n{i}{b}", hs[:, 2 * b:2 * b + 2, :], b)

            def qkv(l, b, part):
                if part == 0:
                    pe.wait_ge(*emptied(l, f"n0{b}"))
                    pe.wait_ge(wa_ld, l * 16 + 16)
                if part < QT:
                    use = f"qk{b}{part}"
                    pe.wait_ge(*free_for(l, use))
                    mm = project(l, use, 0, lambda k: hT[b][:, k, part * P:(part + 1) * P],
                                 lambda k: Wqkv[:, k, 0:2 * D], 2 * D)
                else:
                    use = f"v{b}"
                    pe.wait_ge(*free_for(l, use))
                    for t in range(QT):
                        mm = project(l, use, t * D, lambda k: hT[b][:, k, t * P:(t + 1) * P],
                                     lambda k: Wqkv[:, k, 2 * D:3 * D])
                mm.then_inc(full(use), 1)

            def rotated_T(l, b, k):
                pe.wait_ge(qr_set, l * B + b + 1)
                use = f"tq{b}{k}"
                pe.wait_ge(*free_for(l, use))
                for w in range(2):
                    for t in range(QT):
                        mm = pe.transpose(bank(use)[:, w * L + t * P:w * L + (t + 1) * P],
                                          QR[b][:, t, w * D + k * P:w * D + (k + 1) * P], ident)
                mm.then_inc(full(use), 1)

            def masked_scores(S, b, q, h0, nh, keys, mask, keysT):
                last = keys - P
                pe.matmul(S[:, :].rearrange("p (h k) -> p h k", h=nh)[:, :, last:keys], identB[:, :],
                          mask.unsqueeze(1).broadcast_to([P, nh, P]), start=True, stop=False, skip_group_check=True)
                for j in range(nh):
                    h = h0 + j
                    mm = pe.matmul(S[:, j * keys:(j + 1) * keys], QM[b][:, h // HT, h % HT, q * P:(q + 1) * P],
                                   keysT[:, h // HT, 0:keys], start=False, stop=True, skip_group_check=True)
                return mm

            def scores(l, i):
                cross, b, q, h0, nh, keys = GROUPS[i]
                if i in (S0, S1):
                    pe.wait_ge(*emptied(l, f"tq{b}0"))
                if i in (S0 + 2, S1 + 2):
                    pe.wait_ge(*emptied(l, f"tq{b}1"))
                if i in (C0, C1):
                    pe.wait_ge(mask_set, 1)
                    pe.wait_ge(*emptied(l, f"kv{b}"))
                    pe.wait_ge(*emptied(l, f"qc{b}0"))
                if i in (C0 + 2, C1 + 2):
                    pe.wait_ge(*emptied(l, f"qc{b}1"))
                if i >= SBANKS:
                    pe.wait_ge(s_exp, l * NG + i - SBANKS + 1)
                mask = maskB[:, 2 * b + q, :] if cross else causB[:, :]
                masked_scores(psS[i % SBANKS], b, q, h0, nh, keys, mask, KC[b] if cross else kTs[b])\
                    .then_inc(s_full, 1)

            def probs_T(l, i):
                pe.wait_ge(s_exp, l * NG + i + 1)
                if i >= PBANKS:
                    pe.wait_ge(t_copied, l * NG + i - PBANKS + 1)
                for j in range(4):
                    mm = pe.transpose(psP[i % PBANKS][:, j * P:(j + 1) * P], Pr[:, i % 3, j * P:(j + 1) * P], ident)
                mm.then_inc(t_full, 1)

            def pv(l, i):
                cross, b, q, h0, nh, keys = GROUPS[i]
                first = i in (S0, S1, C0, C1)
                if i == S0:
                    pe.wait_ge(*emptied(l, "v0"))
                    pe.wait_ge(y_free, l * B + 1)
                if i == S1:
                    pe.wait_ge(*emptied(l, "v1"))
                    pe.wait_ge(on_set, l * B + 1)
                if i == C0:
                    pe.wait_ge(on_set, l * B + 2)
                if i == C1:
                    pe.wait_ge(or_copied, l * B + 1)
                pe.wait_ge(t_copied, l * NG + i + 1)
                nk = keys // P
                for j in range(nh):
                    h = h0 + j
                    for k in range(nk):
                        values = VC[b] if cross else V[b][:, k, :]
                        mm = pe.matmul(psO[:, q * D + h * HD:q * D + (h + 1) * HD],
                                       PT[:, i % 3, (j * nk + k) * P:(j * nk + k + 1) * P],
                                       values[:, h * HD:(h + 1) * HD],
                                       start=(first and j == 0 and k == 0), stop=True, skip_group_check=True)
                mm.then_inc(pv_done, 1)

            def out_T(l, b, use, src, ready, value):
                pe.wait_ge(ready, value)
                transposes(l, use, src, b)

            def out_proj(l, b, use, W, source):
                pe.wait_ge(*emptied(l, source))
                pe.wait_ge(*free_for(l, use))
                for t in range(QT):
                    mm = project(l, use, t * D, lambda k: oT[b][:, k, t * P:(t + 1) * P], lambda k: W[:, k, :])
                mm.then_inc(full(use), 1)

            def cross_q(l, b):
                pe.wait_ge(*emptied(l, f"n1{b}"))
                pe.wait_ge(wb_ld, l * 16 + 16)
                for m in range(KT):
                    use = f"qc{b}{m}"
                    pe.wait_ge(*free_for(l, use))
                    project(l, use, 0, lambda k: Wqc[:, k, m * P:(m + 1) * P],
                            lambda k: hT[b][:, k, :]).then_inc(full(use), 1)

            def keys_values(P_bank, b, CTb):
                for m in range(KT):
                    for k in range(KT):
                        pe.matmul(P_bank[:, m * P:(m + 1) * P], Wkv[:, k, m * P:(m + 1) * P], CTb[:, k, :],
                                  start=(k == 0), stop=(k == KT - 1))
                for k in range(KT):
                    mm = pe.matmul(P_bank[:, D:2 * D], CTb[:, k, :], Wkv[:, k, D:2 * D],
                                   start=(k == 0), stop=(k == KT - 1))
                return mm

            def cross_kv(l, b):
                pe.wait_ge(ct_ld, 16)
                pe.wait_ge(wb_ld, l * 16 + 16)
                pe.wait_ge(*free_for(l, f"kv{b}"))
                keys_values(bank(f"kv{b}"), b, CT[:, :, b, :]).then_inc(full(f"kv{b}"), 1)

            def further_blocks(l, b, nx):
                with pe.If(nx > 0):
                    with pe.Fori(0, nx) as j:
                        c = pe.snap((l * B + b) * nx + j)
                        pe.wait_ge(g_ct_ld, c * 16 + 16)
                        pe.wait_ge(*emptied(l, KV_BANK[b]))
                        keys_values(bank(KV_BANK[b]), b, CTg).then_inc(g_kv_full, 1)
                        pe.wait_ge(g_mask, c + 1)
                        pe.wait_ge(g_kv_set, c + 1)
                        pe.wait_ge(or_copied, l * B + b + 1)
                        for i in range(NCROSS + 2):
                            if i < NCROSS:
                                q, h0, nh, keys = CROSS[i]
                                if i >= 2:
                                    pe.wait_ge(g_exp, c * NCROSS + i - 1)
                                masked_scores(psS[i % 2], b, q, h0, nh, keys, maskG[:, q, :], KC[b])\
                                    .then_inc(g_s_full, 1)
                            if 1 <= i <= NCROSS:
                                n = i - 1
                                pe.wait_ge(g_exp, c * NCROSS + n + 1)
                                if n >= 2:
                                    pe.wait_ge(g_t_copied, c * NCROSS + n - 1)
                                for m in range(4):
                                    mm = pe.transpose(psP[n % 2][:, m * P:(m + 1) * P],
                                                      Pr[:, n % 3, m * P:(m + 1) * P], ident)
                                mm.then_inc(g_t_full, 1)
                            if i >= 2:
                                n = i - 2
                                q, h0, nh, keys = CROSS[n]
                                pe.wait_ge(g_t_copied, c * NCROSS + n + 1)
                                for m in range(4):
                                    h = h0 + m
                                    mm = pe.matmul(psO[:, q * D + h * HD:q * D + (h + 1) * HD],
                                                   PT[:, n % 3, m * P:(m + 1) * P], VC[b][:, h * HD:(h + 1) * HD],
                                                   start=(n == 0 and m == 0), stop=True, skip_group_check=True)
                                mm.then_inc(g_pv_done, 1)
                        pe.wait_ge(g_added, c + 1)

            def gate_up(l, b, f):
                n = b * FT + f
                if f == 0:
                    pe.wait_ge(hx_set, l * B + b + 1)
                pe.wait_ge(wl_set, l * B * FT + n + 1)
                if n >= SBANKS:
                    pe.wait_ge(hid_set, l * B * FT + n - SBANKS + 1)
                S = psS[(GU_FIRST + n) % SBANKS]
                for w in range(2):
                    for k in range(KT):
                        m = w * KT + k
                        for j, (wp, hp) in enumerate(((w_high(n), HH), (w_low(n), HH),
                                                      (w_high(n), HL))):
                            mm = pe.matmul(S[:, w * L:(w + 1) * L], wp[:, m, :], hp[:, k, :],
                                           start=(k == 0 and j == 0), stop=(k == KT - 1 and j == 2))
                mm.then_inc(gu_full, 1)

            def down(l, b, tiles=range(QT)):
                if 0 in tiles:
                    pe.wait_ge(hid_set, l * B * FT + (b + 1) * FT - 1)
                    pe.wait_ge(wc_ld, l * 16 + 16)
                    if b == 0:
                        pe.wait_ge(or_copied, l * B + B)
                    else:
                        pe.wait_ge(y_free, l * B + 2)
                for f in range(FT):
                    if f == FT - 1 and 0 in tiles:
                        pe.wait_ge(hid_set, l * B * FT + (b + 1) * FT)
                    for t in tiles:
                        mm = pe.matmul(psO[:, t * D:(t + 1) * D], AT[b][:, f, t * P:(t + 1) * P], Wd[:, f, :],
                                       start=(f == 0 and t == 0), stop=(f == FT - 1), skip_group_check=True)
                if QT - 1 in tiles:
                    mm.then_inc(y_full, 1)

            def attention(l, nx):
                between = {
                    2: lambda: norm_T(l, 0, 1), 3: lambda: qkv(l, 1, 0), 4: lambda: qkv(l, 1, 1),
                    5: lambda: qkv(l, 1, 2), 7: lambda: rotated_T(l, 1, 0), 8: lambda: rotated_T(l, 1, 1),
                    S1 + 1: lambda: out_T(l, 0, "oT0", On[0], on_set, l * B + 1),
                    S1 + 2: lambda: out_proj(l, 0, "wo0", Wo, "oT0"),
                    S1 + 6: lambda: (norm_T(l, 1, 0), cross_kv(l, 0)), S1 + 7: lambda: cross_q(l, 0),
                    C0 + 1: lambda: out_T(l, 1, "oT1", On[1], on_set, l * B + 2),
                    C0 + 2: lambda: out_proj(l, 1, "wo1", Wo, "oT1"),
                    C0 + 4: lambda: norm_T(l, 1, 1), C0 + 5: lambda: cross_kv(l, 1), C0 + 6: lambda: cross_q(l, 1),
                    C1 + 2: lambda: out_T(l, 0, "coT0", On[0], con_set, l * B + 1),
                    C1 + 3: lambda: out_proj(l, 0, "cwo0", Woc, "coT0"), C1 + 5: lambda: norm_T(l, 2, 0),
                }
                for first, end in ((S0, C1), (C1, NG)):
                    scores(l, first)
                    scores(l, first + 1)
                    for i in range(first, end):
                        if i + 2 < end:
                            scores(l, i + 2)
                        between.get(i, lambda: None)()
                        probs_T(l, i)
                        if i == NG - 1:
                            gate_up(l, 0, 0)
                        if i > first:
                            pv(l, i - 1)
                    pv(l, end - 1)
                    further_blocks(l, int(first == C1), nx)

            def hidden_0(l):
                for f in range(FT):
                    if f:
                        gate_up(l, 0, f)
                    if f == 2:
                        out_T(l, 1, "coT1", On[1], con_set, l * B + 2)
                    if f == 3:
                        out_proj(l, 1, "cwo1", Woc, "coT1")
                    if f == 7:
                        norm_T(l, 2, 1)

            pe.wait_ge(c_ld, 16)
            norm_T(0, 0, 0)
            for part in range(3):
                qkv(0, 0, part)
            pe.wait_ge(consts_set, 2)
            for k in range(KT):
                rotated_T(0, 0, k)
            pe.wait_ge(nb_set, 1)
            nx = pe.value_load(NX[0:1, 0:1], min_val=0, max_val=NBLK - 1)
            with pe.Fori(0, NL - 1) as l:
                attention(l, nx)
                hidden_0(l)
                down(l, 0)
                for f in range(FT):
                    gate_up(l, 1, f)
                    if f == 4:
                        norm_T(l + 1, 0, 0)
                    if f == 5:
                        qkv(l + 1, 0, 0)
                        qkv(l + 1, 0, 1)
                qkv(l + 1, 0, 2)
                down(l, 1, [0])
                for k in range(KT):
                    rotated_T(l + 1, 0, k)
                down(l, 1, [1])
            attention(NL - 1, nx)
            hidden_0(NL - 1)

            def window_T(b):
                pe.wait_ge(an_set, b + 1)
                transposes(NL, f"an{b}", hs[:, 2 * b:2 * b + 2, :], b)

            def window_q(b):
                pe.wait_ge(wt_ld, 16)
                pe.wait_ge(*emptied(NL, f"an{b}"))
                for m in range(KT):
                    pe.wait_ge(*free_for(NL, f"wq{m}{b}"))
                    project(NL, f"wq{m}{b}", 0, lambda k: Wt[:, 0, k, m * P:(m + 1) * P],
                            lambda k: hT[b][:, k, :]).then_inc(full(f"wq{m}{b}"), 1)

            def window_kv(b):
                pe.wait_ge(*free_for(NL, f"wk{b}"))
                for m in range(KT):
                    mm = project(NL, f"wk{b}", m * L, lambda k: Wt[:, 1, k, m * P:(m + 1) * P], lambda k: hT[b][:, k, :])
                mm.then_inc(full(f"wk{b}"), 1)
                pe.wait_ge(*free_for(NL, f"wv{b}"))
                for t in range(QT):
                    mm = project(NL, f"wv{b}", t * D, lambda k: hT[b][:, k, t * P:(t + 1) * P], lambda k: Wt[:, 2, k, :])
                mm.then_inc(full(f"wv{b}"), 1)

            def window_scores(i):
                b, (blk, k, half) = i // NW, WINDOW[i % NW]
                if i % NW == 0:
                    pe.wait_ge(*emptied(NL, f"wk{b}"))
                    pe.wait_ge(*emptied(NL, f"wq0{b}"))
                if i % NW == 2:
                    pe.wait_ge(*emptied(NL, f"wq1{b}"))
                if i >= SBANKS:
                    pe.wait_ge(sig_set, i - SBANKS + 1)
                S = psS[i % SBANKS]
                if blk == "corner":
                    for k in range(KT):
                        mm = pe.matmul(S[:, k * P:(k + 1) * P].rearrange("p (h q) -> p h q", h=HT), kTs[b][:, k, 0:P],
                                       QM[b][:, k, :, P:P + HD], start=(k == 0), stop=True, skip_group_check=True)
                else:
                    mm = pe.matmul(S[:, :].rearrange("p (h q) -> p h q", h=4), kTs[b][:, k, blk * P:(blk + 1) * P],
                                   QM[b][:, k, 4 * half:4 * half + 4, blk * P:(blk + 1) * P], start=True, stop=True)
                mm.then_inc(ws_full, 1)

            def window_pv(i):
                b, (blk, k, half) = i // NW, WINDOW[i % NW]
                if i % NW == 0:
                    pe.wait_ge(*emptied(NL, f"wv{b}"))
                    if b:
                        pe.wait_ge(mo_set, b)
                    else:
                        pe.wait_ge(y_free, NL * B + 1)
                pe.wait_ge(tau_set, i + 1)
                T = PT[:, i % 3, :]
                if blk == "corner":
                    for h in range(H):
                        mm = pe.matmul(psO[0:HD, D + h * HD:D + (h + 1) * HD], T[:, h * HD:(h + 1) * HD],
                                       V[b][:, 0, h * HD:(h + 1) * HD], start=False, stop=True, skip_group_check=True)
                else:
                    for j in range(4):
                        h = k * HT + 4 * half + j
                        mm = pe.matmul(psO[:, blk * D + h * HD:blk * D + (h + 1) * HD], T[:, j * P:(j + 1) * P],
                                       V[b][:, blk, h * HD:(h + 1) * HD], start=(i % NW == 0 and j == 0), stop=True,
                                       skip_group_check=True)
                mm.then_inc(wpv_done, 1)

            def rounded_T(b):
                pe.wait_ge(xq_set, 2 * b + 2)
                pe.wait_ge(*free_for(NL, f"fn{b}"))
                for k in range(KT):
                    for t in range(QT):
                        mm = pe.transpose(bank(f"fn{b}")[:, :].bitcast(BF16)[:, k * L + t * P:k * L + (t + 1) * P],
                                          xq[:, 2 * b + t, k * P:(k + 1) * P], identB[:, :])
                mm.then_inc(full(f"fn{b}"), 1)

            def quantised_gate_up(t):
                if t == 0:
                    pe.wait_ge(tern_set, 2)
                if t % 2 == 0:
                    pe.wait_ge(*emptied(NL, f"fn{t // 2}"))
                for j in range(2):
                    for w, (ready, used) in enumerate(((qg_full, qg_free), (qu_full, qu_free))):
                        if t:
                            pe.wait_ge(used, 2 * t + j - 1)
                        Wx = WQ[w].rearrange("p (k n) -> p k n", k=KT)
                        for k in range(KT):
                            mm = pe.matmul(QB[j][w][:, :], xqT[t // 2][:, k, (t % 2) * P:(t % 2 + 1) * P],
                                           Wx[:, k, j * 512:(j + 1) * 512], start=(k == 0), stop=(k == KT - 1))
                        mm.then_inc(ready, 1)

            def quantised_down(t):
                pe.wait_ge(gq_set, t + 1)
                pe.wait_ge(*free_for(NL, f"gT{t}"))
                for f in range(FT):
                    mm = pe.transpose(bank(f"gT{t}")[:, :].bitcast(BF16)[:, f * P:(f + 1) * P],
                                      GQ(t)[:, f * P:(f + 1) * P], identB[:, :])
                mm.then_inc(full(f"gT{t}"), 1)
                pe.wait_ge(tern_set, 4)
                pe.wait_ge(*emptied(NL, f"gT{t}"))
                pe.wait_ge(*free_for(NL, f"d{t}"))
                for f in range(FT):
                    mm = pe.matmul(bank(f"d{t}")[:, 0:D], GQT(t)[:, f * P:(f + 1) * P],
                                   WQ[2][:, f * D:(f + 1) * D], start=(f == 0), stop=(f == FT - 1))
                mm.then_inc(full(f"d{t}"), 1)

            pe.wait_ge(asum_set, 3 * ABS_CHUNKS)
            pe.wait_ge(pool_set, 1)
            pe.wait_ge(*free_for(NL, "sum"))
            pe.matmul(bank("sum")[:, 0:3 * ABS_CHUNKS], ones[:, :], asum[:, :], start=True, stop=True)\
              .then_inc(full("sum"), 1)
            down(NL - 1, 0)
            for f in range(FT):
                gate_up(NL - 1, 1, f)
                if f == 6:
                    window_T(0)
            window_q(0)
            window_kv(0)
            down(NL - 1, 1)

            between = {4: lambda: window_T(1), 5: lambda: window_q(1), 6: lambda: window_kv(1),
                       NW + 1: lambda: out_T(NL, 0, "moT0", On[0], mo_set, 1),
                       NW + 2: lambda: out_proj(NL, 0, "mwo0", Wt[:, 3, :, :], "moT0"),
                       NW + 8: lambda: rounded_T(0)}
            window_scores(0)
            window_scores(1)
            for i in range(2 * NW):
                if i + 2 < 2 * NW:
                    window_scores(i + 2)
                between.get(i, lambda: None)()
                window_pv(i)

            quantised_gate_up(0)
            out_T(NL, 1, "moT1", On[1], mo_set, 2)
            out_proj(NL, 1, "mwo1", Wt[:, 3, :, :], "moT1")
            quantised_gate_up(1)
            rounded_T(1)
            quantised_gate_up(2)
            quantised_down(0)
            quantised_gate_up(3)
            for t in range(1, 4):
                quantised_down(t)

        @block.scalar
        def _(act):
            def squares(i, b, ready, value):
                act.wait_ge(ready, value)
                for t in range(QT):
                    a = nc.scalar.activation(hs[:, 2 * b + t, :], X[:, 2 * b + t, :], ACT.Square,
                                             accum_out=ss[:, i * B + b, t:t + 1])
                a.then_inc(ss_set, 1)

            def masked_q(src, b, k, heads_of=range(HT)):
                for h in heads_of:
                    a = nc.scalar.activation(QM[b][:, k, h, :], src, ACT.Copy, scale=headmask[:, h:h + 1])
                return a

            def self_qk(l, b, half):
                use = f"tq{b}1"
                if half == 0:
                    act.wait_ge(*filled(l, use))
                    nc.scalar.activation(kTs[b][:, 1, :], bank(use)[:, L:2 * L], ACT.Copy)
                    masked_q(bank(use)[:, 0:L], b, 1, range(HT // 2))
                else:
                    masked_q(bank(use)[:, 0:L], b, 1, range(HT // 2, HT)).then_inc(free(use), 1)

            def exp(l, i):
                cross, b, q, h0, nh, keys = GROUPS[i]
                nm, total = (nmR, lR) if cross else (nms, lS)
                act.wait_ge(s_max, l * NG + i + 1)
                if i >= 3:
                    act.wait_ge(t_full, l * NG + i - 2)
                for j in range(nh):
                    s = q * H + h0 + j
                    a = nc.scalar.activation(Pr[:, i % 3, j * keys:(j + 1) * keys],
                                             psS[i % SBANKS][:, j * keys:(j + 1) * keys], ACT.Exp,
                                             bias=nm[:, b, s:s + 1], accum_out=total[:, b, s:s + 1])
                a.then_inc(s_exp, 1)

            def copy_oT(l, b, use):
                act.wait_ge(*filled(l, use))
                a = nc.scalar.activation(oT[b][:, :, :].rearrange("p k n -> p (k n)"), bank(use)[:, :], ACT.Copy)
                a.then_inc(free(use), 1)

            def cross_qm(l, b, half):
                use = f"qc{b}1"
                if half == 0:
                    act.wait_ge(*filled(l, use))
                    masked_q(bank(use)[:, 0:L], b, 1, range(HT // 2))
                else:
                    masked_q(bank(use)[:, 0:L], b, 1, range(HT // 2, HT)).then_inc(free(use), 1)

            def cross_outputs(l, b):
                act.wait_ge(pv_done, l * NG + (C1 if b == 0 else NG))
                nc.scalar.activation(OR[b][:, :, :].rearrange("p t n -> p (t n)"), psO[:, :], ACT.Copy)\
                    .then_inc(or_copied, 1)

            def further_blocks(l, b, nx):
                with act.If(nx > 0):
                    with act.Fori(0, nx) as j:
                        c = act.snap((l * B + b) * nx + j)
                        for i, (q, h0, nh, keys) in enumerate(CROSS):
                            act.wait_ge(g_max, c * NCROSS + i + 1)
                            if i >= 3:
                                act.wait_ge(g_t_full, c * NCROSS + i - 2)
                            for m in range(nh):
                                s = q * H + h0 + m
                                a = nc.scalar.activation(Pr[:, i % 3, m * P:(m + 1) * P],
                                                         psS[i % 2][:, m * P:(m + 1) * P], ACT.Exp,
                                                         bias=nmN[:, b, s:s + 1], accum_out=lB[:, b, s:s + 1])
                            a.then_inc(g_exp, 1)
                        act.wait_ge(g_dm, c + 1)
                        nc.scalar.activation(al[:, b, :], dm[:, b, :], ACT.Exp).then_inc(g_al, 1)
                        act.wait_ge(g_added, c + 1)

            def split_high(l, n):
                if n == 0:
                    act.wait_ge(wc_ld, l * 16 + 16)
                if n >= RING:
                    act.wait_ge(gu_full, l * B * FT + n - RING + 1)
                f = n % FT
                nc.scalar.activation(w_high(n), WCt[:, :, f * P:(f + 1) * P], ACT.Copy).then_inc(wh_set, 1)

            def gate(l, b, f):
                n = b * FT + f
                act.wait_ge(gu_full, l * B * FT + n + 1)
                if n >= 2:
                    act.wait_ge(hid_set, l * B * FT + n - 1)
                nc.scalar.activation(SG[:, n % 2, :], psS[(GU_FIRST + n) % SBANKS][:, 0:L], ACT.Silu).then_inc(sg_set, 1)
                if n + RING < B * FT:
                    split_high(l, n + RING)

            def attention(l, nx, last=False):
                between = {
                    0: lambda: squares(0, 1, y_free, l * B + 1),
                    8: lambda: self_qk(l, 1, 0), 9: lambda: self_qk(l, 1, 1),
                    S1 + 1: lambda: copy_oT(l, 0, "oT0"), S1 + 3: lambda: squares(1, 0, *emptied(l, "wo0")),
                    S1 + 7: lambda: cross_qm(l, 0, 0), S1 + 8: lambda: cross_qm(l, 0, 1),
                    C0 + 1: lambda: copy_oT(l, 1, "oT1"), C0 + 3: lambda: squares(1, 1, *emptied(l, "wo1")),
                    C0 + 7: lambda: (cross_qm(l, 1, 0), cross_qm(l, 1, 1)),
                    C1: lambda: split_high(l, 0), C1 + 2: lambda: copy_oT(l, 0, "coT0"), C1 + 3: lambda: split_high(l, 1),
                    C1 + 4: lambda: squares(2, 0, *emptied(l, "cwo0")), C1 + 5: lambda: split_high(l, 2),
                }
                for first, end in ((S0, C1), (C1, NG)):
                    for i in range(first, end):
                        exp(l, i)
                        between.get(i, lambda: None)()
                        if last and i in ABS_AT:
                            sum_abs(ABS_AT.index(i))
                    b = int(first == C1)
                    cross_outputs(l, b)
                    further_blocks(l, b, nx)

            def sum_abs(n):
                if n == 0:
                    act.wait_ge(wf_ld, 16)
                else:
                    act.wait_ge(asum_set, n)
                w, at = n // ABS_CHUNKS, n % ABS_CHUNKS * 512
                nc.scalar.activation(SG[:, :, :].rearrange("p a n -> p (a n)"), WF[:, w, at:at + 512],
                                     ACT.Abs, accum_out=asum[:, n:n + 1]).then_inc(asum_set, 1)

            def hidden_0(l):
                for f in range(FT):
                    gate(l, 0, f)
                    if f == 2:
                        copy_oT(l, 1, "coT1")
                    if f == 3:
                        squares(2, 1, *emptied(l, "cwo1"))

            act.wait_ge(c_ld, 16)
            squares(0, 0, x_first, 1)
            act.wait_ge(x_first, 2)
            for half in range(2):
                self_qk(0, 0, half)
            act.wait_ge(nb_set, 1)
            nx = act.value_load(NX[0:1, 0:1], min_val=0, max_val=NBLK - 1)
            with act.Fori(0, NL - 1) as l:
                attention(l, nx)
                hidden_0(l)
                squares(0, 0, y_free, l * B + 2)
                for f in range(FT):
                    gate(l, 1, f)
                for half in range(2):
                    self_qk(l + 1, 0, half)
            attention(NL - 1, nx, last=True)
            hidden_0(NL - 1)

            def window_qm(b):
                act.wait_ge(*filled(NL, f"wq1{b}"))
                masked_q(bank(f"wq1{b}")[:, 0:L], b, 1).then_inc(free(f"wq1{b}"), 1)

            def window_v(b):
                act.wait_ge(*filled(NL, f"wv{b}"))
                nc.scalar.activation(V[b][:, :, :].rearrange("p t n -> p (t n)"), bank(f"wv{b}")[:, :], ACT.Copy)\
                  .then_inc(free(f"wv{b}"), 1)

            def ternary(n):
                w, at, size = (n, 0, 2048) if n < 2 else (2, (n - 2) * 1024, 1024)
                act.wait_ge(tern_step, w + 1)
                if n == 0:
                    act.wait_ge(*filled(NL - 1, "cwo1"))
                if n == 2:
                    act.wait_ge(y_full, NL * B)
                nc.scalar.activation(WQ[w][:, at:at + size], WF[:, w, at:at + size], ACT.Sign, bias=negmagic[:, :])\
                  .then_inc(tern_set, 1)

            def quantised_gates(t):
                act.wait_ge(sgu_set, t // 2 * 2 + 2)
                for j in range(2):
                    act.wait_ge(qg_full, 2 * t + j + 1)
                    nc.scalar.activation(GR(t)[:, j * 512:(j + 1) * 512], QB[j][0][:, :], ACT.Silu,
                                         scale=sgu[:, t, 0:1]).then_inc(qg_free, 1)

            def scale_hidden(t):
                act.wait_ge(gq_scale_set, t + 1)
                nc.scalar.activation(GU(t), GU(t), ACT.Copy, scale=am2[:, t, 2:3], bias=MAGIC).then_inc(gq_scaled, 1)

            def unbias_hidden(t):
                act.wait_ge(gq_clamped, t + 1)
                nc.scalar.activation(GQ(t), GU(t), ACT.Copy, bias=-MAGIC).then_inc(gq_set, 1)

            def copy_hidden_T(t):
                act.wait_ge(*filled(NL, f"gT{t}"))
                nc.scalar.activation(GQT(t), bank(f"gT{t}")[:, :].bitcast(BF16), ACT.Copy).then_inc(free(f"gT{t}"), 1)

            squares(0, 0, y_free, (NL - 1) * B + 2)
            for f in range(FT):
                gate(NL - 1, 1, f)
                if f in (3, 5):
                    ternary((f - 3) // 2)
            window_qm(0)
            window_v(0)
            between = {0: lambda: squares(0, 1, y_free, NL * B + 1), 2: lambda: ternary(2), 3: lambda: ternary(3),
                       5: lambda: window_qm(1), 6: lambda: window_v(1), NW + 1: lambda: copy_oT(NL, 0, "moT0")}
            for i in range(2 * NW):
                n = 2 * P if WINDOW[i % NW][0] == "corner" else 512
                act.wait_ge(ws_full, i + 1)
                if i >= 3:
                    act.wait_ge(tau_set, i - 2)
                nc.scalar.activation(Pr[:, i % 3, 0:n], psS[i % SBANKS][:, 0:n], ACT.Sigmoid).then_inc(sig_set, 1)
                between.get(i, lambda: None)()
            quantised_gates(0)
            copy_oT(NL, 1, "moT1")
            quantised_gates(1)
            scale_hidden(0)
            unbias_hidden(0)
            scale_hidden(1)
            copy_hidden_T(0)
            quantised_gates(2)
            unbias_hidden(1)
            copy_hidden_T(1)
            quantised_gates(3)
            for t in range(2, 4):
                scale_hidden(t)
                unbias_hidden(t)
                copy_hidden_T(t)

        @block.vector
        def _(dve):
            steps = [0]

            def done(ins):
                steps[0] += 1
                ins.then_inc(v_step, 1)
                dve.wait_ge(v_step, steps[0])

            def mean_square(l, i, b):
                dve.wait_ge(ss_set, l * NORMS + i * B + b + 1)
                dve.tensor_scalar(ms[:, i * B + b, :], ss[:, i * B + b, :], 1.0 / D, RMS_EPS, ALU.mult, ALU.add)\
                   .then_inc(ms_set, 1)

            def normalise(l, i, b):
                dve.wait_ge(rstd_set, l * NORMS + i * B + b + 1)
                for t in range(QT):
                    v = dve.tensor_scalar(hs[:, 2 * b + t, :], X[:, 2 * b + t, :], rstd[:, i * B + b, t:t + 1], None,
                                          ALU.mult)
                v.then_inc(h_set, 1)

            def weigh_T(l, i, b):
                use = f"n{i}{b}"
                dve.wait_ge(nrm_ld, l * 16 + 16)
                dve.wait_ge(*filled(l, use))
                for k in range(KT):
                    v = dve.tensor_scalar(hT[b][:, k, :], bank(use)[:, k * L:(k + 1) * L],
                                          nrm[:, i * KT + k:i * KT + k + 1], None, ALU.mult)
                v.then_inc(free(use), 1)

            def biased_qkv(l, b, part):
                if part == 0:
                    dve.wait_ge(bias_ld, l * 16 + 16)
                if part < QT:
                    use = f"qk{b}{part}"
                    dve.wait_ge(*filled(l, use))
                    v = dve.tensor_tensor(QK[b][:, part, :], bank(use)[:, :], bias[:, 0:2 * D], ALU.add)
                else:
                    use = f"v{b}"
                    dve.wait_ge(*filled(l, use))
                    v = dve.tensor_tensor(V[b][:, :, :], tiles(bank(use)[:, :]),
                                          bias[:, 2 * D:3 * D].unsqueeze(1).broadcast_to([P, QT, D]), ALU.add)
                v.then_inc(free(use), 1)

            def cosines(l, b):
                for t in range(QT):
                    dve.wait_ge(*emptied(l, f"qk{b}{t}"))
                dve.tensor_tensor(QR[b][:, :, :].rearrange("p t (h d) -> p t h d", d=HD),
                                  QK[b][:, :, :].rearrange("p t (h d) -> p t h d", d=HD),
                                  cos.unsqueeze(2).broadcast_to([P, QT, 2 * H, HD]), ALU.mult).then_inc(cos_set, 1)

            def add_sines(l, b):
                dve.wait_ge(cos_set, l * B + b + 1)
                dve.wait_ge(sin_set, l * B + b + 1)
                dve.tensor_tensor(QR[b][:, :, :], QR[b][:, :, :], RT[:, :, :], ALU.add).then_inc(qr_set, 1)

            def masked_q(src, b, n=HT, h0=0):
                return dve.tensor_tensor(QM[b][:, 0, h0:h0 + n, :], src.unsqueeze(1).broadcast_to([P, n, L]),
                                         headmask[:, h0:h0 + n].unsqueeze(2).broadcast_to([P, n, L]), ALU.mult)

            def self_qk(l, b, half):
                use = f"tq{b}0"
                if half == 0:
                    dve.wait_ge(*filled(l, use))
                    dve.tensor_copy(kTs[b][:, 0, :], bank(use)[:, L:2 * L])
                    masked_q(bank(use)[:, 0:L], b, HT // 2)
                else:
                    masked_q(bank(use)[:, 0:L], b, HT // 2, HT // 2).then_inc(free(use), 1)

            def max_(l, i):
                cross, b, q, h0, nh, keys = GROUPS[i]
                s = q * H + h0
                dve.wait_ge(s_full, l * NG + i + 1)
                dve.tensor_reduce((nmR if cross else nms)[:, b, s:s + nh],
                                  psS[i % SBANKS][:, :].rearrange("p (h k) -> p h k", h=nh),
                                  AX_X, ALU.max, negate=True).then_inc(s_max, 1)

            def copy_T(l, i):
                dve.wait_ge(t_full, l * NG + i + 1)
                if i >= 3:
                    dve.wait_ge(pv_done, l * NG + i - 2)
                dve.tensor_copy(PT[:, i % 3, :], psP[i % PBANKS][:, :]).then_inc(t_copied, 1)

            def divide(src, denominator, b, step_set, step_value, out_set):
                dve.reciprocal(rl[:, b, :], denominator).then_inc(step_set, 1)
                dve.wait_ge(step_set, step_value)
                dve.tensor_tensor(heads(On[b][:, :, :]), src,
                                  rl[:, b, :].unsqueeze(2).broadcast_to([P, QT * H, HD]), ALU.mult).then_inc(out_set, 1)

            def self_out(l, b):
                dve.wait_ge(pv_done, l * NG + (b + 1) * NSELF)
                divide(psO[:, :].rearrange("p (h d) -> p h d", d=HD), lS[:, b, :], b, rl_set, l * B + b + 1, on_set)

            def residual(l, b, use):
                dve.wait_ge(*filled(l, use))
                x = X[:, 2 * b:2 * b + 2, :]
                v = dve.tensor_tensor(x, x, tiles(bank(use)[:, :]), ALU.add)
                v.then_inc(free(use), 1)

            def down_residual(l, b):
                dve.wait_ge(y_full, l * B + b + 1)
                x = X[:, 2 * b:2 * b + 2, :]
                dve.tensor_tensor(x, x, tiles(psO[:, :]), ALU.add).then_inc(y_free, 1)

            def cross_qm(l, b, half):
                use = f"qc{b}0"
                if half == 0:
                    dve.wait_ge(*filled(l, use))
                    masked_q(bank(use)[:, 0:L], b, HT // 2)
                else:
                    masked_q(bank(use)[:, 0:L], b, HT // 2, HT // 2).then_inc(free(use), 1)

            def cross_kv(l, b):
                use = f"kv{b}"
                dve.wait_ge(*filled(l, use))
                dve.tensor_copy(KV[b][:, :], bank(use)[:, :]).then_inc(free(use), 1)

            def cross_out(l, b):
                dve.wait_ge(or_copied, l * B + b + 1)
                divide(heads(OR[b][:, :, :]), lR[:, b, :], b, crl_set, l * B + b + 1, con_set)

            def compare(t0, n, low, high):
                for t in range(t0, t0 + n):
                    dve.tensor_scalar(mA[:, t - t0, :], iota, high[:, t:t + 1], NEG, ALU.is_gt, ALU.mult)
                    v = dve.tensor_scalar(mB[:, t - t0, :], iota, low[:, t:t + 1], NEG, ALU.is_le, ALU.mult)
                return v

            def further_blocks(l, b, nx):
                with dve.If(nx > 0):
                    with dve.Fori(0, nx) as j:
                        c = dve.snap((l * B + b) * nx + j)
                        dve.wait_ge(g_rel, 2 * (c + l * B + b) + 2)
                        compare(2 * b, QT, segL, segR).then_inc(g_cmp, 1)
                        dve.wait_ge(g_cmp, c + 1)
                        dve.tensor_tensor(maskG[:, :, :], mA[:, 0:QT, :], mB[:, 0:QT, :], ALU.add).then_inc(g_mask, 1)
                        dve.wait_ge(g_kv_full, c + 2)
                        dve.tensor_copy(KV[b][:, :], bank(KV_BANK[b])[:, :]).then_inc(g_kv_set, 1)
                        for i in range(NCROSS + 1):
                            if i < NCROSS:
                                q, h0, nh, keys = CROSS[i]
                                s = q * H + h0
                                dve.wait_ge(g_s_full, c * NCROSS + i + 1)
                                dve.tensor_reduce(nmB[:, b, s:s + 4], psS[i % 2][:, :].rearrange("p (h k) -> p h k", h=4),
                                                  AX_X, ALU.max, negate=True).then_inc(g_bmax, 1)
                                dve.wait_ge(g_bmax, c * NCROSS + i + 1)
                                dve.tensor_tensor(nmN[:, b, s:s + 4], nmR[:, b, s:s + 4], nmB[:, b, s:s + 4], ALU.min)\
                                   .then_inc(g_max, 1)
                            if i >= 1:
                                n = i - 1
                                dve.wait_ge(g_t_full, c * NCROSS + n + 1)
                                if n >= 3:
                                    dve.wait_ge(g_pv_done, c * NCROSS + n - 2)
                                dve.tensor_copy(PT[:, n % 3, :], psP[n % 2][:, :]).then_inc(g_t_copied, 1)
                        dve.wait_ge(g_pv_done, (c + 1) * NCROSS)
                        dve.wait_ge(g_scaled, c + 1)
                        o = OR[b][:, :, :].rearrange("p t n -> p (t n)")
                        dve.tensor_tensor(o, o, psO[:, :], ALU.add).then_inc(g_added, 1)
                        dve.wait_ge(g_added, c + 1)

            def split_low(l, n):
                f = n % FT
                dve.wait_ge(wh_set, l * B * FT + n + 1)
                dve.tensor_tensor(w_low(n), WCt[:, :, f * P:(f + 1) * P], w_high(n), ALU.subtract).then_inc(wl_set, 1)

            def split_tokens(l, b):
                dve.wait_ge(*emptied(l, f"n2{b}"))
                if b:
                    dve.wait_ge(gu_full, l * B * FT + FT)
                dve.tensor_copy(HH[:, :, :], hT[b][:, :, :]).then_inc(hh_set, 1)
                dve.wait_ge(hh_set, l * B + b + 1)
                dve.tensor_tensor(HL[:, :, :], hT[b][:, :, :], HH[:, :, :], ALU.subtract).then_inc(hx_set, 1)

            def hidden(l, b, f):
                n = b * FT + f
                dve.wait_ge(sg_set, l * B * FT + n + 1)
                dve.tensor_tensor(AT[b][:, f, :], SG[:, n % 2, :], psS[(GU_FIRST + n) % SBANKS][:, L:2 * L], ALU.mult)\
                   .then_inc(hid_set, 1)
                if n + RING < B * FT:
                    split_low(l, n + RING)

            def layernorm_stats(n, b, src):
                for t in range(QT):
                    v = dve.bn_stats(bst[:, n, t, :], src[:, 2 * b + t, :])
                done(v)
                for t in range(QT):
                    v = dve.bn_aggr(mv[:, n, t, :], bst[:, n, t, :])
                done(v)
                dve.tensor_scalar(lve[:, n, :], mv[:, n, :, 1], LN_EPS, None, ALU.add).then_inc(ln_var, 1)

            def layernorm_apply(n, b, src, dst, last):
                dve.wait_ge(ln_rstd, n + 1)
                for t in range(QT):
                    v = dve.tensor_scalar(dst[:, 2 * b + t, :], src[:, 2 * b + t, :], mv[:, n, t, 0:1],
                                          lrs[:, n, t:t + 1], ALU.subtract, ALU.mult)
                last(v)

            def layernorm(n, b, src, dst, last):
                layernorm_stats(n, b, src)
                layernorm_apply(n, b, src, dst, last)

            def quantise_scales(t, n, src, which):
                a = (am, am2)[which]
                done(dve.tensor_reduce(a[:, t:t + n, 0], src, AX_X, ALU.max, apply_absolute_value=True))
                done(dve.tensor_scalar(a[:, t:t + n, 3], a[:, t:t + n, 0], 1e-5, 1.0 / 127.0, ALU.max, ALU.mult))
                done(dve.reciprocal(a[:, t:t + n, 2], a[:, t:t + n, 3]))

            def round_tile(src, t, which, dst, done_set):
                a = (am, am2)[which]
                done(dve.tensor_scalar(src, src, a[:, t, 2:3], MAGIC, ALU.mult, ALU.add))
                done(dve.tensor_scalar(src, src, MAGIC, 127.0, ALU.subtract, ALU.min))
                dve.tensor_scalar(dst, src, -128.0, None, ALU.max).then_inc(done_set, 1)

            def attention(l, nx):
                between = {
                    0: lambda: mean_square(l, 0, 1), 1: lambda: normalise(l, 0, 1), 2: lambda: weigh_T(l, 0, 1),
                    3: lambda: biased_qkv(l, 1, 0), 4: lambda: (biased_qkv(l, 1, 1), cosines(l, 1)),
                    5: lambda: (biased_qkv(l, 1, 2), add_sines(l, 1)),
                    7: lambda: self_qk(l, 1, 0), 8: lambda: self_qk(l, 1, 1),
                    S1: lambda: self_out(l, 0),
                    S1 + 2: lambda: (dve.wait_ge(xbo_set, l * B + 1), residual(l, 0, "wo0")),
                    S1 + 4: lambda: mean_square(l, 1, 0), S1 + 5: lambda: normalise(l, 1, 0),
                    S1 + 6: lambda: (weigh_T(l, 1, 0), cross_kv(l, 0)),
                    S1 + 7: lambda: cross_qm(l, 0, 0), S1 + 8: lambda: cross_qm(l, 0, 1),
                    C0: lambda: self_out(l, 1),
                    C0 + 2: lambda: (dve.wait_ge(xbo_set, l * B + 2), residual(l, 1, "wo1")),
                    C0 + 3: lambda: (mean_square(l, 1, 1), normalise(l, 1, 1)),
                    C0 + 4: lambda: weigh_T(l, 1, 1), C0 + 5: lambda: cross_kv(l, 1),
                    C0 + 6: lambda: cross_qm(l, 1, 0), C0 + 7: lambda: cross_qm(l, 1, 1),
                    C1: lambda: cross_out(l, 0), C1 + 1: lambda: split_low(l, 0),
                    C1 + 3: lambda: (residual(l, 0, "cwo0"), split_low(l, 1)),
                    C1 + 4: lambda: (mean_square(l, 2, 0), normalise(l, 2, 0)),
                    C1 + 5: lambda: (weigh_T(l, 2, 0), split_tokens(l, 0)), C1 + 6: lambda: split_low(l, 2),
                }
                for first, end in ((S0, C1), (C1, NG)):
                    max_(l, first)
                    max_(l, first + 1)
                    for i in range(first, end):
                        if i + 2 < end:
                            max_(l, i + 2)
                        copy_T(l, i)
                        between.get(i, lambda: None)()
                    further_blocks(l, int(first == C1), nx)

            def hidden_0(l):
                for f in range(FT):
                    if f == 0:
                        cross_out(l, 1)
                    hidden(l, 0, f)
                    if f == 3:
                        residual(l, 1, "cwo1")
                    if f == 4:
                        mean_square(l, 2, 1)
                        normalise(l, 2, 1)
                    if f == 7:
                        weigh_T(l, 2, 1)
                split_tokens(l, 1)

            dve.sem_inc(d_free[0], 1)
            dve.sem_inc(d_free[1], 1)
            dve.sem_inc(y_free, 1)
            dve.sem_inc(g_kv_full, 1)
            dve.wait_ge(x_ld, 16)
            layernorm(0, 0, X0, X, lambda v: v.then_inc(x_first, 1))
            mean_square(0, 0, 0)
            normalise(0, 0, 0)
            layernorm_stats(1, 1, X0)
            weigh_T(0, 0, 0)
            layernorm_apply(1, 1, X0, X, lambda v: v.then_inc(x_first, 1))
            dve.wait_ge(seg_ld, 32)
            done(dve.tensor_copy(rowF[:, :], rowI[:, :]))
            dve.tensor_reduce(few[:, 1:2], rowF[:, :], AX_X, ALU.min)
            done(dve.tensor_reduce(few[:, 0:1], rowF[:, :], AX_X, ALU.max))
            dve.tensor_scalar(few[:, 3:4], few[:, 1:2], 0.0, float(NBLK - 1), ALU.is_lt, ALU.mult)
            done(dve.tensor_scalar(cnt[:, :], iota[0:1, 1:NBLK], float(P), None, ALU.mult))
            done(dve.tensor_scalar(cnt[:, :], cnt[:, :], few[:, 0:1], None, ALU.is_le))
            done(dve.tensor_reduce(few[:, 2:3], cnt[:, :], AX_X, ALU.add))
            dve.tensor_tensor(NX[:, :], few[:, 2:3], few[:, 3:4], ALU.max).then_inc(nb_set, 1)
            dve.tensor_copy(segF[:, :], segI[:, :]).then_inc(consts_set, 1)
            dve.tensor_copy(identB[:, :], ident)
            dve.tensor_copy(causB[:, :], const[:, C_CAUSAL:C_CAUSAL + P]).then_inc(consts_set, 1)
            dve.wait_ge(consts_set, 2)
            done(dve.tensor_scalar(segL[:, :], segF[:, :], float(LOOKBACK), None, ALU.subtract))
            biased_qkv(0, 0, 0)
            biased_qkv(0, 0, 1)
            cosines(0, 0)
            biased_qkv(0, 0, 2)
            add_sines(0, 0)
            for half in range(2):
                self_qk(0, 0, half)
            dve.wait_ge(*filled(0, "tq01"))
            compare(0, 4, segL, segF).then_inc(mask_cmp, 1)
            dve.wait_ge(mask_cmp, 1)
            dve.tensor_tensor(maskB[:, :, :], mA[:, :, :], mB[:, :, :], ALU.add).then_inc(mask_set, 1)

            dve.wait_ge(nb_set, 1)
            nx = dve.value_load(NX[0:1, 0:1], min_val=0, max_val=NBLK - 1)
            with dve.Fori(0, NL - 1) as l:
                attention(l, nx)
                hidden_0(l)
                down_residual(l, 0)
                hidden(l, 1, 0)
                hidden(l, 1, 1)
                mean_square(l + 1, 0, 0)
                hidden(l, 1, 2)
                normalise(l + 1, 0, 0)
                hidden(l, 1, 3)
                weigh_T(l + 1, 0, 0)
                hidden(l, 1, 4)
                hidden(l, 1, 5)
                biased_qkv(l + 1, 0, 0)
                biased_qkv(l + 1, 0, 1)
                hidden(l, 1, 6)
                cosines(l + 1, 0)
                hidden(l, 1, 7)
                biased_qkv(l + 1, 0, 2)
                add_sines(l + 1, 0)
                for half in range(2):
                    self_qk(l + 1, 0, half)
                down_residual(l, 1)
            attention(NL - 1, nx)
            hidden_0(NL - 1)

            def final_norm(b):
                dve.wait_ge(rstd_set, NL * NORMS + b + 1)
                for t in range(QT):
                    v = dve.scalar_tensor_tensor(hs[:, 2 * b + t, :], X[:, 2 * b + t, :], rstd[:, b, t:t + 1],
                                                 vec[:, 0:D], ALU.mult, ALU.mult)
                done(v)
                x = X0[:, 2 * b:2 * b + 2, :]
                done(dve.tensor_tensor(x, x, hs[:, 2 * b:2 * b + 2, :], ALU.add))

            def window_T(b):
                dve.wait_ge(*filled(NL, f"an{b}"))
                dve.tensor_copy(hT[b][:, :, :].rearrange("p k n -> p (k n)"), bank(f"an{b}")[:, :])\
                   .then_inc(free(f"an{b}"), 1)

            def window_qm(b):
                dve.wait_ge(*filled(NL, f"wq0{b}"))
                masked_q(bank(f"wq0{b}")[:, 0:L], b).then_inc(free(f"wq0{b}"), 1)

            def window_k(b):
                dve.wait_ge(*filled(NL, f"wk{b}"))
                dve.tensor_copy(kTs[b][:, :, :].rearrange("p k n -> p (k n)"), bank(f"wk{b}")[:, :])\
                   .then_inc(free(f"wk{b}"), 1)

            def window_out(b):
                dve.wait_ge(wpv_done, (b + 1) * NW)
                dve.tensor_copy(On[b][:, :, :].rearrange("p t n -> p (t n)"), psO[:, :]).then_inc(mo_set, 1)

            def window_stats(b):
                dve.wait_ge(*filled(NL, f"mwo{b}"))
                dve.tensor_tensor(X[:, 2 * b:2 * b + 2, :], hs[:, 2 * b:2 * b + 2, :], tiles(bank(f"mwo{b}")[:, :]), ALU.add)\
                   .then_inc(free(f"mwo{b}"), 1)
                dve.wait_ge(*emptied(NL, f"mwo{b}"))
                layernorm_stats(4 + 2 * b, b, X)

            def add_beta(b):
                x = X0[:, 2 * b:2 * b + 2, :]
                dve.tensor_tensor(x, x, vec[:, 2 * D:3 * D].unsqueeze(1).broadcast_to([P, QT, D]), ALU.add)

            def window_residual(n, b):
                for t in range(QT):
                    v = dve.scalar_tensor_tensor(hs[:, 2 * b + t, :], X[:, 2 * b + t, :], mv[:, n, t, 0:1],
                                                 vec[:, D:2 * D], ALU.subtract, ALU.mult)
                done(v)
                dve.wait_ge(ln_rstd, n + 1)
                for t in range(QT):
                    v = dve.scalar_tensor_tensor(X0[:, 2 * b + t, :], hs[:, 2 * b + t, :], lrs[:, n, t:t + 1],
                                                 X0[:, 2 * b + t, :], ALU.mult, ALU.add)
                done(v)

            def round_tokens(b):
                quantise_scales(b * 2, 2, hs[:, 2 * b:2 * b + 2, :], 0)
                for w in range(2):
                    dve.tensor_scalar(sgu[:, 2 * b:2 * b + 2, w], am[:, 2 * b:2 * b + 2, 3], mw[:, w:w + 1], None, ALU.mult)\
                       .then_inc(sgu_set, 1)
                ts = (2 * b, 2 * b + 1)
                for t in ts:
                    v = dve.tensor_scalar(hs[:, t, :], hs[:, t, :], am[:, t, 2:3], MAGIC, ALU.mult, ALU.add)
                done(v)
                for t in ts:
                    v = dve.tensor_scalar(hs[:, t, :], hs[:, t, :], MAGIC, 127.0, ALU.subtract, ALU.min)
                done(v)
                for t in ts:
                    dve.tensor_scalar(xq[:, t, :], hs[:, t, :], -128.0, None, ALU.max).then_inc(xq_set, 1)

            def rounded_T(b):
                dve.wait_ge(*filled(NL, f"fn{b}"))
                dve.tensor_copy(xqT[b][:, :, :].rearrange("p k n -> p (k n)"),
                                bank(f"fn{b}")[:, :].bitcast(BF16)[:, 0:KT * L]).then_inc(free(f"fn{b}"), 1)

            def quantised_hidden(t):
                dve.wait_ge(sgu_set, t // 2 * 2 + 2)
                for j in range(2):
                    dve.wait_ge(qu_full, 2 * t + j + 1)
                    dve.wait_ge(qg_free, 2 * t + j + 1)
                    dve.scalar_tensor_tensor(GU(t)[:, j * 512:(j + 1) * 512], QB[j][1][:, :],
                                             sgu[:, t, 1:2], GR(t)[:, j * 512:(j + 1) * 512], ALU.mult, ALU.mult)\
                       .then_inc(qu_free, 1)

            def hidden_scales(t):
                dve.wait_ge(qu_free, 2 * t + 2)
                quantise_scales(t, 1, GU(t).unsqueeze(1), 1)
                dve.tensor_scalar(sgu[:, t, 2:3], am2[:, t, 3:4], mw[:, 2:3], None, ALU.mult).then_inc(gq_scale_set, 1)

            def clamp_hidden(t):
                dve.wait_ge(gq_scaled, t + 1)
                dve.tensor_scalar(GU(t), GU(t), MAGIC + 127.0, MAGIC - 128.0, ALU.min, ALU.max).then_inc(gq_clamped, 1)

            def output(t):
                dve.wait_ge(gq_scale_set, t + 1)
                dve.wait_ge(*filled(NL, f"d{t}"))
                dve.scalar_tensor_tensor(X[:, t, :], bank(f"d{t}")[:, 0:D], sgu[:, t, 2:3], X0[:, t, :],
                                         ALU.mult, ALU.add).then_inc(free(f"d{t}"), 1)

            dve.wait_ge(*filled(NL, "sum"))
            dve.tensor_reduce(awsum[:, :], bank("sum")[:, 0:3 * ABS_CHUNKS].rearrange("p (w c) -> p w c", w=3), AX_X,
                              ALU.add).then_inc(free("sum"), 1)
            dve.wait_ge(*emptied(NL, "sum"))
            done(dve.tensor_scalar(mw[:, :], awsum[:, :], 1.0 / (F * D), 1e-5, ALU.mult, ALU.max))
            dve.reciprocal(rw[:, :], mw[:, :]).then_inc(mw_set, 1)
            dve.wait_ge(vec_ld, 16)
            down_residual(NL - 1, 0)
            between = {1: lambda: mean_square(NL, 0, 0), 2: lambda: final_norm(0),
                       3: lambda: layernorm(2, 0, X0, hs, lambda v: v.then_inc(an_set, 1)), 6: lambda: window_T(0)}
            for f in range(FT):
                hidden(NL - 1, 1, f)
                between.get(f, lambda: None)()
            window_qm(0)
            window_k(0)
            add_beta(0)
            down_residual(NL - 1, 1)

            mean_square(NL, 0, 1)
            final_norm(1)
            layernorm(3, 1, X0, hs, lambda v: v.then_inc(an_set, 1))
            window_T(1)
            window_qm(1)
            window_k(1)
            add_beta(1)
            window_out(0)
            window_stats(0)
            window_residual(4, 0)
            layernorm(5, 0, X0, hs, done)
            round_tokens(0)
            rounded_T(0)
            window_out(1)
            quantised_hidden(0)
            window_stats(1)
            window_residual(6, 1)
            layernorm_stats(7, 1, X0)
            hidden_scales(0)
            layernorm_apply(7, 1, X0, hs, done)
            round_tokens(1)
            quantised_hidden(1)
            clamp_hidden(0)
            rounded_T(1)
            hidden_scales(1)
            clamp_hidden(1)
            quantised_hidden(2)
            output(0)
            hidden_scales(2)
            quantised_hidden(3)
            clamp_hidden(2)
            hidden_scales(3)
            output(1)
            clamp_hidden(3)
            output(2)
            output(3)

        @block.gpsimd
        def _(pool):
            pool.memset(mhalf[:, :], -0.5)
            pool.memset(negmagic[:, :], -MAGIC)
            pool.memset(step[:, :], float(P))
            pool.memset(look[:, :], float(LOOKBACK))
            pool.memset(ones[:, :], 1.0).then_inc(pool_set, 1)

            def rsqrt(l, i, b):
                pool.wait_ge(ms_set, l * NORMS + i * B + b + 1)
                nc.gpsimd.tensor_tensor(rstd[:, i * B + b, :], ms[:, i * B + b, :], mhalf[:, :], ALU.pow)\
                    .then_inc(rstd_set, 1)

            def ln_rsqrt(n):
                pool.wait_ge(ln_var, n + 1)
                nc.gpsimd.tensor_tensor(lrs[:, n, :], lve[:, n, :], mhalf[:, :], ALU.pow).then_inc(ln_rstd, 1)

            def sines(l, b, first=False):
                for t in range(QT):
                    pool.wait_ge(*emptied(l, f"qk{b}{t}"))
                if not first:
                    pool.wait_ge(qr_set, l * B + b)
                    if b == 0:
                        pool.wait_ge(*filled(l - 1, "coT1"))
                q = QK[b][:, :, :].rearrange("p t (h d) -> p t h d", d=HD)
                r = RT[:, :, :].rearrange("p t (h d) -> p t h d", d=HD)
                for to, of in ((0, HD // 2), (HD // 2, 0)):
                    g = nc.gpsimd.tensor_tensor(r[:, :, :, to:to + HD // 2], q[:, :, :, of:of + HD // 2],
                                                sin[:, :, to:to + HD // 2].unsqueeze(2)
                                                .broadcast_to([P, QT, 2 * H, HD // 2]), ALU.mult)
                g.then_inc(sin_set, 1)

            def add_bo(l, b):
                pool.wait_ge(h_set, l * NORMS + b + 1)
                pool.wait_ge(bias_ld, l * 16 + 16)
                x = X[:, 2 * b:2 * b + 2, :]
                nc.gpsimd.tensor_tensor(x, x, bias[:, 3 * D:4 * D].unsqueeze(1).broadcast_to([P, QT, D]), ALU.add)\
                    .then_inc(xbo_set, 1)

            def further_blocks(l, b, nx):
                with pool.If(nx > 0):
                    nc.gpsimd.tensor_tensor(segR[:, :], segF[:, :], step[:, :], ALU.subtract).then_inc(g_rel, 1)
                    pool.wait_ge(g_rel, 2 * (l * B + b) * (nx + 1) + 1)
                    nc.gpsimd.tensor_tensor(segL[:, :], segR[:, :], look[:, :], ALU.subtract).then_inc(g_rel, 1)
                    with pool.Fori(0, nx) as j:
                        c = pool.snap((l * B + b) * nx + j)
                        pool.wait_ge(g_mask, c + 1)
                        nc.gpsimd.tensor_tensor(segR[:, :], segR[:, :], step[:, :], ALU.subtract).then_inc(g_rel, 1)
                        nc.gpsimd.tensor_tensor(segL[:, :], segL[:, :], step[:, :], ALU.subtract).then_inc(g_rel, 1)
                        pool.wait_ge(or_copied, l * B + b + 1)
                        pool.wait_ge(g_max, (c + 1) * NCROSS)
                        nc.gpsimd.tensor_tensor(dm[:, b, :], nmN[:, b, :], nmR[:, b, :], ALU.subtract).then_inc(g_dm, 1)
                        pool.wait_ge(g_dm, c + 1)
                        nc.gpsimd.tensor_tensor(nmR[:, b, :], nmN[:, b, :], ones[:, 0:QT * H], ALU.mult).then_inc(g_nmr, 1)
                        pool.wait_ge(g_al, c + 1)
                        nc.gpsimd.tensor_tensor(lR[:, b, :], lR[:, b, :], al[:, b, :], ALU.mult).then_inc(g_lr, 1)
                        pool.wait_ge(g_lr, c + 1)
                        pool.wait_ge(g_exp, (c + 1) * NCROSS)
                        nc.gpsimd.tensor_tensor(lR[:, b, :], lR[:, b, :], lB[:, b, :], ALU.add)
                        nc.gpsimd.tensor_tensor(heads(OR[b][:, :, :]), heads(OR[b][:, :, :]),
                                                al[:, b, :].unsqueeze(2).broadcast_to([P, QT * H, HD]), ALU.mult)\
                            .then_inc(g_scaled, 1)
                        pool.wait_ge(g_added, c + 1)

            def attention(l, nx):
                rsqrt(l, 0, 1)
                add_bo(l, 1)
                sines(l, 1)
                rsqrt(l, 1, 0)
                rsqrt(l, 1, 1)
                further_blocks(l, 0, nx)
                rsqrt(l, 2, 0)
                further_blocks(l, 1, nx)
                rsqrt(l, 2, 1)

            pool.wait_ge(pool_set, 1)
            ln_rsqrt(0)
            rsqrt(0, 0, 0)
            pool.wait_ge(c_ld, 16)
            ln_rsqrt(1)
            add_bo(0, 0)
            sines(0, 0, first=True)
            pool.wait_ge(nb_set, 1)
            nx = pool.value_load(NX[0:1, 0:1], min_val=0, max_val=NBLK - 1)
            pool.wait_ge(consts_set, 2)
            with pool.Fori(0, NL - 1) as l:
                attention(l, nx)
                rsqrt(l + 1, 0, 0)
                add_bo(l + 1, 0)
                sines(l + 1, 0)
            attention(NL - 1, nx)

            pool.wait_ge(wf_ld, 16)
            pool.wait_ge(mw_set, 1)
            nc.gpsimd.tensor_scalar(WF[:, 0, :], WF[:, 0, :], rw[:, 0:1], MAGIC, ALU.mult, ALU.add).then_inc(tern_step, 1)
            rsqrt(NL, 0, 0)
            ln_rsqrt(2)
            for w in range(1, 3):
                nc.gpsimd.tensor_scalar(WF[:, w, :], WF[:, w, :], rw[:, w:w + 1], MAGIC, ALU.mult, ALU.add)\
                    .then_inc(tern_step, 1)
            between = {0: lambda: rsqrt(NL, 0, 1), 2: lambda: ln_rsqrt(3), NW + 3: lambda: ln_rsqrt(4),
                       NW + 5: lambda: ln_rsqrt(5)}
            for i in range(2 * NW):
                pool.wait_ge(sig_set, i + 1)
                if i >= 3:
                    pool.wait_ge(wpv_done, i - 2)
                if WINDOW[i % NW][0] == "corner":
                    o, p, m = PT[:, i % 3, 0:2 * P], Pr[:, i % 3, 0:2 * P], corner
                else:
                    o, p, m = PT[:, i % 3, :], Pr[:, i % 3, :], band
                n = m.shape[1]
                h = o.shape[1] // n
                nc.gpsimd.tensor_tensor(o.rearrange("p (h q) -> p h q", q=n), p.rearrange("p (h q) -> p h q", q=n),
                                        m.unsqueeze(1).broadcast_to([P, h, n]), ALU.mult).then_inc(tau_set, 1)
                between.get(i, lambda: None)()
            ln_rsqrt(6)
            ln_rsqrt(7)


def constants():
    import numpy as np

    c = np.zeros((P, C_N), np.float32)
    p = np.arange(P)
    c[:, C_ID:C_ID + P] = np.eye(P, dtype=np.float32)
    c[:, C_CAUSAL:C_CAUSAL + P] = np.where(p[None, :] > p[:, None], NEG, 0.0)
    c[:, C_HEAD:C_HEAD + HT] = np.where(p[:, None] // HD == np.arange(HT)[None, :], SCALE, 0.0)
    inv = (np.float32(1.0) / np.float32(10000.0) ** (np.arange(0, HD, 2, dtype=np.float32) / np.float32(HD))).astype(np.float32)
    f = (np.arange(L, dtype=np.float32)[:, None] * inv[None, :]).astype(np.float32)
    cos, sin = np.cos(f), np.sin(f)
    cos = np.concatenate([cos, cos], 1).reshape(QT, P, HD).transpose(1, 0, 2)
    sin = np.concatenate([-sin, sin], 1).reshape(QT, P, HD).transpose(1, 0, 2)
    c[:, C_COS:C_COS + QT * HD] = cos.reshape(P, -1)
    c[:, C_SIN:C_SIN + QT * HD] = sin.reshape(P, -1)
    c[:, C_IOTA:C_IOTA + P] = p[None, :]
    back = p[None, :] - p[:, None]
    c[:, C_BAND:C_BAND + P] = (back >= 1) & (back <= HD)
    back = P + np.arange(HD)[None, :] - p[:, None]
    c[:, C_CORNER:C_CORNER + HD] = (back >= 1) & (back <= HD)
    return c


def rows_on_partitions(w):
    import numpy as np

    w = np.swapaxes(w, -1, -2)
    lead, (n_in, n_out) = w.shape[:-2], w.shape[-2:]
    w = w.reshape(*lead, n_in // P, P, n_out)
    return np.moveaxis(w, -2, -3).reshape(*lead, P, -1)


def kernel(**inputs):
    import numpy as np
    import concourse.bacc as bacc
    from concourse.bass_utils import run_bass_kernel_spmd as run

    a = {k: np.asarray(v) for k, v in inputs.items()}
    X, A, G = "L0_xattn_", "L0_attn_", "L0_ffn_"
    x = a["x"].reshape(4, P, D).transpose(1, 0, 2)
    ctx = a["ctx_1024"].reshape(B, NBLK, P, KT, P).transpose(1, 4, 3, 0, 2)
    seg = a["itok_BxS_0_255"].reshape(4, P)
    seg = np.concatenate([seg.T.ravel(), seg.ravel()])
    wa = np.concatenate([rows_on_partitions(a[X + "Wqkv"]), rows_on_partitions(a[X + "Wo"])], -1)
    wb = np.concatenate([rows_on_partitions(a[X + n]) for n in ("Wq_c", "Wkv_c", "Wo_c")], -1)
    wc = np.concatenate([rows_on_partitions(a[X + n]) for n in ("Wg", "Wu", "Wd")], -1)
    nrm = np.stack([a[X + n] for n in ("n1", "n2", "n3")], 1).reshape(NL, 3, KT, P).transpose(0, 3, 1, 2).reshape(NL, P, -1)
    bias = np.concatenate([a[X + "bqkv"], a[X + "bo"]], -1)
    vec = np.concatenate([a[X + "nf"], a[A + "gamma"], a[A + "beta"]])[None, :]
    wkv = a[A + "wkv"].reshape(H, 2, HD, D)
    wt = np.concatenate([rows_on_partitions(w) for w in (a[A + "wq"], wkv[:, 0].reshape(D, D), wkv[:, 1].reshape(D, D), a[A + "wo"])], -1)
    wf = np.stack([rows_on_partitions(a[G + n]) for n in ("w_gate", "w_up", "w_down")], 1)
    arrays = {"x": x, "ctx": ctx, "seg": seg, "wa": wa, "wb": wb, "wc": wc, "nrm": nrm, "bias": bias, "vec": vec,
              "wt": wt, "wf": wf, "const": constants()}
    arrays = {k: np.ascontiguousarray(v) for k, v in arrays.items()}
    nc = bacc.Bacc("TRN2", target_bir_lowering=False, num_devices=1)
    args = [nc.dram_tensor(f"in_{k}", v.shape, mybir.dt.from_np(v.dtype), kind="ExternalInput").ap() for k, v in arrays.items()]
    out = nc.dram_tensor("out_x", (4, P, D), F32, kind="ExternalOutput").ap()
    perceiver(nc, *args, out)
    r = run(nc, [{f"in_{k}": v for k, v in arrays.items()}], core_ids=[0])
    return r.results[0]["out_x"].reshape(B, L, D)
```
